# Optimizing a Trainium2 kernel written in Bass

```python
import numpy as np
import jax
import jax.numpy as jnp

def _softmax(x, axis=-1):
    return jax.nn.softmax(x, axis=axis)

def _gelu(x):
    return jax.nn.gelu(x, approximate=True)

def _silu(x):
    return jax.nn.silu(x)

def _sigmoid(x):
    return jax.nn.sigmoid(x)

def _layernorm(x, axis=-1, eps=1e-05):
    m = jnp.mean(x, axis=axis, keepdims=True)
    v = jnp.var(x, axis=axis, keepdims=True)
    return (x - m) / jnp.sqrt(v + eps)

def _scatter_add(tgt, idx, src, axis=0):
    return tgt.at[idx].add(src)

def _segment_sum(src, seg, n):
    return jax.ops.segment_sum(src, seg, n)
kernel_name = 'mk_xattn_ffn_d4_seqx_r8_31db0a'

def setup_inputs(seed: int=0):
    np.random.seed(seed)
    _w = jnp.asarray

    def _rec_inputs():
        import jax
        import jax.numpy as jnp
        _rk = jax.random.key(seed)
        x = -0.000929 + 1 * jax.random.normal(jax.random.fold_in(_rk, 1), (4, 256, 256), jnp.float32)
        _lenS = 256 - jax.random.randint(jax.random.fold_in(_rk, 7), (4,), 0, max(1, 256 // 4) + 1, jnp.int32)
        _lenS2 = 64 - jax.random.randint(jax.random.fold_in(_rk, 8), (4,), 0, max(1, 64 // 4) + 1, jnp.int32)
        _ctx_2048P = jax.random.normal(jax.random.fold_in(_rk, 11), (4, 16, 256), jnp.float32)
        _ctx_2048c = jax.random.dirichlet(jax.random.fold_in(_rk, 511), 0.3 * jnp.ones((16,), jnp.float32), (4, 64))
        _ctx_2048t = jnp.einsum('bsk,bkd->bsd', _ctx_2048c, _ctx_2048P)
        _ctx_2048t = _ctx_2048t * jax.lax.rsqrt(jnp.mean(jnp.square(_ctx_2048t)) + 1e-12) * 0.953939
        ctx_2048 = 2.81802e-05 + 1.00001 * (_ctx_2048t + 0.3 * jax.random.normal(jax.random.fold_in(_rk, 611), (4, 64, 256), jnp.float32))
        itok_BxS_0_1023 = jax.random.randint(jax.random.fold_in(_rk, 12), (4, 256), 0, 128, jnp.int32)
        return (x, ctx_2048, itok_BxS_0_1023)
    x, ctx_2048, itok_BxS_0_1023 = _rec_inputs()

    def _L0_xattn_setup():
        import jax, jax.numpy as jnp
        import numpy as np
        from jax import lax
        LN_EPS = 1e-05
        key = jax.random.key(seed)
        ks = jax.random.split(key, 8)
        B, S, T, D = (4, 128, 256, 256)
        scale = 0.02
        return {'Z': jax.random.normal(ks[0], (B, S, D), dtype=jnp.float32), 'kv': jax.random.normal(ks[1], (B, T, D), dtype=jnp.float32), 'decay': jnp.float32(0.9), 'W_in': jax.random.normal(ks[2], (D, D), dtype=jnp.float32) * scale, 'b_in': jnp.zeros((D,), dtype=jnp.float32), 'W_out': jax.random.normal(ks[3], (D, D), dtype=jnp.float32) * scale, 'b_out': jnp.zeros((D,), dtype=jnp.float32), 'gamma': jnp.ones((D,), dtype=jnp.float32), 'beta': jnp.zeros((D,), dtype=jnp.float32)}
    _L0_xattn_all = _L0_xattn_setup()
    _L0_xattn_in = {k: v for k, v in _L0_xattn_all.items() if k in ('decay', 'W_in', 'b_in', 'W_out', 'b_out', 'gamma', 'beta')}
    del _L0_xattn_all

    def _L0_ffn_setup():
        import jax, jax.numpy as jnp
        import numpy as np
        E = 32
        K = 6
        H = 256
        I = 128
        T = 256
        CAP = 96
        SCALE = 1.5
        SWIGLU_LIMIT = 10.0
        key = jax.random.key(seed)
        ks = jax.random.split(key, 9)

        def s(k, shape, fan):
            return jax.random.normal(k, shape, jnp.float32) * fan ** (-0.5)
        return {'x': jax.random.normal(ks[0], (1, T, H), jnp.float32), 'gate_w': s(ks[1], (E, H), H), 'bias': jax.random.normal(ks[2], (E,), jnp.float32) * 0.01, 'w_gate': s(ks[3], (E, I, H), H), 'w_up': s(ks[4], (E, I, H), H), 'w_down': s(ks[5], (E, H, I), I), 'sg': s(ks[6], (I, H), H), 'su': s(ks[7], (I, H), H), 'sd': s(ks[8], (H, I), I)}
    _L0_ffn_all = _L0_ffn_setup()
    _L0_ffn_in = {k: v for k, v in _L0_ffn_all.items() if k in ('gate_w', 'bias', 'w_gate', 'w_up', 'w_down', 'sg', 'su', 'sd')}
    del _L0_ffn_all

    def _L1_xattn_setup():
        import jax, jax.numpy as jnp
        import numpy as np
        B, Lq, Lk = (2, 512, 128)
        Q_DIM, KV_DIM = (256, 256)
        H, HD = (16, 128)
        KVC, QC, R = (64, 96, 64)
        LOOKBACK = 8
        NEG = -1e+30

        def _rope(x, L):
            half = x.shape[-1] // 2
            inv_freq = 1.0 / 10000.0 ** (jnp.arange(half, dtype=jnp.float32) / half)
            ang = jnp.arange(L, dtype=jnp.float32)[:, None] * inv_freq
            cos, sin = (jnp.cos(ang), jnp.sin(ang))
            x1, x2 = (x[..., :half], x[..., half:])
            return jnp.concatenate([x1 * cos - x2 * sin, x1 * sin + x2 * cos], axis=-1)
        key = jax.random.key(seed)
        ks = jax.random.split(key, 11)

        def w(k, shape, fan_in):
            return jax.random.normal(k, shape, jnp.float32) / np.sqrt(fan_in).astype(np.float32)
        return {'q': jax.random.normal(ks[0], (B, Lq, Q_DIM), jnp.float32), 'kv': jax.random.normal(ks[1], (B, Lk, KV_DIM), jnp.float32), 'seg_id': jnp.sort(jax.random.randint(ks[2], (B, Lq), 0, Lk), axis=-1), 'W_kvc': w(ks[3], (KV_DIM, KVC), KV_DIM), 'W_dq': w(ks[4], (Q_DIM, QC), Q_DIM), 'W_uq': w(ks[5], (QC, H * HD), QC), 'W_qr': w(ks[6], (QC, H * R), QC), 'W_uk': w(ks[7], (KVC, H * HD), KVC), 'W_kr': w(ks[8], (KVC, R), KVC), 'W_uv': w(ks[9], (KVC, H * HD), KVC), 'W_o': w(ks[10], (H * HD, Q_DIM), H * HD)}
    _L1_xattn_all = _L1_xattn_setup()
    _L1_xattn_in = {k: v for k, v in _L1_xattn_all.items() if k in ('W_kvc', 'W_dq', 'W_uq', 'W_qr', 'W_uk', 'W_kr', 'W_uv', 'W_o')}
    del _L1_xattn_all

    def _L1_ffn_setup():
        import jax, jax.numpy as jnp
        import numpy as np
        BS, SLEN, DIM, HID, E, K = (2, 128, 256, 128, 8, 2)
        INIT_STD = 0.02
        key = jax.random.key(seed)
        ks = jax.random.split(key, 8)
        s = INIT_STD
        return {'x': jax.random.normal(ks[0], (BS, SLEN, DIM), jnp.float32), 'gate_w': jax.random.normal(ks[1], (E, DIM), jnp.float32) * s, 'w1': jax.random.normal(ks[2], (E, HID, DIM), jnp.float32) * s, 'w2': jax.random.normal(ks[3], (E, DIM, HID), jnp.float32) * s, 'w3': jax.random.normal(ks[4], (E, HID, DIM), jnp.float32) * s, 'sw1': jax.random.normal(ks[5], (HID, DIM), jnp.float32) * s, 'sw2': jax.random.normal(ks[6], (DIM, HID), jnp.float32) * s, 'sw3': jax.random.normal(ks[7], (HID, DIM), jnp.float32) * s}
    _L1_ffn_all = _L1_ffn_setup()
    _L1_ffn_in = {k: v for k, v in _L1_ffn_all.items() if k in ('gate_w', 'w1', 'w2', 'w3', 'sw1', 'sw2', 'sw3')}
    del _L1_ffn_all

    def _L2_xattn_setup():
        import jax, jax.numpy as jnp
        import numpy as np
        FP8_MAX = 448.0
        EPS = 1e-05

        def _fp8_roundtrip(x):
            return x.astype(jnp.float8_e4m3fn).astype(jnp.float32)

        def _div_clamp_fp8(x, scale):
            y = jnp.clip(x.astype(jnp.float32) / scale, -FP8_MAX, FP8_MAX)
            y = y.astype(jnp.bfloat16).astype(jnp.float32)
            return _fp8_roundtrip(y)

        def _ln(x, w, b):
            mu = jnp.mean(x, axis=-1, keepdims=True)
            var = jnp.mean(jnp.square(x - mu), axis=-1, keepdims=True)
            return (x - mu) * jax.lax.rsqrt(var + EPS) * w + b

        def _fp8_linear_pertensor(x, wq, w_scale, in_scale):
            xq = _div_clamp_fp8(x, in_scale)
            return jnp.einsum('bsi,oi->bso', xq * in_scale, wq) * w_scale

        def _gqa(q, k, v):
            scale = 1.0 / np.sqrt(q.shape[-1])
            scores = jnp.einsum('bsghd,btgd->bghst', q, k) * scale
            p = jax.nn.softmax(scores, axis=-1)
            return jnp.einsum('bghst,btgd->bsghd', p, v)
        key = jax.random.key(seed)
        ks = jax.random.split(key, 8)
        B, S, SC, H, NH, G, D = (2, 256, 64, 256, 16, 8, 128)

        def qw(k, out_f, in_f):
            w = jax.random.normal(k, (out_f, in_f), jnp.float32) * 0.02
            sc = jnp.max(jnp.abs(w)) / FP8_MAX
            return (_fp8_roundtrip(w / sc), sc.astype(jnp.float32))
        wq, wq_s = qw(ks[0], NH * D, H)
        wqx, wqx_s = qw(ks[1], NH * D, H)
        wk, wk_s = qw(ks[2], G * D, H)
        wv, wv_s = qw(ks[3], G * D, H)
        wproj, wp_s = qw(ks[4], H, 2 * NH * D)
        return {'hidden_states': jax.random.normal(ks[5], (B, S, H), jnp.float32), 'cond': jax.random.normal(ks[6], (B, SC, H), jnp.float32), 'ln_w': jnp.ones((H,), jnp.float32), 'ln_b': jnp.zeros((H,), jnp.float32), 'wq': wq, 'wq_scale': wq_s, 'q_in_scale': jnp.full((H,), 0.05, jnp.float32), 'wqx': wqx, 'wqx_scale': wqx_s, 'qx_in_scale': jnp.full((H,), 0.05, jnp.float32), 'wk': wk, 'wk_scale': wk_s, 'k_in_scale': jnp.full((H,), 0.05, jnp.float32), 'wv': wv, 'wv_scale': wv_s, 'v_in_scale': jnp.full((H,), 0.05, jnp.float32), 'w_kv_x': jax.random.normal(ks[7], (2 * G * D, H), jnp.float32) * 0.02, 'qln_w': jnp.ones((D,), jnp.float32), 'qln_b': jnp.zeros((D,), jnp.float32), 'kln_w': jnp.ones((D,), jnp.float32), 'kln_b': jnp.zeros((D,), jnp.float32), 'qxln_w': jnp.ones((D,), jnp.float32), 'qxln_b': jnp.zeros((D,), jnp.float32), 'kxln_w': jnp.ones((D,), jnp.float32), 'kxln_b': jnp.zeros((D,), jnp.float32), 'wproj': wproj, 'proj_w_scale': wp_s, 'proj_in_scale': jnp.asarray(0.05, jnp.float32), 'proj_smooth': jnp.full((2 * NH * D,), 0.05, jnp.float32)}
    _L2_xattn_all = _L2_xattn_setup()
    _L2_xattn_in = {k: v for k, v in _L2_xattn_all.items() if k in ('ln_w', 'ln_b', 'wq', 'wq_scale', 'q_in_scale', 'wqx', 'wqx_scale', 'qx_in_scale', 'wk', 'wk_scale', 'k_in_scale', 'wv', 'wv_scale', 'v_in_scale', 'w_kv_x', 'qln_w', 'qln_b', 'kln_w', 'kln_b', 'qxln_w', 'qxln_b', 'kxln_w', 'kxln_b', 'wproj', 'proj_w_scale', 'proj_in_scale', 'proj_smooth')}
    del _L2_xattn_all

    def _L2_ffn_setup():
        import jax, jax.numpy as jnp
        import numpy as np
        EPS = 1e-08

        def _quantize(w):
            gamma = jnp.mean(jnp.abs(w))
            return jnp.clip(jnp.round(w / (gamma + EPS)), -1.0, 1.0)

        def _bitlinear(x, w):
            return jnp.matmul(x, _quantize(w).T)
        key = jax.random.key(seed)
        k1, k2, k3, k4 = jax.random.split(key, 4)
        d, h = (256, 704)
        x = jax.random.normal(k1, (4, 256, d), dtype=jnp.float32)
        w1 = jax.random.normal(k2, (h, d), dtype=jnp.float32)
        w2 = jax.random.normal(k3, (h, d), dtype=jnp.float32)
        w3 = jax.random.normal(k4, (d, h), dtype=jnp.float32)
        return {'x': x, 'w1': w1, 'w2': w2, 'w3': w3}
    _L2_ffn_all = _L2_ffn_setup()
    _L2_ffn_in = {k: v for k, v in _L2_ffn_all.items() if k in ('w1', 'w2', 'w3')}
    del _L2_ffn_all

    def _L3_xattn_setup():
        import jax, jax.numpy as jnp
        import numpy as np
        DIM = 256
        NH = 16
        HD = DIM // NH
        EPS = 1e-06
        IMG_LEN = 257

        def rms_norm(x, w, eps=EPS):
            xf = x.astype(jnp.float32)
            y = xf * jax.lax.rsqrt(jnp.mean(xf * xf, axis=-1, keepdims=True) + eps)
            return y.astype(x.dtype) * w

        def linear(x, w, b):
            return jnp.einsum('blc,oc->blo', x, w) + b

        def attention(q, k, v):
            scale = 1.0 / jnp.sqrt(jnp.asarray(HD, q.dtype))
            scores = jnp.einsum('bqhd,bkhd->bhqk', q, k) * scale
            probs = jax.nn.softmax(scores, axis=-1)
            return jnp.einsum('bhqk,bkhd->bqhd', probs, v)
        key = jax.random.key(seed)
        ks = jax.random.split(key, 12)
        B, L = (2, 1024)
        s = 0.02
        inp = {'x': jax.random.normal(ks[0], (B, L, DIM), jnp.float32), 'context': jax.random.normal(ks[1], (B, 769, DIM), jnp.float32), 'q_w': jax.random.normal(ks[2], (DIM, DIM), jnp.float32) * s, 'q_b': jnp.zeros((DIM,), jnp.float32), 'k_w': jax.random.normal(ks[3], (DIM, DIM), jnp.float32) * s, 'k_b': jnp.zeros((DIM,), jnp.float32), 'v_w': jax.random.normal(ks[4], (DIM, DIM), jnp.float32) * s, 'v_b': jnp.zeros((DIM,), jnp.float32), 'k_img_w': jax.random.normal(ks[5], (DIM, DIM), jnp.float32) * s, 'k_img_b': jnp.zeros((DIM,), jnp.float32), 'v_img_w': jax.random.normal(ks[6], (DIM, DIM), jnp.float32) * s, 'v_img_b': jnp.zeros((DIM,), jnp.float32), 'o_w': jax.random.normal(ks[7], (DIM, DIM), jnp.float32) * s, 'o_b': jnp.zeros((DIM,), jnp.float32), 'norm_q_w': jnp.ones((DIM,), jnp.float32), 'norm_k_w': jnp.ones((DIM,), jnp.float32), 'norm_k_img_w': jnp.ones((DIM,), jnp.float32)}
        return inp
    _L3_xattn_all = _L3_xattn_setup()
    _L3_xattn_in = {k: v for k, v in _L3_xattn_all.items() if k in ('q_w', 'q_b', 'k_w', 'k_b', 'v_w', 'v_b', 'k_img_w', 'k_img_b', 'v_img_w', 'v_img_b', 'o_w', 'o_b', 'norm_q_w', 'norm_k_w', 'norm_k_img_w')}
    del _L3_xattn_all

    def _L3_ffn_setup():
        import jax, jax.numpy as jnp
        import numpy as np
        B, S, H = (4, 128, 256)
        E = 16
        K = 2
        I = 128
        N_SHARED = 2
        I_SHARED = I * N_SHARED
        RATIO = 0.1
        EPS = 1e-09

        def _swiglu(x, wg, wu, wd):
            return jax.nn.silu(x @ wg) * (x @ wu) @ wd
        key = jax.random.key(seed)
        ks = jax.random.split(key, 9)
        scale = 0.02
        x = jax.random.normal(ks[0], (B, S, H), dtype=jnp.float32)
        centroids = jax.random.normal(ks[1], (E, H), dtype=jnp.float32)
        gate_bias = jnp.zeros((E,), dtype=jnp.float32)
        wg_s = jax.random.normal(ks[2], (H, I_SHARED), dtype=jnp.float32) * scale
        wu_s = jax.random.normal(ks[3], (H, I_SHARED), dtype=jnp.float32) * scale
        wd_s = jax.random.normal(ks[4], (I_SHARED, H), dtype=jnp.float32) * scale
        wg = jax.random.normal(ks[5], (E, H, I), dtype=jnp.float32) * scale
        wu = jax.random.normal(ks[6], (E, H, I), dtype=jnp.float32) * scale
        wd = jax.random.normal(ks[7], (E, I, H), dtype=jnp.float32) * scale
        return {'x': x, 'centroids': centroids, 'gate_bias': gate_bias, 'wg_s': wg_s, 'wu_s': wu_s, 'wd_s': wd_s, 'wg': wg, 'wu': wu, 'wd': wd}
    _L3_ffn_all = _L3_ffn_setup()
    _L3_ffn_in = {k: v for k, v in _L3_ffn_all.items() if k in ('centroids', 'gate_bias', 'wg_s', 'wu_s', 'wd_s', 'wg', 'wu', 'wd')}
    del _L3_ffn_all
    return {'x': x, 'ctx_2048': ctx_2048, 'itok_BxS_0_1023': itok_BxS_0_1023, 'L0_xattn_decay': _L0_xattn_in['decay'], 'L0_xattn_W_in': _L0_xattn_in['W_in'], 'L0_xattn_b_in': _L0_xattn_in['b_in'], 'L0_xattn_W_out': _L0_xattn_in['W_out'], 'L0_xattn_b_out': _L0_xattn_in['b_out'], 'L0_xattn_gamma': _L0_xattn_in['gamma'], 'L0_xattn_beta': _L0_xattn_in['beta'], 'L0_ffn_gate_w': _L0_ffn_in['gate_w'], 'L0_ffn_bias': _L0_ffn_in['bias'], 'L0_ffn_w_gate': _L0_ffn_in['w_gate'], 'L0_ffn_w_up': _L0_ffn_in['w_up'], 'L0_ffn_w_down': _L0_ffn_in['w_down'], 'L0_ffn_sg': _L0_ffn_in['sg'], 'L0_ffn_su': _L0_ffn_in['su'], 'L0_ffn_sd': _L0_ffn_in['sd'], 'L1_xattn_W_kvc': _L1_xattn_in['W_kvc'], 'L1_xattn_W_dq': _L1_xattn_in['W_dq'], 'L1_xattn_W_uq': _L1_xattn_in['W_uq'], 'L1_xattn_W_qr': _L1_xattn_in['W_qr'], 'L1_xattn_W_uk': _L1_xattn_in['W_uk'], 'L1_xattn_W_kr': _L1_xattn_in['W_kr'], 'L1_xattn_W_uv': _L1_xattn_in['W_uv'], 'L1_xattn_W_o': _L1_xattn_in['W_o'], 'L1_ffn_gate_w': _L1_ffn_in['gate_w'], 'L1_ffn_w1': _L1_ffn_in['w1'], 'L1_ffn_w2': _L1_ffn_in['w2'], 'L1_ffn_w3': _L1_ffn_in['w3'], 'L1_ffn_sw1': _L1_ffn_in['sw1'], 'L1_ffn_sw2': _L1_ffn_in['sw2'], 'L1_ffn_sw3': _L1_ffn_in['sw3'], 'L2_xattn_ln_w': _L2_xattn_in['ln_w'], 'L2_xattn_ln_b': _L2_xattn_in['ln_b'], 'L2_xattn_wq': _L2_xattn_in['wq'], 'L2_xattn_wq_scale': _L2_xattn_in['wq_scale'], 'L2_xattn_q_in_scale': _L2_xattn_in['q_in_scale'], 'L2_xattn_wqx': _L2_xattn_in['wqx'], 'L2_xattn_wqx_scale': _L2_xattn_in['wqx_scale'], 'L2_xattn_qx_in_scale': _L2_xattn_in['qx_in_scale'], 'L2_xattn_wk': _L2_xattn_in['wk'], 'L2_xattn_wk_scale': _L2_xattn_in['wk_scale'], 'L2_xattn_k_in_scale': _L2_xattn_in['k_in_scale'], 'L2_xattn_wv': _L2_xattn_in['wv'], 'L2_xattn_wv_scale': _L2_xattn_in['wv_scale'], 'L2_xattn_v_in_scale': _L2_xattn_in['v_in_scale'], 'L2_xattn_w_kv_x': _L2_xattn_in['w_kv_x'], 'L2_xattn_qln_w': _L2_xattn_in['qln_w'], 'L2_xattn_qln_b': _L2_xattn_in['qln_b'], 'L2_xattn_kln_w': _L2_xattn_in['kln_w'], 'L2_xattn_kln_b': _L2_xattn_in['kln_b'], 'L2_xattn_qxln_w': _L2_xattn_in['qxln_w'], 'L2_xattn_qxln_b': _L2_xattn_in['qxln_b'], 'L2_xattn_kxln_w': _L2_xattn_in['kxln_w'], 'L2_xattn_kxln_b': _L2_xattn_in['kxln_b'], 'L2_xattn_wproj': _L2_xattn_in['wproj'], 'L2_xattn_proj_w_scale': _L2_xattn_in['proj_w_scale'], 'L2_xattn_proj_in_scale': _L2_xattn_in['proj_in_scale'], 'L2_xattn_proj_smooth': _L2_xattn_in['proj_smooth'], 'L2_ffn_w1': _L2_ffn_in['w1'], 'L2_ffn_w2': _L2_ffn_in['w2'], 'L2_ffn_w3': _L2_ffn_in['w3'], 'L3_xattn_q_w': _L3_xattn_in['q_w'], 'L3_xattn_q_b': _L3_xattn_in['q_b'], 'L3_xattn_k_w': _L3_xattn_in['k_w'], 'L3_xattn_k_b': _L3_xattn_in['k_b'], 'L3_xattn_v_w': _L3_xattn_in['v_w'], 'L3_xattn_v_b': _L3_xattn_in['v_b'], 'L3_xattn_k_img_w': _L3_xattn_in['k_img_w'], 'L3_xattn_k_img_b': _L3_xattn_in['k_img_b'], 'L3_xattn_v_img_w': _L3_xattn_in['v_img_w'], 'L3_xattn_v_img_b': _L3_xattn_in['v_img_b'], 'L3_xattn_o_w': _L3_xattn_in['o_w'], 'L3_xattn_o_b': _L3_xattn_in['o_b'], 'L3_xattn_norm_q_w': _L3_xattn_in['norm_q_w'], 'L3_xattn_norm_k_w': _L3_xattn_in['norm_k_w'], 'L3_xattn_norm_k_img_w': _L3_xattn_in['norm_k_img_w'], 'L3_ffn_centroids': _L3_ffn_in['centroids'], 'L3_ffn_gate_bias': _L3_ffn_in['gate_bias'], 'L3_ffn_wg_s': _L3_ffn_in['wg_s'], 'L3_ffn_wu_s': _L3_ffn_in['wu_s'], 'L3_ffn_wd_s': _L3_ffn_in['wd_s'], 'L3_ffn_wg': _L3_ffn_in['wg'], 'L3_ffn_wu': _L3_ffn_in['wu'], 'L3_ffn_wd': _L3_ffn_in['wd']}

def reference(x, ctx_2048, itok_BxS_0_1023, L0_xattn_decay, L0_xattn_W_in, L0_xattn_b_in, L0_xattn_W_out, L0_xattn_b_out, L0_xattn_gamma, L0_xattn_beta, L0_ffn_gate_w, L0_ffn_bias, L0_ffn_w_gate, L0_ffn_w_up, L0_ffn_w_down, L0_ffn_sg, L0_ffn_su, L0_ffn_sd, L1_xattn_W_kvc, L1_xattn_W_dq, L1_xattn_W_uq, L1_xattn_W_qr, L1_xattn_W_uk, L1_xattn_W_kr, L1_xattn_W_uv, L1_xattn_W_o, L1_ffn_gate_w, L1_ffn_w1, L1_ffn_w2, L1_ffn_w3, L1_ffn_sw1, L1_ffn_sw2, L1_ffn_sw3, L2_xattn_ln_w, L2_xattn_ln_b, L2_xattn_wq, L2_xattn_wq_scale, L2_xattn_q_in_scale, L2_xattn_wqx, L2_xattn_wqx_scale, L2_xattn_qx_in_scale, L2_xattn_wk, L2_xattn_wk_scale, L2_xattn_k_in_scale, L2_xattn_wv, L2_xattn_wv_scale, L2_xattn_v_in_scale, L2_xattn_w_kv_x, L2_xattn_qln_w, L2_xattn_qln_b, L2_xattn_kln_w, L2_xattn_kln_b, L2_xattn_qxln_w, L2_xattn_qxln_b, L2_xattn_kxln_w, L2_xattn_kxln_b, L2_xattn_wproj, L2_xattn_proj_w_scale, L2_xattn_proj_in_scale, L2_xattn_proj_smooth, L2_ffn_w1, L2_ffn_w2, L2_ffn_w3, L3_xattn_q_w, L3_xattn_q_b, L3_xattn_k_w, L3_xattn_k_b, L3_xattn_v_w, L3_xattn_v_b, L3_xattn_k_img_w, L3_xattn_k_img_b, L3_xattn_v_img_w, L3_xattn_v_img_b, L3_xattn_o_w, L3_xattn_o_b, L3_xattn_norm_q_w, L3_xattn_norm_k_w, L3_xattn_norm_k_img_w, L3_ffn_centroids, L3_ffn_gate_bias, L3_ffn_wg_s, L3_ffn_wu_s, L3_ffn_wd_s, L3_ffn_wg, L3_ffn_wu, L3_ffn_wd):
    import jax
    import jax.numpy as jnp

    def _L0_xattn_ref(Z, kv, decay, W_in, b_in, W_out, b_out, gamma, beta):
        import jax, jax.numpy as jnp
        import numpy as np
        from jax import lax
        LN_EPS = 1e-05
        B, T, D = kv.shape
        K = jax.nn.sigmoid(decay)
        x = jnp.einsum('btd,ed->bte', kv, W_in) + b_in

        def scan_fn(s, xt):
            s = K * s + xt
            return (s, s)
        s0 = jnp.zeros((B, D), dtype=kv.dtype)
        _, states = lax.scan(scan_fn, s0, jnp.swapaxes(x, 0, 1))
        states = jnp.swapaxes(states, 0, 1)
        proj = jnp.einsum('btd,ed->bte', states, W_out) + b_out
        summary = jnp.mean(proj, axis=1, keepdims=True)
        y = Z + summary
        mu = jnp.mean(y, axis=-1, keepdims=True)
        var = jnp.mean((y - mu) ** 2, axis=-1, keepdims=True)
        return (y - mu) / jnp.sqrt(var + LN_EPS) * gamma + beta

    def _L0_ffn_ref(x, gate_w, bias, w_gate, w_up, w_down, sg, su, sd):
        import jax, jax.numpy as jnp
        import numpy as np
        E = 32
        K = 6
        H = 256
        I = 128
        T = 256
        CAP = 96
        SCALE = 1.5
        SWIGLU_LIMIT = 10.0
        B, S, Hd = x.shape
        h = x.reshape(-1, Hd)
        logits = h @ gate_w.T
        scores = jnp.sqrt(jax.nn.softplus(logits))
        _, topk_idx = jax.lax.top_k(scores + bias[None, :], K)
        topk_w = jnp.take_along_axis(scores, topk_idx, axis=1)
        topk_w = topk_w / jnp.sum(topk_w, axis=-1, keepdims=True)
        topk_w = topk_w * SCALE
        eid = topk_idx.reshape(-1)
        onehot = jax.nn.one_hot(eid, E, dtype=jnp.int32)
        pos = jnp.cumsum(onehot, axis=0) - 1
        pos = jnp.take_along_axis(pos, eid[:, None], axis=1)[:, 0]
        valid = pos < CAP
        pos = jnp.where(valid, pos, CAP)
        h_rep = jnp.repeat(h, K, axis=0)
        xb = jnp.zeros((E, CAP + 1, Hd), x.dtype).at[eid, pos].set(h_rep)
        g = jnp.einsum('ech,eih->eci', xb, w_gate)
        u = jnp.einsum('ech,eih->eci', xb, w_up)
        inter = jax.nn.silu(g) * u
        yb = jnp.einsum('eci,ehi->ech', inter, w_down)
        w_slot = jnp.where(valid, topk_w.reshape(-1), 0.0)
        y = yb[eid, pos] * w_slot[:, None]
        routed = y.reshape(-1, K, Hd).sum(axis=1)
        si = jax.nn.silu(h @ sg.T) * (h @ su.T)
        si = jnp.clip(si, -SWIGLU_LIMIT, SWIGLU_LIMIT)
        shared = si @ sd.T
        return (routed + shared).reshape(B, S, Hd)

    def _L1_xattn_ref(q, kv, seg_id, W_kvc, W_dq, W_uq, W_qr, W_uk, W_kr, W_uv, W_o):
        import jax, jax.numpy as jnp
        import numpy as np
        B, Lq, Lk = (2, 512, 128)
        Q_DIM, KV_DIM = (256, 256)
        H, HD = (16, 128)
        KVC, QC, R = (64, 96, 64)
        LOOKBACK = 8
        NEG = -1e+30

        def _rope(x, L):
            half = x.shape[-1] // 2
            inv_freq = 1.0 / 10000.0 ** (jnp.arange(half, dtype=jnp.float32) / half)
            ang = jnp.arange(L, dtype=jnp.float32)[:, None] * inv_freq
            cos, sin = (jnp.cos(ang), jnp.sin(ang))
            x1, x2 = (x[..., :half], x[..., half:])
            return jnp.concatenate([x1 * cos - x2 * sin, x1 * sin + x2 * cos], axis=-1)
        b, lq, _ = q.shape
        lk = kv.shape[1]
        kv_c = kv @ W_kvc
        q_c = q @ W_dq
        q_nope = (q_c @ W_uq).reshape(b, lq, H, HD).transpose(0, 2, 1, 3)
        q_rope = (q_c @ W_qr).reshape(b, lq, H, R).transpose(0, 2, 1, 3)
        k_nope = (kv_c @ W_uk).reshape(b, lk, H, HD)
        v = (kv_c @ W_uv).reshape(b, lk, H, HD)
        k_rope = kv_c @ W_kr
        q_rope = _rope(q_rope, lq)
        k_rope = _rope(k_rope, lk)
        scale = 1.0 / np.sqrt(HD + R).astype(np.float32)
        scores = (jnp.einsum('bhqd,bkhd->bhqk', q_nope, k_nope) + jnp.einsum('bhqr,bkr->bhqk', q_rope, k_rope)) * scale
        k_ids = jnp.arange(lk)[None, None, :]
        qs = seg_id[:, :, None]
        good = (k_ids <= qs) & (k_ids >= qs - LOOKBACK)
        scores = jnp.where(good[:, None, :, :], scores, NEG)
        attn = jax.nn.softmax(scores, axis=-1)
        out = jnp.einsum('bhqk,bkhd->bqhd', attn, v).reshape(b, lq, H * HD)
        return out @ W_o

    def _L1_ffn_ref(x, gate_w, w1, w2, w3, sw1, sw2, sw3):
        import jax, jax.numpy as jnp
        import numpy as np
        BS, SLEN, DIM, HID, E, K = (2, 128, 256, 128, 8, 2)
        INIT_STD = 0.02
        bs, slen, dim = x.shape
        xt = x.reshape(-1, dim)
        scores = jax.nn.sigmoid((xt @ gate_w.T).astype(jnp.float32))
        top_scores, sel = jax.lax.top_k(scores, K)
        flat_sel = sel.reshape(-1)
        order = jnp.argsort(flat_sel, stable=True)
        token_idx = order // K
        expert_sorted = flat_sel[order]
        slot_scores = top_scores.reshape(-1)[order]
        routed_x = xt[token_idx] * slot_scores[:, None].astype(xt.dtype)
        out_r = jnp.zeros_like(routed_x)
        for e in range(E):
            m = (expert_sorted == e)[:, None].astype(routed_x.dtype)
            h = jax.nn.silu(routed_x @ w1[e].T) * (routed_x @ w3[e].T)
            out_r = out_r + h @ w2[e].T * m
        shared = jax.nn.silu(xt @ sw1.T) * (xt @ sw3.T) @ sw2.T
        out = shared.at[token_idx].add(out_r)
        return out.reshape(bs, slen, dim)

    def _L2_xattn_ref(hidden_states, cond, ln_w, ln_b, wq, wq_scale, q_in_scale, wqx, wqx_scale, qx_in_scale, wk, wk_scale, k_in_scale, wv, wv_scale, v_in_scale, w_kv_x, qln_w, qln_b, kln_w, kln_b, qxln_w, qxln_b, kxln_w, kxln_b, wproj, proj_w_scale, proj_in_scale, proj_smooth):
        import jax, jax.numpy as jnp
        import numpy as np
        FP8_MAX = 448.0
        EPS = 1e-05

        def _fp8_roundtrip(x):
            return x.astype(jnp.float8_e4m3fn).astype(jnp.float32)

        def _div_clamp_fp8(x, scale):
            y = jnp.clip(x.astype(jnp.float32) / scale, -FP8_MAX, FP8_MAX)
            y = y.astype(jnp.bfloat16).astype(jnp.float32)
            return _fp8_roundtrip(y)

        def _ln(x, w, b):
            mu = jnp.mean(x, axis=-1, keepdims=True)
            var = jnp.mean(jnp.square(x - mu), axis=-1, keepdims=True)
            return (x - mu) * jax.lax.rsqrt(var + EPS) * w + b

        def _fp8_linear_pertensor(x, wq, w_scale, in_scale):
            xq = _div_clamp_fp8(x, in_scale)
            return jnp.einsum('bsi,oi->bso', xq * in_scale, wq) * w_scale

        def _gqa(q, k, v):
            scale = 1.0 / np.sqrt(q.shape[-1])
            scores = jnp.einsum('bsghd,btgd->bghst', q, k) * scale
            p = jax.nn.softmax(scores, axis=-1)
            return jnp.einsum('bghst,btgd->bsghd', p, v)
        b, s, _ = hidden_states.shape
        sc = cond.shape[1]
        d = qln_w.shape[0]
        nh = wq.shape[0] // d
        g = wk.shape[0] // d
        hpg = nh // g
        ln_out = _ln(hidden_states, ln_w, ln_b)
        q = _fp8_linear_pertensor(ln_out, wq, wq_scale, q_in_scale).reshape(b, s, g, hpg, d)
        q = _ln(q, qln_w, qln_b)
        k = _fp8_linear_pertensor(ln_out, wk, wk_scale, k_in_scale).reshape(b, s, g, d)
        k = _ln(k, kln_w, kln_b)
        v = _fp8_linear_pertensor(ln_out, wv, wv_scale, v_in_scale).reshape(b, s, g, d)
        core = _gqa(q, k, v).reshape(b, s, nh * d)
        qx = _fp8_linear_pertensor(ln_out, wqx, wqx_scale, qx_in_scale).reshape(b, s, g, hpg, d)
        qx = _ln(qx, qxln_w, qxln_b)
        kvx = jnp.einsum('bsi,oi->bso', cond, w_kv_x)
        kx, vx = jnp.split(kvx, 2, axis=-1)
        kx = _ln(kx.reshape(b, sc, g, d), kxln_w, kxln_b)
        vx = vx.reshape(b, sc, g, d)
        xout = _gqa(qx, kx, vx).reshape(b, s, nh * d)
        cat = jnp.concatenate([core, xout], axis=-1)
        catq = _div_clamp_fp8(cat, proj_smooth)
        return jnp.einsum('bsi,oi->bso', catq, wproj) * (proj_in_scale * proj_w_scale)

    def _L2_ffn_ref(x, w1, w2, w3):
        import jax, jax.numpy as jnp
        import numpy as np
        EPS = 1e-08

        def _quantize(w):
            gamma = jnp.mean(jnp.abs(w))
            return jnp.clip(jnp.round(w / (gamma + EPS)), -1.0, 1.0)

        def _bitlinear(x, w):
            return jnp.matmul(x, _quantize(w).T)
        x1 = _bitlinear(x, w1)
        x2 = _bitlinear(x, w2)
        hidden = jax.nn.sigmoid(x1) * x2
        return _bitlinear(hidden, w3)

    def _L3_xattn_ref(x, context, q_w, q_b, k_w, k_b, v_w, v_b, k_img_w, k_img_b, v_img_w, v_img_b, o_w, o_b, norm_q_w, norm_k_w, norm_k_img_w):
        import jax, jax.numpy as jnp
        import numpy as np
        DIM = 256
        NH = 16
        HD = DIM // NH
        EPS = 1e-06
        IMG_LEN = 257

        def rms_norm(x, w, eps=EPS):
            xf = x.astype(jnp.float32)
            y = xf * jax.lax.rsqrt(jnp.mean(xf * xf, axis=-1, keepdims=True) + eps)
            return y.astype(x.dtype) * w

        def linear(x, w, b):
            return jnp.einsum('blc,oc->blo', x, w) + b

        def attention(q, k, v):
            scale = 1.0 / jnp.sqrt(jnp.asarray(HD, q.dtype))
            scores = jnp.einsum('bqhd,bkhd->bhqk', q, k) * scale
            probs = jax.nn.softmax(scores, axis=-1)
            return jnp.einsum('bhqk,bkhd->bqhd', probs, v)
        B, L, _ = x.shape
        ctx_img = context[:, :IMG_LEN]
        ctx_txt = context[:, IMG_LEN:]
        q = rms_norm(linear(x, q_w, q_b), norm_q_w).reshape(B, L, NH, HD)
        k = rms_norm(linear(ctx_txt, k_w, k_b), norm_k_w).reshape(B, -1, NH, HD)
        v = linear(ctx_txt, v_w, v_b).reshape(B, -1, NH, HD)
        k_img = rms_norm(linear(ctx_img, k_img_w, k_img_b), norm_k_img_w).reshape(B, -1, NH, HD)
        v_img = linear(ctx_img, v_img_w, v_img_b).reshape(B, -1, NH, HD)
        img_x = attention(q, k_img, v_img)
        txt_x = attention(q, k, v)
        out = (txt_x + img_x).reshape(B, L, DIM)
        return linear(out, o_w, o_b)

    def _L3_ffn_ref(x, centroids, gate_bias, wg_s, wu_s, wd_s, wg, wu, wd):
        import jax, jax.numpy as jnp
        import numpy as np
        B, S, H = (4, 128, 256)
        E = 16
        K = 2
        I = 128
        N_SHARED = 2
        I_SHARED = I * N_SHARED
        RATIO = 0.1
        EPS = 1e-09

        def _swiglu(x, wg, wu, wd):
            return jax.nn.silu(x @ wg) * (x @ wu) @ wd
        shared = _swiglu(x, wg_s, wu_s, wd_s) * RATIO
        affinity = jax.nn.sigmoid(jnp.einsum('bsh,eh->bse', x, centroids))
        biased = affinity + gate_bias
        _, top_idx = jax.lax.top_k(biased, K)
        top_aff = jnp.take_along_axis(affinity, top_idx, axis=-1)
        weights = top_aff / (top_aff.sum(-1, keepdims=True) + EPS)
        mask = (jax.nn.one_hot(top_idx, E, dtype=x.dtype) * weights[..., None]).sum(-2)
        routed = jnp.zeros_like(x)
        for e in range(E):
            routed = routed + mask[..., e:e + 1] * _swiglu(x, wg[e], wu[e], wd[e])
        return shared + routed
    x = x + _L0_xattn_ref(_layernorm(x, axis=-1), ctx_2048, L0_xattn_decay, L0_xattn_W_in, L0_xattn_b_in, L0_xattn_W_out, L0_xattn_b_out, L0_xattn_gamma, L0_xattn_beta)
    x = x + _L0_ffn_ref(_layernorm(x, axis=-1), L0_ffn_gate_w, L0_ffn_bias, L0_ffn_w_gate, L0_ffn_w_up, L0_ffn_w_down, L0_ffn_sg, L0_ffn_su, L0_ffn_sd)
    x = x + _L1_xattn_ref(_layernorm(x, axis=-1), ctx_2048, itok_BxS_0_1023, L1_xattn_W_kvc, L1_xattn_W_dq, L1_xattn_W_uq, L1_xattn_W_qr, L1_xattn_W_uk, L1_xattn_W_kr, L1_xattn_W_uv, L1_xattn_W_o)
    x = x + _L1_ffn_ref(_layernorm(x, axis=-1), L1_ffn_gate_w, L1_ffn_w1, L1_ffn_w2, L1_ffn_w3, L1_ffn_sw1, L1_ffn_sw2, L1_ffn_sw3)
    x = x + _L2_xattn_ref(_layernorm(x, axis=-1), ctx_2048, L2_xattn_ln_w, L2_xattn_ln_b, L2_xattn_wq, L2_xattn_wq_scale, L2_xattn_q_in_scale, L2_xattn_wqx, L2_xattn_wqx_scale, L2_xattn_qx_in_scale, L2_xattn_wk, L2_xattn_wk_scale, L2_xattn_k_in_scale, L2_xattn_wv, L2_xattn_wv_scale, L2_xattn_v_in_scale, L2_xattn_w_kv_x, L2_xattn_qln_w, L2_xattn_qln_b, L2_xattn_kln_w, L2_xattn_kln_b, L2_xattn_qxln_w, L2_xattn_qxln_b, L2_xattn_kxln_w, L2_xattn_kxln_b, L2_xattn_wproj, L2_xattn_proj_w_scale, L2_xattn_proj_in_scale, L2_xattn_proj_smooth)
    x = x + _L2_ffn_ref(_layernorm(x, axis=-1), L2_ffn_w1, L2_ffn_w2, L2_ffn_w3)
    x = x + _L3_xattn_ref(_layernorm(x, axis=-1), ctx_2048, L3_xattn_q_w, L3_xattn_q_b, L3_xattn_k_w, L3_xattn_k_b, L3_xattn_v_w, L3_xattn_v_b, L3_xattn_k_img_w, L3_xattn_k_img_b, L3_xattn_v_img_w, L3_xattn_v_img_b, L3_xattn_o_w, L3_xattn_o_b, L3_xattn_norm_q_w, L3_xattn_norm_k_w, L3_xattn_norm_k_img_w)
    x = x + _L3_ffn_ref(_layernorm(x, axis=-1), L3_ffn_centroids, L3_ffn_gate_bias, L3_ffn_wg_s, L3_ffn_wu_s, L3_ffn_wd_s, L3_ffn_wg, L3_ffn_wu, L3_ffn_wd)
    return x

_drawn_inputs = setup_inputs


def setup_inputs(seed=0):
    import zlib

    import numpy as np

    out = dict(_drawn_inputs(seed))
    spreads = {'L0_xattn_b_in': (0.0, 0.1),
     'L0_xattn_b_out': (0.0, 0.1),
     'L0_xattn_gamma': (1.0, 0.2),
     'L0_xattn_beta': (0.0, 0.1),
     'L2_xattn_ln_w': (1.0, 0.6),
     'L2_xattn_ln_b': (0.0, 0.926),
     'L2_xattn_q_in_scale': (0.05000000074505806, 0.6),
     'L2_xattn_qx_in_scale': (0.05000000074505806, 0.6),
     'L2_xattn_k_in_scale': (0.05000000074505806, 0.6),
     'L2_xattn_v_in_scale': (0.05000000074505806, 0.6),
     'L2_xattn_qln_w': (1.0, 0.6),
     'L2_xattn_qln_b': (0.0, 2.0),
     'L2_xattn_kln_w': (1.0, 0.6),
     'L2_xattn_kln_b': (0.0, 2.0),
     'L2_xattn_qxln_w': (1.0, 0.6),
     'L2_xattn_qxln_b': (0.0, 2.0),
     'L2_xattn_kxln_w': (1.0, 0.6),
     'L2_xattn_kxln_b': (0.0, 2.0),
     'L2_xattn_proj_smooth': (0.05000000074505806, 0.551),
     'L3_xattn_q_b': (0.0, 2.0),
     'L3_xattn_k_b': (0.0, 0.1),
     'L3_xattn_v_b': (0.0, 0.1),
     'L3_xattn_k_img_b': (0.0, 2.0),
     'L3_xattn_v_img_b': (0.0, 2.0),
     'L3_xattn_o_b': (0.0, 2.0),
     'L3_xattn_norm_q_w': (1.0, 0.6),
     'L3_xattn_norm_k_w': (1.0, 0.2),
     'L3_xattn_norm_k_img_w': (1.0, 0.6),
     'L3_ffn_gate_bias': (0.0, 2.0)}
    factors = {'L1_ffn_gate_w': 8.0,
     'L1_ffn_w1': 8.0,
     'L1_ffn_w2': 8.0,
     'L1_ffn_w3': 8.0,
     'L1_ffn_sw1': 6.137,
     'L1_ffn_sw2': 6.049,
     'L1_ffn_sw3': 6.071,
     'L3_xattn_q_w': 47.157,
     'L3_xattn_k_img_w': 43.751,
     'L3_xattn_v_img_w': 23.645,
     'L3_xattn_o_w': 21.413,
     'L3_ffn_centroids': 64.0,
     'L3_ffn_wg_s': 64.0,
     'L3_ffn_wu_s': 64.0,
     'L3_ffn_wd_s': 64.0,
     'L3_ffn_wg': 57.381,
     'L3_ffn_wu': 50.547,
     'L3_ffn_wd': 50.785}
    for name, (base, spread) in spreads.items():
        noise = np.random.default_rng([zlib.crc32(name.encode()), seed]).standard_normal(out[name].shape)
        drawn = base * np.exp(spread * noise) if base else spread * noise
        out[name] = jnp.asarray(drawn.astype(out[name].dtype))
    for name, factor in factors.items():
        out[name] = (out[name] * factor).astype(out[name].dtype)
    return out
```

```python
from contextlib import ExitStack

import numpy as np

import concourse.bass as bass
from concourse import mybir

F32 = mybir.dt.float32
BF16 = mybir.dt.bfloat16
U32 = mybir.dt.uint32
U16 = mybir.dt.uint16
I32 = mybir.dt.int32
ALU = mybir.AluOpType
ACT = mybir.ActivationFunctionType
AX = mybir.AxisListType

P = 128
B, S, D = 4, 256, 256
TOK = B * S
NT = TOK // P
DC = D // P
SC = 64
CTX = B * SC
TPB = S // P
BANK = 512
HALF = 4

E0, K0, CAP = 32, 6, 96
E1, K1 = 8, 2
E3, K3 = 16, 2
I = 128
UNIT = DC * 2 * I + D
SINK = CAP

H1, HD1, R1, KVC, QC, LOOK = 16, 128, 64, 64, 96, 8
NH2, G2, D2 = 16, 8, 128
HPG = NH2 // G2
GW = 8 * P
FFN2 = 704
FC2 = -(-FFN2 // P)
H3, HD3 = 16, 16
NEG = -1e30
ROUND = 1.5 * 2.0 ** 23
FP8_MAX = 448.0


CONST = [("ident", P), ("ones", P), ("before", P), ("iota_e", 32), ("iota_c", CAP), ("cos_q", S), ("sin_q", S),
         ("cos_k", SC), ("sin_k", SC), ("head16", 8), ("pair", D), ("slot1", 1), ("tokpart", 1), ("half", 8),
         ("minus_half", 16)]
CTXP = [("ctx", DC * CTX), ("twice", DC * B * 2 * SC)]
L0A = [("w_in", DC * D), ("w_out", DC * D), ("b_in", DC), ("b_out", D), ("gamma", D), ("beta", D), ("decay", 1),
       ("gate0", DC * E0), ("bias0", E0), ("gate1", DC * E1), ("gate3", DC * E3), ("bias3", E3)]
L1A = [("kvc", DC * KVC), ("dq", DC * QC), ("uq", H1 * QC), ("qr", H1 * R1), ("qr_swap", H1 * R1),
       ("uk", H1 * HD1), ("kr", P), ("kr_swap", P), ("uv", H1 * HD1), ("wo", H1 * D)]
L2A = [("ln_w", DC), ("ln_b", DC), ("q_in", DC), ("qx_in", DC), ("k_in", DC), ("v_in", DC),
       ("wq_s", 1), ("wqx_s", 1), ("wk_s", 1), ("wv_s", 1), ("p_w", 1), ("p_in", 1),
       ("qln_w", 1), ("qln_b", 1), ("kln_w", 1), ("kln_b", 1), ("qxln_w", 1), ("qxln_b", 1), ("kxln_w", 1),
       ("kxln_b", 1), ("smooth", 2 * NH2)]
L2G = [("w", DC * GW), ("proj", 2 * HPG * D)]
L2F = [("w1", DC * FFN2), ("w2", DC * FFN2), ("w3", FC2 * D)]
L3A = [("qw", DC * D), ("kw", DC * D), ("vw", DC * D), ("ow", DC * D), ("qb", D), ("kb", D), ("vb", D), ("ob", D),
       ("nq", DC), ("nk", DC)]


def width(spec):
    return sum(n for _, n in spec)


def views(tile, spec, at=0):
    out = {}
    for name, n in spec:
        out[name] = tile[:, at:at + n]
        at += n
    return out


class Line:

    def __init__(self, engine, sem):
        self.engine, self.sem, self.count, self.met = engine, sem, 0, {}

    def wait(self, ticks):
        for t in ticks:
            if t is None:
                continue
            if isinstance(t, list):
                self.wait(t)
                continue
            sem, value = t
            if self.met.get(id(sem), 0) < value:
                self.met[id(sem)] = value
                self.engine.wait_ge(sem, value)

    def __call__(self, after, *steps):
        self.wait(after)
        for step in steps:
            last = step(self.engine)
        last.then_inc(self.sem, 1)
        self.count += 1
        return (self.sem, self.count)

    def dma(self, after, arrival, step):
        self.wait(after)
        step(self.engine).then_inc(arrival.sem, 16)
        arrival.count += 16
        return (arrival.sem, arrival.count)


class Arrival:

    def __init__(self, sem):
        self.sem, self.count = sem, 0


class Ring:

    def __init__(self, buffers, after=()):
        self.buffers, self.free, self.idle = buffers, [list(after) for _ in buffers], list(range(len(buffers)))

    def take(self):
        n = self.idle.pop(0)
        return n, self.buffers[n], self.free[n]

    def give(self, n, *ticks):
        self.free[n] = list(ticks)
        self.idle.append(n)


def skew(n, *stages, oldest_first=False):
    for r in range(n + len(stages) - 1):
        for k, stage in sorted(enumerate(stages), reverse=oldest_first, key=lambda pair: pair[0]):
            if 0 <= r - k < n:
                stage(r - k)


def over(ap, n):
    return ap.unsqueeze(2).broadcast_to([ap.shape[0], ap.shape[1], n])


def under(ap, n):
    return ap.unsqueeze(1).broadcast_to([ap.shape[0], n, ap.shape[1]])


class Core:

    def __init__(self, nc, ctx):
        self.nc, self.ctx = nc, ctx
        self.pe, self.dve, self.act, self.pool, self.sp = (
            Line(engine, ctx.enter_context(nc.semaphore(name))) for engine, name in (
                (nc.tensor, "matmul_done"), (nc.vector, "vector_done"), (nc.scalar, "scalar_done"),
                (nc.gpsimd, "pool_done"), (nc.sync, "sync_done")))
        self.banks = Ring([ctx.enter_context(nc.psum_tensor(f"bank{n}", [P, BANK], F32)) for n in range(8)])
        self.named = {}

    def sb(self, name, shape, dt=F32, scope=None):
        self.named[name] = self.named.get(name, 0) + 1
        if self.named[name] > 1:
            name += f"_{self.named[name]}"
        return (scope or self.ctx).enter_context(self.nc.sbuf_tensor(name, shape, dt))

    def arrival(self, name):
        return Arrival(self.ctx.enter_context(self.nc.semaphore(name)))

    def load(self, name, dst, src, after=()):
        return self.sp.dma(after, self.arrival(name), lambda e: e.dma_start(dst, src))

    def mm(self, out, pairs, after, start=True, stop=True, shared=False):
        builds = []
        for n, (lhs, rhs) in enumerate(pairs):
            builds.append(lambda e, a=lhs, b=rhs, s=start and n == 0, t=stop and n == len(pairs) - 1:
                          e.matmul(out, a, b, start=s, stop=t, skip_group_check=shared))
        return self.pe(after, *builds)

    def turn(self, jobs, after):
        ident = self.c["ident"]
        return self.pe(after, *[lambda e, o=o, i=i: e.transpose(o, i, ident[0:i.shape[0], 0:i.shape[0]])
                                for o, i in jobs])

    def copy(self, line, out, src, after):
        if line is self.act:
            return line(after, lambda e: e.activation(out, src, ACT.Copy))
        return line(after, lambda e: e.tensor_copy(out, src))


def moments(k, src, n, stats, mv, rstd, eps, after):
    rows = src[0].shape[0]
    done = []
    for i in range(n):
        done.append(k.dve([after[i] if isinstance(after, list) and len(after) == n else after],
                          lambda e, i=i: e.bn_stats(stats[0:rows, i, :], src[i])))
    t = k.dve([done[-1]], *[lambda e, i=i: e.bn_aggr(mv[0:rows, i, :], stats[0:rows, i, :]) for i in range(n)])
    t = k.dve([t], lambda e: e.tensor_scalar(rstd[0:rows, 0:n], mv[0:rows, 0:n, 1], eps, None, ALU.add))
    t = k.pool([t], lambda e: e.tensor_tensor(rstd[0:rows, 0:n], rstd[0:rows, 0:n], k.c["minus_half"][0:rows, 0:n],
                                              ALU.pow))
    return t


def normalise(k, src, out, after, eps=1e-5):
    t = moments(k, [src[:, i, :] for i in range(NT)], NT, k.stats, k.mv, k.rstd, eps, after)
    line = [k.dve, k.pool]
    return [line[i % 2]([t], lambda e, i=i: e.tensor_scalar(
        out[:, i, :], src[:, i, :], k.mv[:, i, 0:1], k.rstd[:, i:i + 1], ALU.subtract, ALU.mult)) for i in range(NT)]


def transpose_rows(k, rows, cols, ready, scale=None, bias=None, free=()):
    ticks = [[None, None] for _ in range(DC)]
    for half in range(NT // HALF):
        for j in range(DC):
            n, bank, freed = k.banks.take()
            t = k.turn([(bank[:, i * P:(i + 1) * P], rows[:, half * HALF + i, j * P:(j + 1) * P])
                        for i in range(HALF)], [freed, ready[half * HALF:(half + 1) * HALF]])
            dst = cols[:, j, half * BANK:(half + 1) * BANK]
            if scale is None:
                u = k.copy(k.act if j else k.dve, dst, bank[:], [t, *free])
            else:
                u = k.act([t, *free], lambda e, j=j, dst=dst, bank=bank: e.activation(
                    dst, bank[:], ACT.Identity, bias=bias[:, j:j + 1], scale=scale[:, j:j + 1]))
            k.banks.give(n, u)
            ticks[j][half] = u
    return ticks


def both(ticks, tile):
    return [t[tile // HALF] for t in ticks]


def norm_pass(k, x_ready):
    k.rows_ready = normalise(k, k.x, k.rows, x_ready)
    k.cols_ready = transpose_rows(k, k.rows, k.cols, k.rows_ready)


def tile_cols(k, t, cols=None):
    cols = cols if cols is not None else k.cols
    return [cols[:, j, t * P:(t + 1) * P] for j in range(DC)]


def layer0_attention(k, x_ready):
    with ExitStack() as scope:
        w = k.l0
        seq = k.sb("l0_seq", [P, DC, CTX], scope=scope)
        states = k.sb("l0_states", [P, DC, CTX], scope=scope)
        keep = k.sb("l0_keep", [P, 1], scope=scope)
        keeps = k.sb("l0_keeps", [P, SC], scope=scope)
        mean_state = k.sb("l0_mean_state", [P, DC, B], scope=scope)
        mean_wide = k.sb("l0_mean_wide", [P, DC * B, P], scope=scope)
        y = k.sb("l0_y", [P, NT, D], scope=scope)
        k.rows_ready = normalise(k, k.x, k.rows, x_ready)
        t = k.act([k.l0_in], lambda e: e.activation(keep[:], w["decay"], ACT.Sigmoid))
        kept = k.dve([t, k.const_in], lambda e: e.tensor_scalar(keeps[:], k.c["ones"][:, 0:SC], keep[:, 0:1], None,
                                                                ALU.mult))
        n, bank, freed = k.banks.take()
        w_in = w["w_in"].rearrange("p (j e) -> p j e", j=DC)
        ctx = k.ctxt["ctx"].rearrange("p (j t) -> p j t", j=DC)
        for i in range(DC):
            t = k.mm(bank[:, i * CTX:(i + 1) * CTX], [(w_in[:, j, i * P:(i + 1) * P], ctx[:, j, :])
                                                      for j in range(DC)], [freed, k.l0_in, k.ctx_in])
        ticks = []
        for i in range(DC):
            ticks.append(k.act([t], lambda e, i=i: e.activation(seq[:, i, :], bank[:, i * CTX:(i + 1) * CTX],
                                                                ACT.Identity, bias=w["b_in"][:, i:i + 1])))
        k.banks.give(n, *ticks)
        for i in range(DC):
            for b in range(B):
                t = k.dve([ticks[i], kept], lambda e, i=i, b=b: e.tensor_tensor_scan(
                    states[:, i, b * SC:(b + 1) * SC], keeps[:], seq[:, i, b * SC:(b + 1) * SC], 0.0, ALU.mult,
                    ALU.add))
        t = k.dve([t], lambda e: e.tensor_reduce(
            mean_state[:].rearrange("p j b -> p (j b)"), states[:].rearrange("p j (b t) -> p (j b) t", b=B), AX.X,
            ALU.add))
        t = k.dve([t], lambda e: e.tensor_scalar(
            mean_wide[:], over(mean_state[:].rearrange("p j b -> p (j b)"), P), 1.0 / SC, None, ALU.mult))
        w_out = w["w_out"].rearrange("p (j e) -> p j e", j=DC)
        wide = t
        added = []
        for b in range(B):
            n, bank, freed = k.banks.take()
            t = k.mm(bank[:, 0:D], [(mean_wide[:, j * B + b, :], w_out[:, j, :]) for j in range(DC)]
                     + [(k.c["ones"][0:1, :], w["b_out"][0:1, :])], [freed, wide, k.l0_in])
            for i in range(b * TPB, (b + 1) * TPB):
                t2 = k.dve([t, k.rows_ready[i]], lambda e, i=i, bank=bank: e.tensor_tensor(
                    y[:, i, :], k.rows[:, i, :], bank[:, 0:D], ALU.add))
                added.append(t2)
            k.banks.give(n, t2)
        done = normalise(k, y, y, added)
        out = []
        for i in range(NT):
            t = k.pool([done[i]], lambda e, i=i: e.tensor_tensor(y[:, i, :], y[:, i, :], w["gamma"], ALU.mult))
            t = k.pool([t], lambda e, i=i: e.tensor_tensor(y[:, i, :], y[:, i, :], w["beta"], ALU.add))
            out.append(k.dve([t], lambda e, i=i: e.tensor_tensor(k.x[:, i, :], k.x[:, i, :], y[:, i, :], ALU.add)))
    return out


def expert_weights(k, slot):
    return slot[:, 0:DC * 2 * I].rearrange("p (j n) -> p j n", j=DC), slot[:, DC * 2 * I:UNIT]


def fetch_expert(k, e):
    n, slot, freed = k.experts.take()
    k.fetched[e] = (n, slot, k.sp.dma(freed, k.expert_arrival[n], lambda q: q.dma_start(slot[:], k.expert_dram[e])))


def use_expert(k, e):
    return k.fetched.pop(e)


def drop_expert(k, n, *ticks):
    k.experts.give(n, *ticks)
    if k.next_expert < k.n_experts:
        fetch_expert(k, k.next_expert)
        k.next_expert += 1


def routing(k, scope, n_exp, top, logits_ticks, scores, biased, biased_ready):
    best = k.sb("route_best", [P, NT, 8], scope=scope)
    where = k.sb("route_where", [P, NT, 8], U32, scope=scope)
    where_f = k.sb("route_where_f", [P, NT, 8], scope=scope)
    hits = k.sb("route_hits", [P, NT, top, n_exp], scope=scope)
    mask = k.sb("route_mask", [P, NT, n_exp], scope=scope)
    t = k.dve([biased_ready], *[lambda e, i=i: e.max(best[:, i, :], biased[:, i, :]) for i in range(NT)])
    t = k.dve([t], *[lambda e, i=i: e.max_index(where[:, i, :], best[:, i, :], biased[:, i, :]) for i in range(NT)])
    t = k.dve([t], lambda e: e.tensor_copy(where_f[:], where[:]))
    t = k.dve([t], *[lambda e, i=i: e.tensor_tensor(
        hits[:, i, :, :], over(where_f[:, i, 0:top], n_exp), under(k.c["iota_e"][:, 0:n_exp], top), ALU.is_equal)
        for i in range(NT)])
    t = k.dve([t], lambda e: e.tensor_reduce(mask[:], hits[:].rearrange("p t k e -> p t e k"), AX.X, ALU.add))
    return mask, t


def gate_logits(k, gate, n_exp, logits, ready):
    n, bank, freed = k.banks.take()
    gate = gate.rearrange("p (j e) -> p j e", j=DC)
    for i in range(NT):
        t = k.mm(bank[:, i * n_exp:(i + 1) * n_exp], [(c, gate[:, j, :]) for j, c in enumerate(tile_cols(k, i))],
                 [freed, both(ready, i), k.l0_in])
    u = k.copy(k.dve, logits[:].rearrange("p t e -> p (t e)"), bank[:, 0:NT * n_exp], [t])
    k.banks.give(n, u)
    return u


class Swiglu:

    def __init__(self, k, scope, depth=3):
        self.k = k
        self.gated = Ring([k.sb(f"swi_gated{n}", [P, I], scope=scope) for n in range(depth)])
        self.inner = Ring([k.sb(f"swi_inner{n}", [P, I], scope=scope) for n in range(depth)])
        self.turned = Ring([k.sb(f"swi_turned{n}", [P, I], scope=scope) for n in range(depth)])

    def open(self, job):
        k, m = self.k, job["m"]
        gu, _ = expert_weights(k, job["slot"])
        nb, bank, freed = k.banks.take()
        t = k.mm(bank[0:m, 0:2 * I], [(c, gu[:, j, :]) for j, c in enumerate(job["cols"])], [freed, job["after"]])
        ng, gated, gfree = self.gated.take()
        t1 = k.act([t, gfree, job.get("s_ready")], lambda e, s=job["s"]: e.activation(
            gated[0:m, :], bank[0:m, 0:I], ACT.Silu, scale=s))
        ni, inner, ifree = self.inner.take()
        t2 = k.dve([t1, ifree, job.get("s_ready")], lambda e, w=job["w"]: e.scalar_tensor_tensor(
            inner[0:m, :], bank[0:m, I:2 * I], w, gated[0:m, :], ALU.mult, ALU.mult))
        self.gated.give(ng, t2)
        if job.get("clip"):
            t2 = k.dve([t2], lambda e, c=job["clip"]: e.tensor_scalar(inner[0:m, :], inner[0:m, :], c, -c, ALU.min,
                                                                      ALU.max))
        job.update(nb=nb, bank=bank, ni=ni, inner=inner, inner_ready=t2, gu_done=t)

    def flip(self, job):
        k, m, bank = self.k, job["m"], job["bank"]
        t = k.turn([(bank[:, 2 * I:2 * I + m], job["inner"][0:m, :])], [job["inner_ready"]])
        self.inner.give(job["ni"], t)
        nt, turned, tfree = self.turned.take()
        u = k.copy(k.act if job.get("evac") == "act" else k.dve, turned[:, 0:m], bank[:, 2 * I:2 * I + m], [t, tfree])
        k.banks.give(job["nb"], u)
        job.update(nt=nt, turned=turned, turned_ready=u)

    def close(self, job, out, after, start, stop, shared=False):
        k, m = self.k, job["m"]
        _, down = expert_weights(k, job["slot"])
        t = k.mm(out, [(job["turned"][:, 0:m], down)], [job["turned_ready"], after], start, stop, shared)
        self.turned.give(job["nt"], t)
        return t


def layer0_ffn(k, x_ready):
    norm_pass(k, x_ready)
    nc = k.nc
    with ExitStack() as scope:
        sb = lambda name, shape, dt=F32: k.sb(name, shape, dt, scope)
        n_rows = TOK + SINK
        h_rows = nc.dram_tensor("h_rows", [n_rows, D], F32, kind="Internal").ap()
        sums = [nc.dram_tensor(f"sum{n}", [n_rows, D], F32, kind="Internal").ap() for n in range(2)]
        tiled = lambda dram: dram[0:TOK, :].rearrange("(t p) d -> p t d", p=P)
        zeros = sb("f0_zeros", [SINK, D])
        shared = sb("f0_shared", [P, NT, D])
        second = sb("f0_second", [P, NT, D])
        t = k.pool([], lambda e: e.memset(zeros[:], 0.0))
        rows_out = k.arrival("h_rows_out")
        k.sp.dma([k.rows_ready], rows_out, lambda e: e.dma_start(tiled(h_rows), k.rows[:]))
        k.sp.dma([t], rows_out, lambda e: e.dma_start(h_rows[TOK:n_rows, :], zeros[:]))
        rows_stored = (rows_out.sem, rows_out.count)
        sum_out = [k.arrival(f"sum{n}_out") for n in range(2)]
        k.sp.dma([x_ready], sum_out[0], lambda e: e.dma_start(tiled(sums[0]), k.x[:]))
        k.sp.dma([t], sum_out[0], lambda e: e.dma_start(sums[0][TOK:n_rows, :], zeros[:]))
        k.sp.dma([t], sum_out[1], lambda e: e.dma_start(sums[1][TOK:n_rows, :], zeros[:]))

        logits = sb("f0_logits", [P, NT, E0])
        size = sb("f0_size", [P, NT, E0])
        small = sb("f0_small", [P, NT, E0])
        one_plus = sb("f0_one_plus", [P, NT, E0])
        log1p = sb("f0_log1p", [P, NT, E0])
        flat = sb("f0_flat", [P, NT, E0])
        scores = sb("f0_scores", [P, NT, E0])
        biased = sb("f0_biased", [P, NT, E0])
        halves = sb("f0_halves", [P, NT, E0])
        h = k.pool([], lambda e: e.memset(halves[:], 0.5))
        lg = gate_logits(k, k.l0["gate0"], E0, logits, k.cols_ready)
        t = k.act([lg], lambda e: e.activation(size[:], logits[:], ACT.Abs))
        z = k.act([t], lambda e: e.activation(small[:], size[:], ACT.Exp, scale=-1.0))
        t = k.dve([z], lambda e: e.tensor_scalar(one_plus[:], small[:], 1.0, None, ALU.add))
        ln = k.act([t], lambda e: e.activation(log1p[:], one_plus[:], ACT.Ln))
        t = k.dve([t, ln], lambda e: e.tensor_scalar(one_plus[:], one_plus[:], 1.0, None, ALU.subtract))
        t = k.dve([t], lambda e: e.tensor_scalar(flat[:], one_plus[:], 0.0, None, ALU.is_equal))
        t = k.dve([t], lambda e: e.tensor_tensor(one_plus[:], one_plus[:], flat[:], ALU.add))
        t = k.dve([t], lambda e: e.reciprocal(one_plus[:], one_plus[:]))
        t = k.dve([t], lambda e: e.tensor_tensor(log1p[:], log1p[:], one_plus[:], ALU.mult))
        t = k.dve([t], lambda e: e.tensor_tensor(log1p[:], log1p[:], flat[:], ALU.add))
        t = k.dve([t], lambda e: e.tensor_tensor(log1p[:], log1p[:], small[:], ALU.mult))
        t = k.dve([t], lambda e: e.scalar_tensor_tensor(log1p[:], logits[:], 0.0, log1p[:], ALU.max, ALU.add))
        t = k.pool([t, h], lambda e: e.tensor_tensor(scores[:], log1p[:], halves[:], ALU.pow))
        t = k.dve([t], lambda e: e.tensor_tensor(biased[:], scores[:], under(k.l0["bias0"], NT), ALU.add))
        mask, t = routing(k, scope, E0, K0, lg, scores, biased, t)

        weight = sb("f0_weight", [P, NT, E0])
        total = sb("f0_total", [P, NT])
        w = k.dve([t], lambda e: e.tensor_tensor(weight[:], mask[:], scores[:], ALU.mult))
        w = k.dve([w], lambda e: e.tensor_reduce(total[:], weight[:], AX.X, ALU.add))
        w = k.dve([w], lambda e: e.reciprocal(total[:], total[:]))
        w = k.dve([w], lambda e: e.tensor_scalar(total[:], total[:], 1.5, None, ALU.mult))
        w = k.dve([w], lambda e: e.tensor_tensor(weight[:], weight[:], over(total[:], E0), ALU.mult))

        before = sb("f0_before", [P, NT, E0])
        b = k.pool([], lambda e: e.memset(before[:, 0, :], 0.0))
        for i in range(1, NT):
            b = k.dve([t, b], lambda e, i=i: e.tensor_tensor(before[:, i, :], before[:, i - 1, :], mask[:, i - 1, :],
                                                             ALU.add))
        n, bank, freed = k.banks.take()
        for i in range(NT):
            q = k.mm(bank[:, i * E0:(i + 1) * E0], [(k.c["before"], mask[:, i, :]), (k.c["ones"], before[:, i, :])],
                     [freed, b, t])
        place = sb("f0_place", [P, NT, E0])
        u = k.dve([t], lambda e: e.tensor_scalar(place[:], mask[:], -999.0, 999.0, ALU.mult, ALU.add))
        u = k.dve([u, q], lambda e: e.tensor_tensor(place[:].rearrange("p t e -> p (t e)"),
                                                    place[:].rearrange("p t e -> p (t e)"), bank[:, 0:NT * E0],
                                                    ALU.add))
        k.banks.give(n, u)

        facts = sb("f0_facts", [P, NT, E0, 5], BF16)
        rest = sb("f0_rest", [P, NT, E0])
        f = k.pool([k.const_in], *[lambda e, i=i: e.memset(facts[:, i, :, 1], float(i * P)) for i in range(NT)])
        f = k.dve([w, f], lambda e: e.tensor_scalar(
            facts[:, :, :, 0].rearrange("p t e -> p (t e)"), weight[:].rearrange("p t e -> p (t e)"), 0.0,
            k.c["tokpart"], ALU.mult, ALU.add))
        f = k.dve([f], lambda e: e.tensor_copy(facts[:, :, :, 2], weight[:]))
        f = k.dve([f], lambda e: e.tensor_tensor(rest[:], weight[:], facts[:, :, :, 2], ALU.subtract))
        f = k.dve([f], lambda e: e.tensor_copy(facts[:, :, :, 3], rest[:]))
        f = k.dve([f], lambda e: e.tensor_tensor(rest[:], rest[:], facts[:, :, :, 3], ALU.subtract))
        f = k.dve([f], lambda e: e.tensor_copy(facts[:, :, :, 4], rest[:]))

        picks = Ring([sb(f"f0_pick{n}", [P, E0, CAP], BF16) for n in range(2)])
        nt_, tbank, tfree = k.banks.take()
        for i in range(NT):
            np_, pick, pfree = picks.take()
            t1 = k.dve([u, pfree], lambda e, i=i, pick=pick: e.tensor_tensor(
                pick[:], over(place[:, i, :], CAP), under(k.c["iota_c"], E0), ALU.is_equal))
            builds = [lambda e, i=i, x=x, pick=pick: e.matmul(
                tbank[0:CAP, x * 5:(x + 1) * 5], pick[:, x, :], facts[:, i, x, :], start=(i == 0 and x == 0),
                stop=(i == NT - 1), skip_group_check=True) for x in range(E0)]
            t2 = k.pe([t1, f, tfree], *builds)
            picks.give(np_, t2)
        table = sb("f0_table", [CAP, E0, 5])
        number = sb("f0_number", [CAP, E0])
        empty = sb("f0_empty", [CAP, E0])
        index = sb("f0_index", [CAP, E0], U32)
        slot_w = sb("f0_slot_w", [CAP, E0])
        t = k.dve([t2], lambda e: e.tensor_copy(table[:].rearrange("p e f -> p (e f)"), tbank[0:CAP, 0:E0 * 5]))
        k.banks.give(nt_, t)
        t1 = k.dve([t], lambda e: e.tensor_tensor(number[:], table[:, :, 0], table[:, :, 1], ALU.add))
        t1 = k.dve([t1], lambda e: e.tensor_scalar(empty[:], number[:], 0.0, k.c["slot1"][0:CAP, :], ALU.is_equal,
                                                   ALU.mult))
        t1 = k.dve([t1], lambda e: e.scalar_tensor_tensor(number[:], number[:], -1.0, empty[:], ALU.add, ALU.add))
        indexed = k.dve([t1], lambda e: e.tensor_copy(index[:], number[:]))
        t1 = k.dve([t], lambda e: e.tensor_tensor(slot_w[:], table[:, :, 2], table[:, :, 3], ALU.add))
        weighed = k.dve([t1], lambda e: e.tensor_tensor(slot_w[:], slot_w[:], table[:, :, 4], ALU.add))

        swi = Swiglu(k, scope)
        n, slot, came = use_expert(k, 0)
        jobs = [dict(cols=tile_cols(k, i), m=P, slot=slot, s=1.0, w=1.0, clip=10.0,
                     after=[came, *both(k.cols_ready, i)]) for i in range(NT)]
        outs = {}

        def finish_shared(i):
            if i % 2 == 0:
                outs[i] = k.banks.take()
            nb, bank, freed = outs[i - i % 2]
            half = bank[:, (i % 2) * D:(i % 2 + 1) * D]
            t = swi.close(jobs[i], half, freed, True, True)
            if i % 2:
                outs["mm"] = t
                outs["t"] = k.copy(k.act, shared[:, i - 1:i + 1, :], bank[:].rearrange("p (t d) -> p t d", t=2), [t])
                k.banks.give(nb, outs["t"])

        skew(NT, lambda i: swi.open(jobs[i]), lambda i: swi.flip(jobs[i]), finish_shared)
        drop_expert(k, n, outs["mm"])
        k.sp.dma([outs["t"]], sum_out[1], lambda e: e.dma_start(tiled(sums[1]), shared[:]))
        stored = [(s.sem, s.count) for s in sum_out]

        depth = 4
        got = Ring([sb(f"f0_got{n}", [CAP, D]) for n in range(depth)])
        got_arrival = [k.arrival(f"f0_got{n}_in") for n in range(depth)]
        tcols = Ring([sb(f"f0_cols{n}", [P, DC, CAP]) for n in range(3)])
        ys = Ring([sb(f"f0_ys{n}", [CAP, D]) for n in range(depth)])
        added = [k.arrival(f"f0_added{n}") for n in range(2)]
        jobs = [dict(m=CAP, evac="act") for _ in range(E0)]

        def gather(x):
            n, buf, freed = got.take()
            jobs[x].update(ng=n, got=buf, came=k.pool.dma(
                [freed, indexed, rows_stored], got_arrival[n], lambda e: e.indirect_dma_start(
                    buf[:], None, h_rows, bass.IndirectOffsetOnAxis(ap=index[:, x:x + 1], axis=0))))

        def flip_in(x):
            job = jobs[x]
            nb, bank, freed = k.banks.take()
            t = k.turn([(bank[:, j * P:j * P + CAP], job["got"][:, j * P:(j + 1) * P]) for j in range(DC)],
                       [freed, job["came"]])
            got.give(job["ng"], t)
            nc_, cols, cfree = tcols.take()
            u = k.copy(k.dve, cols[:], bank[:, 0:DC * P].rearrange("p (j n) -> p j n", j=DC)[:, :, 0:CAP], [t, cfree])
            k.banks.give(nb, u)
            ns, slot, arrived = use_expert(k, 1 + x)
            job.update(nc=nc_, cols=[cols[:, j, :] for j in range(DC)], ns=ns, slot=slot, after=[arrived, u],
                       s=1.0, w=slot_w[:, x:x + 1], s_ready=weighed)

        def first(x):
            swi.open(jobs[x])
            tcols.give(jobs[x]["nc"], jobs[x]["gu_done"])

        def add_back(x):
            job = jobs[x]
            nb, bank, freed = k.banks.take()
            t = swi.close(job, bank[0:CAP, 0:D], freed, True, True)
            drop_expert(k, job["ns"], t)
            ny, y, yfree = ys.take()
            u = k.copy(k.act, y[:], bank[0:CAP, 0:D], [t, yfree])
            k.banks.give(nb, u)
            a = added[x % 2]
            tick = k.pool.dma([u, stored[x % 2], (a.sem, a.count) if a.count else None, indexed], a,
                              lambda e: e.indirect_dma_start(
                sums[x % 2], bass.IndirectOffsetOnAxis(ap=index[:, x:x + 1], axis=0), y[:], None,
                compute_op=ALU.add))
            ys.give(ny, tick)

        skew(E0, gather, lambda x: None, flip_in, first, lambda x: swi.flip(jobs[x]), add_back)
        back = k.arrival("sums_in")
        every = [(a.sem, a.count) for a in added]
        k.sp.dma([every, x_ready], back, lambda e: e.dma_start(k.x[:], tiled(sums[0])))
        k.sp.dma([], back, lambda e: e.dma_start(second[:], tiled(sums[1])))
        done = (back.sem, back.count)
        out = [(k.dve if i % 2 else k.pool)([done], lambda e, i=i: e.tensor_tensor(
            k.x[:, i, :], k.x[:, i, :], second[:, i, :], ALU.add)) for i in range(NT)]
    return out


def layer1_attention(k, x_ready):
    norm_pass(k, x_ready)
    with ExitStack() as scope:
        sb = lambda name, shape, dt=F32: k.sb(name, shape, dt, scope)
        w, c, W = k.l1, k.c, k.l1_in
        scale = float(1.0 / np.sqrt(np.float32(HD1 + R1)))
        ctx = k.ctxt["ctx"].rearrange("p (j t) -> p j t", j=DC)
        kvc = sb("a1_kvc", [KVC, CTX])
        n, bank, freed = k.banks.take()
        t = k.mm(bank[0:KVC, 0:CTX], [(w["kvc"].rearrange("p (j n) -> p j n", j=DC)[:, j, :], ctx[:, j, :])
                                      for j in range(DC)], [freed, W, k.ctx_in])
        kvc_ready = k.copy(k.act, kvc[:], bank[0:KVC, 0:CTX], [t, x_ready])
        k.banks.give(n, kvc_ready)
        qc = sb("a1_qc", [QC, TOK])
        dq = w["dq"].rearrange("p (j n) -> p j n", j=DC)
        qc_ready = []
        for half in range(TOK // BANK):
            n, bank, freed = k.banks.take()
            sl = slice(half * BANK, (half + 1) * BANK)
            t = k.mm(bank[0:QC, :], [(dq[:, j, :], k.cols[:, j, sl]) for j in range(DC)],
                     [freed, W, [r[half] for r in k.cols_ready]])
            qc_ready.append(k.copy(k.dve, qc[:, sl], bank[0:QC, :], [t]))
            k.banks.give(n, qc_ready[-1])
        key_blocks = sb("a1_key_blocks", [P, B, 2 * SC])
        turn_a = sb("a1_turn_a", [P, CTX])
        turn_b = sb("a1_turn_b", [P, CTX])
        n, bank, freed = k.banks.take()
        t = k.mm(bank[:, 0:CTX], [(w["kr"][0:KVC, :], kvc[:])], [freed, W, kvc_ready])
        t = k.mm(bank[:, CTX:2 * CTX], [(w["kr_swap"][0:KVC, :], kvc[:])], [])
        by_b = lambda ap: ap.rearrange("p (b s) -> p b s", b=B)
        u1 = k.dve([t, x_ready], lambda e: e.tensor_tensor(by_b(turn_a[:]), by_b(bank[:, 0:CTX]),
                                                           under(c["cos_k"], B), ALU.mult))
        u2 = k.dve([t], lambda e: e.tensor_tensor(by_b(turn_b[:]), by_b(bank[:, CTX:2 * CTX]),
                                                  under(c["sin_k"], B), ALU.mult))
        k.banks.give(n, u2)
        z = k.pool([x_ready], lambda e: e.memset(key_blocks[:], 0.0))
        u = k.dve([u1, u2], lambda e: e.tensor_tensor(turn_a[:], turn_a[:], turn_b[:], ALU.add))
        blocks_ready = k.dve([u, z], *[lambda e, h=h: e.tensor_scalar(
            key_blocks[h * R1:(h + 1) * R1, :, h * SC:(h + 1) * SC], by_b(turn_a[h * R1:(h + 1) * R1, :]), scale, None,
            ALU.mult) for h in range(2)])
        kq = sb("a1_kq", [QC, B, H1, SC])
        vo = sb("a1_vo", [P, B, H1 // 2, D])
        knope = Ring([sb(f"a1_knope{n}", [P, CTX]) for n in range(3)])
        vhead = Ring([sb(f"a1_vhead{n}", [P, CTX]) for n in range(3)])
        uk = w["uk"][0:KVC, :].rearrange("p (h d) -> p h d", h=H1)
        uv = w["uv"][0:KVC, :].rearrange("p (h d) -> p h d", h=H1)
        uq = w["uq"].rearrange("p (h d) -> p h d", h=H1)
        wo = w["wo"].rearrange("p (h d) -> p h d", h=H1)
        heads = [dict() for _ in range(H1)]

        def head_kv(h):
            n, bank, freed = k.banks.take()
            t = k.mm(bank[:, 0:CTX], [(uk[:, h, :], kvc[:])], [freed, W, kvc_ready])
            t = k.mm(bank[:, CTX:2 * CTX], [(uv[:, h, :], kvc[:])], [])
            nk, kb, kf = knope.take()
            nv, vb, vf = vhead.take()
            line = k.act if h % 2 else k.dve
            t1 = k.copy(line, kb[:], bank[:, 0:CTX], [t, kf])
            t2 = k.copy(line, vb[:], bank[:, CTX:2 * CTX], [t, vf])
            k.banks.give(n, t2)
            heads[h].update(nk=nk, kb=kb, nv=nv, vb=vb, t1=t1, t2=t2)

        def head_fold(h):
            d = heads[h]
            n, bank, freed = k.banks.take()
            t = k.mm(bank[0:QC, 0:CTX], [(uq[:, h, :], d["kb"][:])], [freed, d["t1"]])
            knope.give(d["nk"], t)
            d["kq"] = k.act([t], lambda e: e.activation(kq[:, :, h, :], by_b(bank[0:QC, 0:CTX]), ACT.Copy, scale=scale))
            k.banks.give(n, d["kq"])
            lo = (h % 2) * SC
            d["vo"] = []
            for pair in range(B // 2):
                n, bank, freed = k.banks.take()
                for b in range(2):
                    bb = pair * 2 + b
                    t = k.mm(bank[lo:lo + SC, b * D:(b + 1) * D], [(d["vb"][:, bb * SC:(bb + 1) * SC], wo[:, h, :])],
                             [freed, d["t2"], W])
                d["vo"].append(k.copy(k.dve if pair else k.act, vo[lo:lo + SC, pair * 2:pair * 2 + 2, h // 2, :],
                                      bank[lo:lo + SC, :].rearrange("p (b d) -> p b d", b=2), [t]))
                k.banks.give(n, d["vo"][-1])
            vhead.give(d["nv"], t)

        skew(H1, head_kv, head_fold)
        kq_ready = [d["kq"] for d in heads]
        vo_ready = [d["vo"] for d in heads]
        qrot = sb("a1_qrot", [P, H1 // 2, BANK])
        part = Ring([sb(f"a1_part{n}", [P, BANK]) for n in range(3)])
        qr = w["qr"][0:QC, :].rearrange("p (h d) -> p h d", d=P)
        qrs = w["qr_swap"][0:QC, :].rearrange("p (h d) -> p h d", d=P)
        qrot_ready = [[None] * (H1 // 2) for _ in range(2)]
        by_s = lambda ap: ap.rearrange("p (b s) -> p b s", s=S)

        def rotate(half, free):
            sl = slice(half * BANK, (half + 1) * BANK)
            for pr in range(H1 // 2):
                ticks = []
                for src, tab, dst in ((qr, "cos_q", None), (qrs, "sin_q", part)):
                    n, bank, freed = k.banks.take()
                    t = k.mm(bank[:], [(src[:, pr, :], qc[:, sl])], [freed, W, qc_ready[half]])
                    if dst is None:
                        o, pf = qrot[:, pr, :], free
                    else:
                        npart, pbuf, pf = part.take()
                        o = pbuf[:]
                    ticks.append(k.dve([t, pf], lambda e, o=o, bank=bank, tab=tab: e.tensor_tensor(
                        by_s(o), by_s(bank[:]), under(c[tab], 2), ALU.mult)))
                    k.banks.give(n, ticks[-1])
                t = k.pool(ticks, lambda e: e.tensor_tensor(qrot[:, pr, :], qrot[:, pr, :], pbuf[:], ALU.add))
                part.give(npart, t)
                qrot_ready[half][pr] = t
        seg = sb("a1_seg", [P, NT])
        block = sb("a1_block", [P, NT, SC])
        under_seg = sb("a1_under", [P, NT, SC])
        t = k.dve([k.seg_in, x_ready], lambda e: e.tensor_copy(seg[:], k.seg_i[:]))
        keys = under(k.keys[:], NT)
        t1 = k.dve([t, k.const_in], lambda e: e.tensor_tensor(block[:], keys, over(seg[:], SC), ALU.is_le))
        t2 = k.dve([t1], lambda e: e.tensor_scalar(seg[:], seg[:], float(LOOK), None, ALU.subtract))
        t2 = k.dve([t2], lambda e: e.tensor_tensor(under_seg[:], keys, over(seg[:], SC), ALU.is_ge))
        t = k.dve([t1, t2], lambda e: e.tensor_tensor(block[:], block[:], under_seg[:], ALU.mult))
        block_ready = k.dve([t], lambda e: e.tensor_scalar(block[:], block[:], -1.0, -NEG, ALU.add, ALU.mult))

        soft = Soft(k, scope, k.l1_space, [kq_ready, vo_ready])
        jobs = [dict() for _ in range(NT)]

        def score(i):
            b, job = i // TPB, jobs[i]
            sbuf = soft.begin(job)
            for hb in range(2):
                n, bank, freed = k.banks.take()
                hs = slice(hb * 8, hb * 8 + 8)
                t = k.mm(bank[:], [(qc[:, i * P:(i + 1) * P], kq[:, b, hs, :].rearrange("p h s -> p (h s)"))],
                         [freed, qc_ready, kq_ready], stop=False, shared=True)
                for pr in range(4):
                    t = k.mm(bank[:, pr * P:(pr + 1) * P], [(qrot[:, hb * 4 + pr, (i % HALF) * P:(i % HALF + 1) * P],
                                                             key_blocks[:, b, :])],
                             [blocks_ready, qrot_ready[i // HALF][hb * 4 + pr]], start=False, stop=(pr == 3),
                             shared=True)
                u = k.dve([t, block_ready, job["free"]], lambda e, bank=bank, hs=hs: e.tensor_tensor(
                    sbuf[:, hs, :], bank[:].rearrange("p (h s) -> p h s", h=8), under(block[:, i, :], 8), ALU.add))
                k.banks.give(n, u)
            job["scored"] = t
            soft.shift(job, sbuf, [u])

        def out(i):
            b, job = i // TPB, jobs[i]
            n, bank, freed = k.banks.take()
            t = k.mm(bank[:, 0:D], [(job["pt"][:, pr, :], vo[:, b, pr, :]) for pr in range(H1 // 2)],
                     [freed, vo_ready, job["pt_ready"]])
            soft.end(job, t)
            job["x"] = k.dve([t], lambda e: e.tensor_tensor(k.x[:, i, :], k.x[:, i, :], bank[:, 0:D], ALU.add))
            k.banks.give(n, job["x"])

        rotate(0, [])

        def score_or_rotate(i):
            score(i)
            if i == HALF - 1:
                rotate(1, [jobs[i]["scored"]])

        skew(NT, score_or_rotate, lambda i: soft.power(jobs[i], 1.0), lambda i: soft.flip(jobs[i]), out)
    return [job["x"] for job in jobs]


class Soft:

    def __init__(self, k, scope, space=None, after=()):
        self.k, heads, depth, cols = k, 16, 3, 16 * SC
        space = space if space is not None else k.sb("soft_space", [P, 5 * cols], scope=scope)
        part = [space[:, n * cols:(n + 1) * cols] for n in range(5)]
        self.s = Ring([a.rearrange("p (h s) -> p h s", h=heads) for a in part[:depth]], after)
        self.pt = Ring([a.rearrange("p (r q) -> p r q", q=P) for a in part[depth:]], after)
        self.top = Ring([k.sb(f"soft_top{n}", [P, heads], scope=scope) for n in range(depth)])
        self.sum = Ring([k.sb(f"soft_sum{n}", [P, heads], scope=scope) for n in range(depth)])

    def begin(self, job):
        job["ns"], job["s"], free = self.s.take()
        job["free"] = list(free)
        return job["s"]

    def shift(self, job, src, after):
        k, s = self.k, job["s"]
        nt, top, tf = self.top.take()
        t = k.dve([after, tf], lambda e: e.tensor_reduce(top[:], src, AX.X, ALU.max))
        job["shifted"] = k.pool([t], lambda e: e.tensor_tensor(s, src, over(top[:], SC), ALU.subtract))
        self.top.give(nt, job["shifted"])

    def power(self, job, scale):
        k, s = self.k, job["s"]
        nm, total, mf = self.sum.take()
        t = k.act([job["shifted"]], lambda e: e.activation(s, s, ACT.Exp, scale=scale))
        u = k.dve([t, mf], lambda e: e.tensor_reduce(total[:], s, AX.X, ALU.add))
        u = k.dve([u], lambda e: e.reciprocal(total[:], total[:]))
        job["probs"] = k.pool([u], lambda e: e.tensor_tensor(s, s, over(total[:], SC), ALU.mult))
        self.sum.give(nm, job["probs"])

    def flip(self, job):
        k, s = self.k, job["s"]
        npt, pt, pf = self.pt.take()
        job.update(npt=npt, pt=pt, pt_ready=[])
        for hb in range(2):
            n, bank, freed = k.banks.take()
            t = k.turn([(bank[:, pr * P:(pr + 1) * P],
                         s[:, 2 * (hb * 4 + pr):2 * (hb * 4 + pr) + 2, :].rearrange("p h s -> p (h s)"))
                        for pr in range(4)], [freed, job["probs"]])
            u = k.copy(k.act, pt[:, hb * 4:hb * 4 + 4, :].rearrange("p a b -> p (a b)"), bank[:], [t, pf])
            k.banks.give(n, u)
            job["pt_ready"].append(u)
        self.s.give(job["ns"], t)

    def end(self, job, tick):
        self.pt.give(job["npt"], tick)


def dense_experts(k, scope, first, count, scales, weights, ready):
    swi = Swiglu(k, scope)
    acc = [k.banks.take() for _ in range(NT // 2)]
    jobs, used = [], {}
    for e in range(count):
        for i in range(NT):
            jobs.append(dict(e=e, i=i, m=P, s=scales(e, i), w=weights(e, i), s_ready=ready, cols=tile_cols(k, i),
                             evac="act" if i % 2 else "dve"))

    def open_(n):
        job = jobs[n]
        if job["i"] == 0:
            used[job["e"]] = use_expert(k, first + job["e"])
        job["slot"] = used[job["e"]][1]
        job["after"] = [used[job["e"]][2], *both(k.cols_ready, job["i"])]
        swi.open(job)

    def close(n):
        job = jobs[n]
        e, i = job["e"], job["i"]
        _, bank, freed = acc[i // 2]
        job["t"] = swi.close(job, bank[:, (i % 2) * D:(i % 2 + 1) * D], freed, e == 0 and i % 2 == 0,
                             e == count - 1, shared=True)
        if i == NT - 1:
            drop_expert(k, used[e][0], job["t"])

    skew(len(jobs), open_, lambda n: swi.flip(jobs[n]), close)
    out = []
    for i in range(NT):
        n, bank, _ = acc[i // 2]
        out.append(k.dve([jobs[-NT + i]["t"], k.cols_ready, jobs[-1]["t"]], lambda e, i=i, bank=bank: e.tensor_tensor(
            k.x[:, i, :], k.x[:, i, :], bank[:, (i % 2) * D:(i % 2 + 1) * D], ALU.add)))
        if i % 2:
            k.banks.give(n, out[-1])
    return out


def sigmoid_exact(k, out, src, after):
    t = k.dve(after, lambda e: e.tensor_scalar(out[:], src[:], -88.0, None, ALU.max))
    t = k.act([t], lambda e: e.activation(out[:], out[:], ACT.Exp, scale=-1.0))
    t = k.dve([t], lambda e: e.tensor_scalar(out[:], out[:], 1.0, None, ALU.add))
    return k.dve([t], lambda e: e.reciprocal(out[:], out[:]))


def layer1_ffn(k, x_ready):
    norm_pass(k, x_ready)
    with ExitStack() as scope:
        sb = lambda name, shape, dt=F32: k.sb(name, shape, dt, scope)
        logits = sb("f1_logits", [P, NT, E1])
        scores = sb("f1_scores", [P, NT, E1])
        lg = gate_logits(k, k.l0["gate1"], E1, logits, k.cols_ready)
        t = sigmoid_exact(k, scores, logits, [lg])
        mask, t = routing(k, scope, E1, K1, lg, scores, scores, t)
        t = k.dve([t], lambda e: e.tensor_tensor(scores[:], scores[:], mask[:], ALU.mult))
        pick = lambda e, i: 1.0 if e == 0 else scores[:, i, e - 1:e]
        return dense_experts(k, scope, 1 + E0, 1 + E1, pick, pick, t)


def layer3_ffn(k, x_ready):
    norm_pass(k, x_ready)
    with ExitStack() as scope:
        sb = lambda name, shape, dt=F32: k.sb(name, shape, dt, scope)
        logits = sb("f3_logits", [P, NT, E3])
        affinity = sb("f3_affinity", [P, NT, E3])
        biased = sb("f3_biased", [P, NT, E3])
        total = sb("f3_total", [P, NT])
        lg = gate_logits(k, k.l0["gate3"], E3, logits, k.cols_ready)
        t = sigmoid_exact(k, affinity, logits, [lg])
        t = k.dve([t], lambda e: e.tensor_tensor(biased[:], affinity[:], under(k.l0["bias3"], NT), ALU.add))
        mask, t = routing(k, scope, E3, K3, lg, affinity, biased, t)
        t = k.dve([t], lambda e: e.tensor_tensor(mask[:], affinity[:], mask[:], ALU.mult))
        t = k.dve([t], lambda e: e.tensor_reduce(total[:], mask[:], AX.X, ALU.add))
        t = k.dve([t], lambda e: e.tensor_scalar(total[:], total[:], 1e-9, None, ALU.add))
        t = k.dve([t], lambda e: e.reciprocal(total[:], total[:]))
        t = k.dve([t], lambda e: e.tensor_tensor(mask[:], mask[:], over(total[:], E3), ALU.mult))
        return dense_experts(k, scope, 1 + E0 + 1 + E1, 2 + E3, lambda e, i: 1.0,
                             lambda e, i: 0.1 if e < 2 else mask[:, i, e - 2:e - 1], t)


def round_fp8(k, y, m, s, out, after, line):
    t = k.dve(after, lambda e: e.tensor_scalar(m.bitcast(U16), y.bitcast(U16), 0x7F80, None, ALU.bitwise_and))
    t = k.dve([t], lambda e: e.tensor_scalar(m, m, 2.0 ** -6, 1.5 * 2.0 ** 20, ALU.max, ALU.mult))
    t = line([t], lambda e: e.tensor_tensor(s, y, m, ALU.add))
    return line([t], lambda e: e.tensor_tensor(out, s, m, ALU.subtract))


def layer2_attention(k, x_ready):
    with ExitStack() as scope:
        sb = lambda name, shape, dt=F32: k.sb(name, shape, dt, scope)
        w, W = k.l2, k.l2_in
        again = normalise(k, k.rows, k.rows, normalise(k, k.x, k.rows, x_ready))
        ln, acc = k.cols, k.rows
        ln_ready = transpose_rows(k, k.rows, ln, again, w["ln_w"], w["ln_b"], free=[W, x_ready])
        names = ("q", "qx", "k", "v")
        scaled = {n: sb(f"a2_in_{n}", [P, DC, TOK]) for n in names}
        inv = sb("a2_inv", [P, 4, DC])
        fold = sb("a2_fold", [P, 4, DC])
        early = scope.enter_context(ExitStack())
        y = Ring([k.sb(f"a2_y{n}", [P, TOK], BF16, early) for n in range(2)])
        m = Ring([k.sb(f"a2_m{n}", [P, TOK], BF16, early) for n in range(2)])
        in_ready = {}
        for q, name in enumerate(names):
            ti = k.dve([W, x_ready], lambda e, q=q, name=name: e.reciprocal(inv[:, q, :], w[f"{name}_in"]))
            tf = k.dve([W], lambda e, q=q, name=name: e.tensor_scalar(fold[:, q, :], w[f"{name}_in"],
                                                                    w[f"w{name}_s"], None, ALU.mult))
            for j in range(DC):
                ny, yb, yf = y.take()
                nm, mb, mf = m.take()
                t = k.act([ti, ln_ready[j], yf], lambda e, q=q, j=j, yb=yb: e.activation(
                    yb[:], ln[:, j, :], ACT.Copy, scale=inv[:, q, j:j + 1]))
                t = k.dve([t], lambda e, yb=yb: e.tensor_scalar(yb[:], yb[:], FP8_MAX, -FP8_MAX, ALU.min, ALU.max))
                dst = scaled[name][:, j, :]
                t = round_fp8(k, yb[:], mb[:], dst, dst, [t, mf], k.pool if j else k.dve)
                y.give(ny, t)
                m.give(nm, t)
                t = k.act([t, tf], lambda e, q=q, j=j, dst=dst: e.activation(dst, dst, ACT.Copy,
                                                                            scale=fold[:, q, j:j + 1]))
                in_ready.setdefault(name, []).append(t)
        early.close()
        used = list(in_ready.values())
        qt = Ring([sb(f"a2_qt{n}", [P, 2 * HPG, S]) for n in range(2)], used)
        qn = Ring([sb(f"a2_qn{n}", [P, 5, P]) for n in range(3)], used)
        ismooth = sb("a2_ismooth", [P, 2 * NH2])
        pscale = sb("a2_pscale", [P, 1])
        sm = k.dve([W], lambda e: e.reciprocal(ismooth[:], w["smooth"]))
        ps = k.dve([W], lambda e: e.tensor_tensor(pscale[:], w["p_in"], w["p_w"], ALU.mult))
        ctx = k.ctxt["ctx"].rearrange("p (j t) -> p j t", j=DC)
        twice = k.ctxt["twice"].rearrange("p (j b t) -> p j b t", j=DC, b=B)
        softscale = float(1.0 / np.sqrt(D2))

        kt = Ring([sb(f"a2_kt{n}", [P, S]) for n in range(2)])
        vs = Ring([sb(f"a2_vs{n}", [P, TPB, D2]) for n in range(3)])
        kx = Ring([sb(f"a2_kx{n}", [P, CTX]) for n in range(2)])
        kxn = Ring([sb(f"a2_kxn{n}", [P, CTX // P, D2]) for n in range(1)])
        vx = Ring([sb(f"a2_vx{n}", [P, B, D2]) for n in range(2)])
        stats = Ring([sb(f"a2_stats{n}", [P, 5, 6]) for n in range(3)])
        mvs = Ring([sb(f"a2_mv{n}", [P, 5, 2]) for n in range(3)])
        rs = Ring([sb(f"a2_rs{n}", [P, 5]) for n in range(3)])
        probs = Ring([sb(f"a2_p{n}", [P, HPG * S + HPG * SC]) for n in range(3)])
        own = lambda p: p[:, 0:HPG * S].rearrange("p (h s) -> p h s", h=HPG)
        cross = lambda p: p[:, HPG * S:HPG * (S + SC)].rearrange("p (h s) -> p h s", h=HPG)
        top = Ring([sb(f"a2_top{n}", [P, 4]) for n in range(3)])
        tot = Ring([sb(f"a2_tot{n}", [P, 4]) for n in range(3)])
        pt = Ring([sb(f"a2_pt{n}", [P, HPG, TPB, S]) for n in range(2)])
        px = Ring([sb(f"a2_px{n}", [P, S]) for n in range(2)])
        cat = Ring([sb(f"a2_cat{n}", [P, 2 * HPG, S], BF16) for n in range(2)])
        catm = Ring([sb(f"a2_catm{n}", [P, 2 * HPG, S], BF16) for n in range(2)])
        catq = Ring([k.cols[:, n, :].rearrange("p (c t) -> p c t", t=S) for n in range(2)], used)
        acc_ready = [k.pool([ln_ready], lambda e, i=i: e.memset(acc[:, i, :], 0.0)) for i in range(NT)]
        units = [dict(g=g, b=b) for g in range(G2) for b in range(B)]
        groups = {}

        def ln_heads(srcs, dst, after, free):
            n = len(srcs)
            n1, st, f1 = stats.take()
            n2, mv, f2 = mvs.take()
            n3, r, f3 = rs.take()
            t = moments(k, srcs, n, st, mv, r, 1e-5, [after, f1, f2, f3])
            t = k.dve([t, free], *[lambda e, i=i: e.tensor_scalar(dst[i], srcs[i], mv[:, i, 0:1], r[:, i:i + 1],
                                                                ALU.subtract, ALU.mult) for i in range(n)])
            stats.give(n1, t)
            mvs.give(n2, t)
            rs.give(n3, t)
            return t

        def group_open(g):
            gr = groups[g] = dict()
            n, wt, came = k.groups_in.pop(g)
            gv = views(wt, L2G)
            gr.update(n=n, w=gv["w"].rearrange("p (j n) -> p j n", j=DC), came=came,
                      proj=gv["proj"].rearrange("p (c d) -> p c d", d=D))
            wg = gr["w"]
            nb, bank, freed = k.banks.take()
            for i in range(CTX // P):
                t = k.mm(bank[:, i * P:(i + 1) * P], [(ctx[:, j, i * P:(i + 1) * P], wg[:, j, 6 * P:7 * P])
                                                      for j in range(DC)], [freed, came])
            nn, kn, kf = kxn.take()
            u = ln_heads([bank[:, i * P:(i + 1) * P] for i in range(CTX // P)], [kn[:, i, :] for i in range(CTX // P)],
                         t, kf)
            k.banks.give(nb, u)
            nv, vb, vf = vx.take()
            nb, bank, freed = k.banks.take()
            for b in range(B):
                t = k.mm(bank[:, b * P:(b + 1) * P], [(twice[:, j, b, :], wg[:, j, 7 * P:8 * P])
                                                      for j in range(DC)], [freed, came])
            gr["vx_ready"] = k.copy(k.act, vb[:].rearrange("p b d -> p (b d)"), bank[:], [t, vf])
            k.banks.give(nb, gr["vx_ready"])
            nb, bank, freed = k.banks.take()
            t = k.turn([(bank[:, i * P:(i + 1) * P], kn[:, i, :]) for i in range(CTX // P)], [freed, u])
            kxn.give(nn, t)
            nk, kb, kf = kx.take()
            gr["kx_ready"] = k.act([t, kf], lambda e: e.activation(
                kb[:], bank[:, 0:CTX], ACT.Identity, bias=w["kxln_b"], scale=w["kxln_w"]))
            k.banks.give(nb, gr["kx_ready"])
            gr.update(nv=nv, vx=vb, nk=nk, kx=kb)

        def project(n):
            un = units[n]
            g, b = un["g"], un["b"]
            if b == 0:
                group_open(g)
            gr = groups[g]
            wg = gr["w"]
            nv, v, vf = vs.take()
            nq, qb, qf = qt.take()
            nk, kb, kf = kt.take()
            un.update(nv=nv, v=v, nq=nq, q=qb, nk=nk, kt=kb, v_ready=[], q_ready=[])
            for ti in range(TPB):
                i = b * TPB + ti
                tok = slice(i * P, (i + 1) * P)
                lhs = {nm: [scaled[nm][:, j, tok] for j in range(DC)] for nm in names}
                n1, b1, f1 = k.banks.take()
                for part, nm in enumerate(("q", "qx")):
                    t = k.mm(b1[:, part * 2 * P:(part + 1) * 2 * P],
                             [(lhs[nm][j], wg[:, j, part * 2 * P:(part + 1) * 2 * P]) for j in range(DC)],
                             [f1, in_ready[nm], gr["came"]])
                n2, b2, f2 = k.banks.take()
                for part, nm in enumerate(("k", "v")):
                    t2 = k.mm(b2[:, part * P:(part + 1) * P],
                              [(lhs[nm][j], wg[:, j, (4 + part) * P:(5 + part) * P]) for j in range(DC)],
                              [f2, in_ready[nm]])
                u = k.copy(k.act, v[:, ti, :], b2[:, P:2 * P], [t2, vf])
                un["v_ready"].append(u)
                nn, q_n, nf = qn.take()
                t = ln_heads([b1[:, c * P:(c + 1) * P] for c in range(4)] + [b2[:, 0:P]],
                             [q_n[:, c, :] for c in range(5)], [t, t2, u], nf)
                k.banks.give(n1, t)
                k.banks.give(n2, t)
                n1, b1, f1 = k.banks.take()
                n2, b2, f2 = k.banks.take()
                t1 = k.turn([(b1[:, c * P:(c + 1) * P], q_n[:, c, :]) for c in range(4)], [f1, t])
                t2 = k.turn([(b2[:, 0:P], q_n[:, 4, :])], [f2])
                qn.give(nn, t2)
                for part, nm in enumerate(("qln", "qxln")):
                    u = k.act([t1, qf], lambda e, part=part, nm=nm, b1=b1, ti=ti, qb=qb: e.activation(
                        qb[:, 2 * part:2 * part + 2, ti * P:(ti + 1) * P],
                        b1[:, part * 2 * P:(part + 1) * 2 * P].rearrange("p (c t) -> p c t", c=2), ACT.Identity,
                        bias=w[f"{nm}_b"], scale=w[f"{nm}_w"]))
                k.banks.give(n1, u)
                u2 = k.act([t2, kf], lambda e, b2=b2, ti=ti, kb=kb: e.activation(
                    kb[:, ti * P:(ti + 1) * P], b2[:, 0:P], ACT.Identity, bias=w["kln_b"], scale=w["kln_w"]))
                k.banks.give(n2, u2)
                un["q_ready"] += [u, u2]

        def attend(n):
            un = units[n]
            gr, b = groups[un["g"]], un["b"]
            qb, kb = un["q"], un["kt"]
            un["p"] = []
            for ti in range(TPB):
                tok = slice(ti * P, (ti + 1) * P)
                n1, b1, f1 = k.banks.take()
                n2, b2, f2 = k.banks.take()
                for h in range(HPG):
                    t = k.mm(b1[:, h * S:(h + 1) * S], [(qb[:, h, tok], kb[:])], [f1, un["q_ready"]])
                for h in range(HPG):
                    t2 = k.mm(b2[:, h * SC:(h + 1) * SC], [(qb[:, HPG + h, tok], gr["kx"][:, b * SC:(b + 1) * SC])],
                              [f2, gr["kx_ready"]])
                nt, tp, tf = top.take()
                u = k.dve([t, tf], lambda e, b1=b1, tp=tp: e.tensor_reduce(
                    tp[:, 0:2], b1[:].rearrange("p (h s) -> p h s", h=HPG), AX.X, ALU.max))
                u = k.dve([t2, tf], lambda e, b2=b2, tp=tp: e.tensor_reduce(
                    tp[:, 2:4], b2[:, 0:HPG * SC].rearrange("p (h s) -> p h s", h=HPG), AX.X, ALU.max))
                u = k.dve([u], lambda e, tp=tp: e.tensor_scalar(tp[:], tp[:], -softscale, None, ALU.mult))
                np_, p, pf = probs.take()
                ns, tt, sf = tot.take()
                for h in range(HPG):
                    a = k.act([u, pf, sf], lambda e, h=h, p=p, b1=b1, tp=tp, tt=tt: e.activation(
                        own(p)[:, h, :], b1[:, h * S:(h + 1) * S], ACT.Exp, bias=tp[:, h:h + 1], scale=softscale,
                        accum_out=tt[:, h:h + 1]))
                    a2 = k.act([], lambda e, h=h, p=p, b2=b2, tp=tp, tt=tt: e.activation(
                        cross(p)[:, h, :], b2[:, h * SC:(h + 1) * SC], ACT.Exp, bias=tp[:, 2 + h:3 + h],
                        scale=softscale, accum_out=tt[:, 2 + h:3 + h]))
                k.banks.give(n1, a2)
                k.banks.give(n2, a2)
                top.give(nt, a2)
                r = k.dve([a2], lambda e, tt=tt: e.reciprocal(tt[:], tt[:]))
                z = k.pool([r], lambda e, p=p, tt=tt: e.tensor_tensor(own(p), own(p), over(tt[:, 0:2], S),
                                                                      ALU.mult))
                z = k.pool([], lambda e, p=p, tt=tt: e.tensor_tensor(cross(p), cross(p),
                                                                     over(tt[:, 2:4], SC), ALU.mult))
                tot.give(ns, z)
                un["p"].append((np_, p, z))
            qt.give(un["nq"], t2)
            kt.give(un["nk"], t2)
            if b == B - 1:
                kx.give(gr["nk"], t2)

        def flip(n):
            un = units[n]
            nt, ptb, tf = pt.take()
            nx, pxb, xf = px.take()
            ready = []
            nc_, cbank, cfree = k.banks.take()
            for ti, (np_, p, z) in enumerate(un["p"]):
                tok = slice(ti * P, (ti + 1) * P)
                n1, b1, f1 = k.banks.take()
                t = k.turn([(b1[:, (h * TPB + kk) * P:(h * TPB + kk + 1) * P], own(p)[:, h, kk * P:(kk + 1) * P])
                            for h in range(HPG) for kk in range(TPB)], [f1, z])
                u = k.copy(k.act if ti else k.dve, ptb[:, :, :, tok],
                           b1[:].rearrange("p (h c t) -> p h c t", h=HPG, c=TPB), [t, tf])
                k.banks.give(n1, u)
                ready.append(u)
                t = k.turn([(cbank[:, tok], p[:, HPG * S:HPG * (S + SC)])], [cfree, z])
                probs.give(np_, t)
            u = k.copy(k.dve, pxb[:], cbank[:, 0:S], [t, xf])
            k.banks.give(nc_, u)
            ready.append(u)
            un.update(nt=nt, pt=ptb, nx=nx, px=pxb, p_ready=ready)

        def values(n):
            un = units[n]
            g, b = un["g"], un["b"]
            gr = groups[g]
            n1, b1, f1 = k.banks.take()
            n2, b2, f2 = k.banks.take()
            for h in range(HPG):
                t = k.mm(b1[:, h * S:(h + 1) * S], [(un["v"][:, kk, :], un["pt"][:, h, kk, :]) for kk in range(TPB)],
                         [f1, un["v_ready"], un["p_ready"]])
            n3, b3, f3 = k.banks.take()
            for h, (bank, freed) in enumerate(((b2, f2), (b3, f3))):
                part = slice(h * SC, (h + 1) * SC)
                t2 = k.mm(bank[:, 0:S], [(gr["vx"][part, b, :], un["px"][part, :])], [freed, gr["vx_ready"]])
            vs.give(un["nv"], t2)
            pt.give(un["nt"], t2)
            px.give(un["nx"], t2)
            if b == B - 1:
                vx.give(gr["nv"], t2)
            nc_, cb, cf = cat.take()
            for part, outs, tick in ((0, (b1[:, 0:S], b1[:, S:2 * S]), t), (1, (b2[:, 0:S], b3[:, 0:S]), t2)):
                for h in range(HPG):
                    ch = part * NH2 + g * HPG + h
                    u = k.act([tick, cf, sm], lambda e: e.activation(
                        cb[:, part * HPG + h, :], outs[h], ACT.Copy, scale=ismooth[:, ch:ch + 1]))
            k.banks.give(n1, u)
            k.banks.give(n2, u)
            k.banks.give(n3, u)
            flat = lambda a: a[:, :, :].rearrange("p c t -> p (c t)")
            t = k.dve([u], lambda e: e.tensor_scalar(flat(cb), flat(cb), FP8_MAX, -FP8_MAX, ALU.min, ALU.max))
            nm, mb, mf = catm.take()
            nq, qb, qf = catq.take()
            t = round_fp8(k, flat(cb), flat(mb), flat(qb), flat(qb), [t, mf, qf], k.pool)
            cat.give(nc_, t)
            catm.give(nm, t)
            un.update(ncq=nq, catq=qb, cat_ready=t)

        def output(n):
            un = units[n]
            gr, b = groups[un["g"]], un["b"]
            nb, bank, freed = k.banks.take()
            for ti in range(TPB):
                t = k.mm(bank[:, ti * D:(ti + 1) * D], [(un["catq"][:, c, ti * P:(ti + 1) * P], gr["proj"][:, c, :])
                                                        for c in range(2 * HPG)], [freed, un["cat_ready"]])
            catq.give(un["ncq"], t)
            i = b * TPB
            u = k.dve([t, acc_ready[i]], lambda e: e.tensor_tensor(
                acc[:, i:i + TPB, :], acc[:, i:i + TPB, :], bank[:].rearrange("p (t d) -> p t d", t=TPB), ALU.add))
            acc_ready[i] = acc_ready[i + 1] = u
            k.banks.give(nb, u)
            if b == B - 1:
                give_group(k, gr["n"], t)

        skew(len(units), project, attend, flip, values, output, oldest_first=True)
        out = [k.dve([acc_ready[i], ps], lambda e, i=i: e.scalar_tensor_tensor(
            k.x[:, i, :], acc[:, i, :], pscale[:, 0:1], k.x[:, i, :], ALU.mult, ALU.add)) for i in range(NT)]
    return out


def fetch_group(k):
    g = k.next_group
    n, buf, freed = k.group_ring.take()
    k.groups_in[g] = (n, buf, k.sp.dma(freed, k.group_arrival[n], lambda e: e.dma_start(buf, k.group_dram[g])))
    k.next_group += 1


def give_group(k, n, tick):
    k.group_ring.give(n, tick)
    if k.next_group < G2:
        fetch_group(k)


def layer2_ffn(k, x_ready):
    with ExitStack() as scope:
        sb = lambda name, shape, dt=F32: k.sb(name, shape, dt, scope)
        w, W = k.l2f, k.l2f_in
        quantised = {}
        absum = sb("f2_absum", [P, 3])
        gamma = sb("f2_gamma", [P, 3])
        n, bank, freed = k.banks.take()
        t = [k.dve([W, x_ready], lambda e, q=q, name=name: e.tensor_reduce(
            absum[:, q:q + 1], w[name], AX.X, ALU.add, apply_absolute_value=True))
            for q, name in enumerate(("w1", "w2", "w3"))]
        t = k.mm(bank[:, 0:3], [(k.c["ones"], absum[:])], [freed, t])
        t = k.dve([t], lambda e: e.tensor_scalar(gamma[:], bank[:, 0:3], 1.0 / (FFN2 * D), 1e-8, ALU.mult, ALU.add))
        k.banks.give(n, t)
        g = k.dve([t], lambda e: e.reciprocal(gamma[:], gamma[:]))
        for q, name in enumerate(("w1", "w2", "w3")):
            t = k.dve([g], lambda e, q=q, name=name: e.tensor_scalar(w[name], w[name], gamma[:, q:q + 1], ROUND,
                                                                   ALU.mult, ALU.add))
            t = k.dve([t], lambda e, name=name: e.tensor_scalar(w[name], w[name], ROUND, 1.0, ALU.subtract, ALU.min))
            quantised[name] = k.dve([t], lambda e, name=name: e.tensor_scalar(w[name], w[name], -1.0, None, ALU.max))
        norm_pass(k, x_ready)
        hidden = sb("f2_hidden", [P, FC2, TOK])
        gate = Ring([sb(f"f2_gate{n}", [P, BANK]) for n in range(3)])
        w1 = w["w1"].rearrange("p (j n) -> p j n", j=DC)
        w2 = w["w2"].rearrange("p (j n) -> p j n", j=DC)
        w3 = w["w3"].rearrange("p (c d) -> p c d", d=D)
        last = {}
        for half in range(TOK // BANK):
            sl = slice(half * BANK, (half + 1) * BANK)
            for c in range(FC2):
                rows = min(P, FFN2 - c * P)
                tb = []
                for wt, nm in ((w1, "w1"), (w2, "w2")):
                    n, bank, freed = k.banks.take()
                    t = k.mm(bank[0:rows, :], [(wt[:, j, c * P:c * P + rows], k.cols[:, j, sl]) for j in range(DC)],
                             [freed, quantised[nm], [r[half] for r in k.cols_ready]])
                    tb.append((n, bank, t))
                ng, gb, gf = gate.take()
                u = k.act([tb[0][2], gf], lambda e, rows=rows, gb=gb, bank=tb[0][1]: e.activation(
                    gb[0:rows, :], bank[0:rows, :], ACT.Sigmoid))
                k.banks.give(tb[0][0], u)
                v = k.dve([u, tb[1][2]], lambda e, rows=rows, gb=gb, bank=tb[1][1], c=c, sl=sl: e.tensor_tensor(
                    hidden[0:rows, c, sl], gb[0:rows, :], bank[0:rows, :], ALU.mult))
                k.banks.give(tb[1][0], v)
                gate.give(ng, v)
                last[half] = v
        out = []
        for i in range(NT):
            n, bank, freed = k.banks.take()
            pairs = [(hidden[0:min(P, FFN2 - c * P), c, i * P:(i + 1) * P], w3[0:min(P, FFN2 - c * P), c, :])
                     for c in range(FC2)]
            t = k.mm(bank[:, 0:D], pairs, [freed, last[i // HALF], quantised["w3"]])
            out.append(k.dve([t], lambda e, i=i, bank=bank: e.tensor_tensor(k.x[:, i, :], k.x[:, i, :], bank[:, 0:D],
                                                                          ALU.add)))
            k.banks.give(n, out[-1])
    return out


def layer3_attention(k, x_ready):
    norm_pass(k, x_ready)
    with ExitStack() as scope:
        sb = lambda name, shape, dt=F32: k.sb(name, shape, dt, scope)
        w, W, c = k.l3, k.l3_in, k.c
        mat = {n: w[n].rearrange("p (j n) -> p j n", j=DC) for n in ("qw", "kw", "vw", "ow")}
        ctx = k.ctxt["ctx"].rearrange("p (j t) -> p j t", j=DC)
        twice = k.ctxt["twice"].rearrange("p (j b t) -> p j b t", j=DC, b=B)
        junk = Ring([sb(f"a3_junk{n}", [P, D]) for n in range(2)])
        ms = sb("a3_ms", [P, 10])
        qrow = sb("a3_q", [P, 10, D])
        qcol = sb("a3_qt", [P, DC, TOK])
        kcol = sb("a3_kt", [P, DC, CTX])
        kblock = sb("a3_kb", [P, B, DC, 8, SC])
        vblock = sb("a3_vb", [P, B, D])
        ones = c["ones"]

        def linear(lhs, weight, bias, bank_half, after):
            return k.mm(bank_half, [(a, mat[weight][:, j, :]) for j, a in enumerate(lhs)]
                        + [(ones[0:1, :], w[bias][0:1, :])], after)

        kept, squares = [], []
        for i in range(NT + CTX // P):
            n, bank, freed = k.banks.take()
            if i < NT:
                t = linear(tile_cols(k, i), "qw", "qb", bank[:, 0:D], [freed, both(k.cols_ready, i), W])
            else:
                m = i - NT
                t = linear([ctx[:, j, m * P:(m + 1) * P] for j in range(DC)], "kw", "kb", bank[:, 0:D], [freed, W])
            nj, jb, jf = junk.take()
            squares.append(k.act([t, jf, x_ready], lambda e, i=i, jb=jb, bank=bank: e.activation(
                jb[:], bank[:, 0:D], ACT.Square, accum_out=ms[:, i:i + 1])))
            junk.give(nj, squares[-1])
            kept.append(k.copy(k.dve, qrow[:, i, :], bank[:, 0:D], [t, squares[-1]]))
            k.banks.give(n, kept[-1])
        t = k.dve([squares[-1]], lambda e: e.tensor_scalar(ms[:], ms[:], 1.0 / D, 1e-6, ALU.mult, ALU.add))
        t = k.pool([t], lambda e: e.tensor_tensor(ms[:], ms[:], c["minus_half"][:, 0:10], ALU.pow))
        scaled = [(k.dve if i % 2 else k.pool)([t, kept[i]], lambda e, i=i: e.tensor_scalar(
            qrow[:, i, :], qrow[:, i, :], ms[:, i:i + 1], 0.0, ALU.mult, ALU.add)) for i in range(10)]
        no_bias = sb("a3_zero", [P, DC])
        z = k.pool([x_ready], lambda e: e.memset(no_bias[:], 0.0))
        q_ready = transpose_rows(k, qrow, qcol, scaled, w["nq"], no_bias[:], free=[z])
        n, bank, freed = k.banks.take()
        t = k.turn([(bank[:, (j * 2 + m) * P:(j * 2 + m + 1) * P], qrow[:, NT + m, j * P:(j + 1) * P])
                    for j in range(DC) for m in range(CTX // P)], [freed, scaled[8:]])
        kk = [k.act([t], lambda e, j=j, bank=bank: e.activation(kcol[:, j, :], bank[:, j * CTX:(j + 1) * CTX], ACT.Copy,
                                                              scale=w["nk"][:, j:j + 1])) for j in range(DC)]
        k.banks.give(n, kk[-1])
        kb_ready = [k.dve([kk], *[lambda e, b=b, j=j: e.tensor_tensor(
            kblock[:, b, j, :, :], under(kcol[:, j, b * SC:(b + 1) * SC], 8), over(c["head16"], SC), ALU.mult)
            for j in range(DC)]) for b in range(B)]
        vb_ready = []
        for b in range(B):
            n, bank, freed = k.banks.take()
            t = linear([twice[:, j, b, :] for j in range(DC)], "vw", "vb", bank[:, 0:D], [freed, W])
            vb_ready.append(k.dve([t], lambda e, b=b, bank=bank: e.tensor_tensor(vblock[:, b, :], bank[:, 0:D],
                                                                              c["pair"], ALU.mult)))
            k.banks.give(n, vb_ready[-1])
        soft = Soft(k, scope)
        orow = Ring([sb(f"a3_o{n}", [P, D]) for n in range(2)])
        ocol = Ring([sb(f"a3_ot{n}", [P, DC, P]) for n in range(2)])
        jobs = [dict() for _ in range(NT)]

        def score(i):
            b, job = i // TPB, jobs[i]
            sbuf = soft.begin(job)
            for j in range(DC):
                n, bank, freed = k.banks.take()
                t = k.mm(bank[:], [(qcol[:, j, i * P:(i + 1) * P], kblock[:, b, j, :, :].rearrange("p h s -> p (h s)"))],
                         [freed, kb_ready[b], both(q_ready, i)])
                u = k.copy(k.act, sbuf[:, j * 8:(j + 1) * 8, :].rearrange("p h s -> p (h s)"), bank[:],
                           [t, job["free"]])
                k.banks.give(n, u)
            soft.shift(job, sbuf, [u])

        def mix(i):
            b, job = i // TPB, jobs[i]
            n, bank, freed = k.banks.take()
            for pr in range(H3 // 2):
                cs = slice(pr * 2 * HD3, (pr + 1) * 2 * HD3)
                t = k.mm(bank[:, cs], [(job["pt"][:, pr, :], vblock[:, b, cs])], [freed, vb_ready[b], job["pt_ready"]])
            soft.end(job, t)
            no, o, of = orow.take()
            u = k.copy(k.dve, o[:], bank[:, 0:D], [t, of])
            t = k.turn([(bank[:, D + j * P:D + (j + 1) * P], o[:, j * P:(j + 1) * P]) for j in range(DC)], [u])
            orow.give(no, t)
            nt, ot, tf = ocol.take()
            u = k.copy(k.act, ot[:].rearrange("p j t -> p (j t)"), bank[:, D:2 * D], [t, tf])
            k.banks.give(n, u)
            job.update(nt=nt, ot=ot, ot_ready=u)

        def out(i):
            job = jobs[i]
            n, bank, freed = k.banks.take()
            t = linear([job["ot"][:, j, :] for j in range(DC)], "ow", "ob", bank[:, 0:D], [freed, job["ot_ready"]])
            ocol.give(job["nt"], t)
            job["x"] = k.dve([t], lambda e: e.tensor_tensor(k.x[:, i, :], k.x[:, i, :], bank[:, 0:D], ALU.add))
            k.banks.give(n, job["x"])

        skew(NT, score, lambda i: soft.power(jobs[i], float(HD3) ** -0.5), lambda i: soft.flip(jobs[i]), mix, out)
    return [job["x"] for job in jobs]


LAYERS = [layer0_attention, layer0_ffn, layer1_attention, layer1_ffn, layer2_attention, layer2_ffn,
          layer3_attention, layer3_ffn]


def build(nc, a, upto=len(LAYERS), only=None):
    with ExitStack() as ctx:
        k = Core(nc, ctx)
        k.x = k.sb("x", [P, NT, D])
        k.rows = k.sb("rows", [P, NT, D])
        k.cols = k.sb("cols", [P, DC, TOK])
        k.stats = k.sb("stats", [P, NT, 6])
        k.mv = k.sb("mv", [P, NT, 2])
        k.rstd = k.sb("rstd", [P, NT])
        k.seg_i = k.sb("seg_i", [P, NT], I32)
        k.keys = k.sb("keys", [P, SC])
        const = k.sb("const", [P, width(CONST)])
        ctxt = k.sb("ctxt", [P, width(CTXP)])
        l0 = k.sb("l0_weights", [P, width(L0A)])
        l2 = k.sb("l2_vectors", [P, width(L2A)])
        after_l1 = L2F + L3A + L2G + L2G
        late = k.sb("late", [P, max(width(L1A), width(after_l1))])
        ring = [k.sb(f"expert{n}", [P, UNIT]) for n in range(6)]
        base = width(L2F) + width(L3A)
        groups = [late[:, base + n * width(L2G):base + (n + 1) * width(L2G)] for n in range(2)]
        k.c, k.ctxt, k.l0, k.l2 = views(const, CONST), views(ctxt, CTXP), views(l0, L0A), views(l2, L2A)
        k.l1_space = late[:, width(L1A) - (H1 * HD1 + H1 * D):width(L1A)]
        k.l1, k.l2f, k.l3 = views(late, L1A), views(late, L2F), views(late, L3A, width(L2F))

        x_in = k.load("x_in", k.x[:], a["x"])
        k.const_in = k.load("const_in", const[:], a["const"])
        k.l0_in = k.load("l0_in", l0[:], a["l0"])
        k.ctx_in = k.load("ctx_in", ctxt[:], a["ctx"])
        k.experts, k.expert_arrival = Ring(ring), [k.arrival(f"expert{n}_in") for n in range(len(ring))]
        k.expert_dram, k.n_experts, k.fetched, k.next_expert = a["experts"], a["experts"].shape[0], {}, 0
        while k.next_expert < len(ring):
            fetch_expert(k, k.next_expert)
            k.next_expert += 1
        k.seg_in = k.load("seg_in", k.seg_i[:], a["seg"])
        k.l1_in = k.load("l1_in", late[:, 0:width(L1A)], a["l1"])
        k.l2_in = k.load("l2_in", l2[:], a["l2"])
        k.group_dram, k.group_ring, k.next_group, k.groups_in = a["groups"], Ring(groups), 0, {}
        k.group_arrival = [k.arrival(f"group{n}_in") for n in range(len(groups))]
        k.pool.wait([k.const_in])
        keys_ready = k.pool([k.const_in], lambda e: e.iota(k.keys[:], [[1, SC]], base=0, channel_multiplier=0,
                                                           allow_small_or_imprecise_dtypes=True))
        k.dve.wait([keys_ready, k.const_in])
        k.act.wait([k.const_in])
        k.pe.wait([k.const_in])

        ready = [x_in] * NT
        for n, layer in enumerate(LAYERS[:upto]):
            if only is not None and n not in only:
                if n == 0:
                    drop_expert
                continue
            ready = layer(k, ready)
            if layer is layer1_attention:
                k.l2f_in = k.load("l2f_in", late[:, 0:width(L2F)], a["l2f"], [ready])
                k.l3_in = k.load("l3_in", late[:, width(L2F):base], a["l3"])
                while k.next_group < len(groups):
                    fetch_group(k)
        stored = k.sp.dma([ready], k.arrival("out_stored"), lambda e: e.dma_start(a["out"], k.x[:]))
        k.sp.wait([stored])


def pack(spec, parts):
    out = np.zeros((P, width(spec)), np.float32)
    at = 0
    for name, n in spec:
        v = np.asarray(parts[name])
        v = v.reshape(v.shape[0], -1)
        out[:v.shape[0], at:at + v.shape[1]] = v
        assert v.shape[1] == n, (name, v.shape, n)
        at += n
    return out


def chunks(w):
    w = np.asarray(w)
    return w.reshape(-1, P, w.shape[-1]).transpose(1, 0, 2).reshape(P, -1)


def column(v):
    return np.ascontiguousarray(np.asarray(v).reshape(-1, P).T)


def everywhere(v):
    v = np.asarray(v).reshape(1, -1)
    return np.broadcast_to(v, (P, v.shape[1]))


def expert(gate_t, up_t, down_t):
    gu = np.concatenate([gate_t.reshape(DC, P, I), up_t.reshape(DC, P, I)], axis=2)
    return np.concatenate([gu.transpose(1, 0, 2).reshape(P, -1), down_t], axis=1)


def constants():
    part = np.arange(P)
    half = R1 // 2
    inv_freq = np.float32(1.0) / np.float32(10000.0) ** (np.arange(half, dtype=np.float32) / np.float32(half))

    def tables(n):
        ang = (np.arange(n, dtype=np.float32)[:, None] * inv_freq).astype(np.float32)
        feature = part % R1
        cos, sin = np.cos(ang).T[feature % half], np.sin(ang).T[feature % half]
        return cos.astype(np.float32), (sin * np.where(feature < half, -1.0, 1.0)[:, None]).astype(np.float32)

    cos_q, sin_q = tables(S)
    cos_k, sin_k = tables(SC)
    head = np.arange(D) // HD3
    return pack(CONST, {
        "ident": np.eye(P), "ones": np.ones((P, P)), "before": (part[:, None] < part[None, :]),
        "iota_e": everywhere(np.arange(32)), "iota_c": everywhere(np.arange(CAP)),
        "cos_q": cos_q, "sin_q": sin_q, "cos_k": cos_k, "sin_k": sin_k,
        "head16": (part[:, None] // HD3 == np.arange(8)[None, :]),
        "pair": ((part[:, None] // SC) == (head[None, :] % 2)),
        "slot1": (TOK + 1 + part)[:, None], "tokpart": (part + 1)[:, None], "half": np.full((P, 8), 0.5),
        "minus_half": np.full((P, 16), -0.5)})


def swap_halves(w):
    w = np.asarray(w)
    return w.reshape(w.shape[0], -1, 2, R1 // 2)[:, :, ::-1, :].reshape(w.shape[0], -1)


def lay_out(v):
    v = {n: np.asarray(x) for n, x in v.items()}
    ctx_t = v["ctx_2048"].reshape(CTX, D).T
    by_batch = ctx_t.reshape(D, B, 1, SC)
    twice = np.broadcast_to(by_batch, (D, B, 2, SC)).reshape(D, B * 2 * SC)
    a = {"x": v["x"].reshape(NT, P, D).transpose(1, 0, 2), "const": constants(),
         "ctx": pack(CTXP, {"ctx": chunks(ctx_t), "twice": chunks(twice)}),
         "seg": v["itok_BxS_0_1023"].reshape(NT, P).T}
    g = lambda n: v["L0_xattn_" + n]
    a["l0"] = pack(L0A, {
        "w_in": chunks(g("W_in").T), "w_out": chunks(g("W_out").T), "b_in": column(g("b_in")),
        "b_out": everywhere(g("b_out")), "gamma": everywhere(g("gamma")), "beta": everywhere(g("beta")),
        "decay": everywhere(g("decay")), "gate0": chunks(v["L0_ffn_gate_w"].T), "bias0": everywhere(v["L0_ffn_bias"]),
        "gate1": chunks(v["L1_ffn_gate_w"].T), "gate3": chunks(v["L3_ffn_centroids"].T),
        "bias3": everywhere(v["L3_ffn_gate_bias"])})
    ex = [expert(v["L0_ffn_sg"].T, v["L0_ffn_su"].T, v["L0_ffn_sd"].T)]
    ex += [expert(v["L0_ffn_w_gate"][e].T, v["L0_ffn_w_up"][e].T, v["L0_ffn_w_down"][e].T) for e in range(E0)]
    ex += [expert(v["L1_ffn_sw1"].T, v["L1_ffn_sw3"].T, v["L1_ffn_sw2"].T)]
    ex += [expert(v["L1_ffn_w1"][e].T, v["L1_ffn_w3"][e].T, v["L1_ffn_w2"][e].T) for e in range(E1)]
    ex += [expert(v["L3_ffn_wg_s"][:, s], v["L3_ffn_wu_s"][:, s], v["L3_ffn_wd_s"][s, :])
           for s in (slice(0, I), slice(I, 2 * I))]
    ex += [expert(v["L3_ffn_wg"][e], v["L3_ffn_wu"][e], v["L3_ffn_wd"][e]) for e in range(E3)]
    a["experts"] = np.stack(ex)
    g = lambda n: v["L1_xattn_" + n]
    by_head = lambda w: w.reshape(-1, H1, HD1)
    a["l1"] = pack(L1A, {
        "kvc": chunks(g("W_kvc")), "dq": chunks(g("W_dq")),
        "uq": by_head(g("W_uq")).transpose(2, 1, 0).reshape(P, -1), "qr": g("W_qr"), "qr_swap": swap_halves(g("W_qr")),
        "uk": g("W_uk"), "kr": np.concatenate([g("W_kr")] * 2, axis=1),
        "kr_swap": np.concatenate([swap_halves(g("W_kr"))] * 2, axis=1), "uv": g("W_uv"), "wo": chunks(g("W_o"))})
    g = lambda n: v["L2_xattn_" + n]
    vec = {n: column(g(n)) for n in ("ln_w", "ln_b", "qln_w", "qln_b", "kln_w", "kln_b", "qxln_w", "qxln_b",
                                     "kxln_w", "kxln_b")}
    a["l2"] = pack(L2A, {
        **vec, "q_in": column(g("q_in_scale")), "qx_in": column(g("qx_in_scale")), "k_in": column(g("k_in_scale")),
        "v_in": column(g("v_in_scale")), "wq_s": everywhere(g("wq_scale")), "wqx_s": everywhere(g("wqx_scale")),
        "wk_s": everywhere(g("wk_scale")), "wv_s": everywhere(g("wv_scale")), "p_w": everywhere(g("proj_w_scale")),
        "p_in": everywhere(g("proj_in_scale")), "smooth": column(g("proj_smooth"))})
    kvx = g("w_kv_x")
    proj = g("wproj").T.reshape(2, G2, HPG, P, D)
    a["groups"] = np.stack([pack(L2G, {
        "w": chunks(np.concatenate([
            g("wq")[q * HPG * P:(q + 1) * HPG * P], g("wqx")[q * HPG * P:(q + 1) * HPG * P],
            g("wk")[q * P:(q + 1) * P], g("wv")[q * P:(q + 1) * P], kvx[q * P:(q + 1) * P],
            kvx[(G2 + q) * P:(G2 + q + 1) * P]]).T),
        "proj": proj[:, q].reshape(2 * HPG, P, D).transpose(1, 0, 2)}) for q in range(G2)])
    pad = lambda w: np.concatenate([w, np.zeros((FC2 * P - FFN2, D), np.float32)])
    a["l2f"] = pack(L2F, {"w1": chunks(v["L2_ffn_w1"].T), "w2": chunks(v["L2_ffn_w2"].T),
                          "w3": chunks(pad(v["L2_ffn_w3"].T))})
    g = lambda n: v["L3_xattn_" + n]
    a["l3"] = pack(L3A, {
        "qw": chunks(g("q_w").T), "kw": chunks(g("k_img_w").T), "vw": chunks(g("v_img_w").T), "ow": chunks(g("o_w").T),
        "qb": everywhere(g("q_b")), "kb": everywhere(g("k_img_b")), "vb": everywhere(g("v_img_b")),
        "ob": everywhere(g("o_b")), "nq": column(g("norm_q_w")), "nk": column(g("norm_k_img_w"))})
    return {n: np.ascontiguousarray(x) for n, x in a.items()}


def program(nc, arrays, **options):
    a = {n: nc.dram_tensor(f"in_{n}", x.shape, mybir.dt.from_np(x.dtype), kind="ExternalInput").ap()
         for n, x in arrays.items()}
    a["out"] = nc.dram_tensor("out", [P, NT, D], F32, kind="ExternalOutput").ap()
    build(nc, a, **options)


def kernel(**inputs):
    import concourse.bacc as bacc
    from concourse.bass_utils import run_bass_kernel_spmd

    nc = bacc.Bacc("TRN2", target_bir_lowering=False, num_devices=1)
    arrays = lay_out(inputs)
    program(nc, arrays)
    got = run_bass_kernel_spmd(nc, [{f"in_{n}": x for n, x in arrays.items()}], core_ids=[0])
    return got.results[0]["out"].transpose(1, 0, 2).reshape(B, S, D)
```

```python
from contextlib import ExitStack

import numpy as np

import concourse.bass as bass
from concourse import mybir

F32 = mybir.dt.float32
F32R = mybir.dt.float32r
BF16 = mybir.dt.bfloat16
U32 = mybir.dt.uint32
U16 = mybir.dt.uint16
I32 = mybir.dt.int32
ALU = mybir.AluOpType
ACT = mybir.ActivationFunctionType
AX = mybir.AxisListType

P = 128
B, S, D = 4, 256, 256
TOK = B * S
NT = TOK // P
DC = D // P
SC = 64
CTX = B * SC
TPB = S // P
BANK = 512
HALF = 4

E0, K0, CAP = 32, 6, 96
E1, K1 = 8, 2
E3, K3 = 16, 2
I = 128
UNIT = DC * 2 * I + D
SINK = CAP

H1, HD1, R1, KVC, QC, LOOK = 16, 128, 64, 64, 96, 8
NH2, G2, D2 = 16, 8, 128
HPG = NH2 // G2
GW = 8 * P
FFN2 = 704
FC2 = -(-FFN2 // P)
H3, HD3 = 16, 16
NEG = -1e30
ROUND = 1.5 * 2.0 ** 23
FP8_MAX = 448.0


CONST = [("ident", P), ("ones", P), ("before", P), ("iota_e", 32), ("iota_c", CAP), ("cos_q", S), ("sin_q", S),
         ("cos_k", SC), ("sin_k", SC), ("head16", 8), ("pair", D), ("slot1", 1), ("tokpart", 1)]
CTXP = [("ctx", DC * CTX), ("twice", DC * B * 2 * SC)]
L0A = [("w_in", DC * D), ("w_out", DC * D), ("b_in", DC), ("b_out", D), ("gamma", D), ("beta", D), ("decay", 1),
       ("gate0", DC * E0), ("bias0", E0), ("gate1", DC * E1), ("gate3", DC * E3), ("bias3", E3)]
L1A = [("kvc", DC * KVC), ("dq", DC * QC), ("uq", H1 * QC), ("qr", H1 * R1), ("qr_swap", H1 * R1),
       ("uk", H1 * HD1), ("kr", P), ("kr_swap", P), ("uv", H1 * HD1), ("wo", H1 * D)]
L2A = [("ln_w", DC), ("ln_b", DC), ("q_in", DC), ("qx_in", DC), ("k_in", DC), ("v_in", DC),
       ("wq_s", 1), ("wqx_s", 1), ("wk_s", 1), ("wv_s", 1), ("p_w", 1), ("p_in", 1),
       ("qln_w", 1), ("qln_b", 1), ("kln_w", 1), ("kln_b", 1), ("qxln_w", 1), ("qxln_b", 1), ("kxln_w", 1),
       ("kxln_b", 1), ("smooth", 2 * NH2)]
L2G = [("w", DC * GW), ("proj", 2 * HPG * D)]
L2F = [("w1", DC * FFN2), ("w2", DC * FFN2), ("w3", FC2 * D)]
L3A = [("qw", DC * D), ("kw", DC * D), ("vw", DC * D), ("ow", DC * D), ("qb", D), ("kb", D), ("vb", D), ("ob", D),
       ("nq", DC), ("nk", DC)]


def width(spec):
    return sum(n for _, n in spec)


def views(tile, spec, at=0):
    out = {}
    for name, n in spec:
        out[name] = tile[:, at:at + n]
        at += n
    return out


class Line:

    def __init__(self, engine, sem):
        self.engine, self.sem, self.count, self.met = engine, sem, 0, {}

    def wait(self, ticks):
        for t in ticks:
            if t is None:
                continue
            if isinstance(t, list):
                self.wait(t)
                continue
            sem, value = t
            if self.met.get(id(sem), 0) < value:
                self.met[id(sem)] = value
                self.engine.wait_ge(sem, value)

    def __call__(self, after, *steps):
        self.wait(after)
        for step in steps:
            last = step(self.engine)
        last.then_inc(self.sem, 1)
        self.count += 1
        return (self.sem, self.count)

    def dma(self, after, arrival, step):
        self.wait(after)
        step(self.engine).then_inc(arrival.sem, 16)
        arrival.count += 16
        return (arrival.sem, arrival.count)


class Arrival:

    def __init__(self, sem):
        self.sem, self.count = sem, 0


class Ring:

    def __init__(self, buffers, after=()):
        self.buffers, self.free, self.idle = buffers, [list(after) for _ in buffers], list(range(len(buffers)))

    def take(self):
        n = self.idle.pop(0)
        return n, self.buffers[n], self.free[n]

    def give(self, n, *ticks):
        self.free[n] = list(ticks)
        self.idle.append(n)


def skew(n, *stages, oldest_first=False):
    for r in range(n + len(stages) - 1):
        for k, stage in sorted(enumerate(stages), reverse=oldest_first, key=lambda pair: pair[0]):
            if 0 <= r - k < n:
                stage(r - k)


def over(ap, n):
    return ap.unsqueeze(2).broadcast_to([ap.shape[0], ap.shape[1], n])


def under(ap, n):
    return ap.unsqueeze(1).broadcast_to([ap.shape[0], n, ap.shape[1]])


class Core:

    def __init__(self, nc, ctx):
        self.nc, self.ctx = nc, ctx
        self.pe, self.dve, self.act, self.pool, self.sp = (
            Line(engine, ctx.enter_context(nc.semaphore(name))) for engine, name in (
                (nc.tensor, "matmul_done"), (nc.vector, "vector_done"), (nc.scalar, "scalar_done"),
                (nc.gpsimd, "pool_done"), (nc.sync, "sync_done")))
        self.banks = Ring([ctx.enter_context(nc.psum_tensor(f"bank{n}", [P, BANK], F32)) for n in range(8)])
        self.named = {}

    def sb(self, name, shape, dt=F32, scope=None):
        self.named[name] = self.named.get(name, 0) + 1
        if self.named[name] > 1:
            name += f"_{self.named[name]}"
        return (scope or self.ctx).enter_context(self.nc.sbuf_tensor(name, shape, dt))

    def arrival(self, name):
        return Arrival(self.ctx.enter_context(self.nc.semaphore(name)))

    def load(self, name, dst, src, after=()):
        return self.sp.dma(after, self.arrival(name), lambda e: e.dma_start(dst, src))

    def mm(self, out, pairs, after, start=True, stop=True, shared=False):
        builds = []
        for n, (lhs, rhs) in enumerate(pairs):
            builds.append(lambda e, a=lhs, b=rhs, s=start and n == 0, t=stop and n == len(pairs) - 1:
                          e.matmul(out, a, b, start=s, stop=t, skip_group_check=shared))
        return self.pe(after, *builds)

    def turn(self, jobs, after):
        ident = self.c["ident"]
        return self.pe(after, *[lambda e, o=o, i=i: e.transpose(o, i, ident[0:i.shape[0], 0:i.shape[0]])
                                for o, i in jobs])

    def copy(self, line, out, src, after):
        if line is self.act:
            return line(after, lambda e: e.activation(out, src, ACT.Copy))
        return line(after, lambda e: e.tensor_copy(out, src))


def rsqrt(k, out, v, spare, after):
    bits = out.bitcast(I32)
    t = k.dve(after, lambda e: e.tensor_scalar(bits, v.bitcast(I32), 1, None, ALU.logical_shift_right))
    t = k.dve([t], lambda e: e.tensor_scalar(bits, bits, -1, 0x5F3759DF, ALU.mult, ALU.add))
    for _ in range(3):
        t = k.dve([t], lambda e: e.scalar_tensor_tensor(spare, out, -0.5, v, ALU.mult, ALU.mult))
        t = k.dve([t], lambda e: e.tensor_tensor(spare, spare, out, ALU.mult))
        t = k.dve([t], lambda e: e.scalar_tensor_tensor(out, spare, 1.5, out, ALU.add, ALU.mult))
    return t


class Moments:

    def __init__(self, k, n, scope=None):
        self.stats = k.sb("stats", [P, n, 6], scope=scope)
        self.mv = k.sb("mean_var", [P, n, 2], scope=scope)
        self.minus, self.var, self.spare, self.rstd, self.shift = (
            k.sb(name, [P, n], scope=scope) for name in ("minus_mean", "var", "spare", "rstd", "shift"))


def moments(k, src, m, eps, after):
    n = len(src)
    for i in range(n):
        t = k.dve([after[i]], lambda e, i=i: e.bn_stats(m.stats[:, i, :], src[i]))
    t = k.dve([t], *[lambda e, i=i: e.bn_aggr(m.mv[:, i, :], m.stats[:, i, :]) for i in range(n)])
    var, rstd, minus = m.var[:, 0:n], m.rstd[:, 0:n], m.minus[:, 0:n]
    k.dve([t], lambda e: e.tensor_scalar(minus, m.mv[:, 0:n, 0], -1.0, None, ALU.mult))
    t = k.dve([], lambda e: e.tensor_scalar(var, m.mv[:, 0:n, 1], eps, None, ALU.add))
    t = rsqrt(k, rstd, var, m.spare[:, 0:n], [t])
    return k.dve([t], lambda e: e.tensor_tensor(m.shift[:, 0:n], minus, rstd, ALU.mult))


def normalise(k, src, out, after, eps=1e-5):
    m = k.moments
    t = moments(k, [src[:, i, :] for i in range(NT)], m, eps, after)
    by = lambda line, i: line([t], lambda e: e.tensor_scalar(
        out[:, i, :], src[:, i, :], m.minus[:, i:i + 1], m.rstd[:, i:i + 1], ALU.add, ALU.mult))
    return [k.act([t], lambda e, i=i: e.activation(
        out[:, i, :], src[:, i, :], ACT.Identity, bias=m.shift[:, i:i + 1], scale=m.rstd[:, i:i + 1]))
            if i % 3 == 1 else by(k.pool if i % 3 == 2 else k.dve, i) for i in range(NT)]


def transpose_rows(k, rows, cols, ready, scale=None, bias=None, free=()):
    ticks = [[None, None] for _ in range(DC)]
    for half in range(NT // HALF):
        for j in range(DC):
            n, bank, freed = k.banks.take()
            t = k.turn([(bank[:, i * P:(i + 1) * P], rows[:, half * HALF + i, j * P:(j + 1) * P])
                        for i in range(HALF)], [freed, ready[half * HALF:(half + 1) * HALF]])
            dst = cols[:, j, half * BANK:(half + 1) * BANK]
            if scale is None:
                u = k.copy(k.act if j else k.dve, dst, bank[:], [t, *free])
            else:
                u = k.act([t, *free], lambda e, j=j, dst=dst, bank=bank: e.activation(
                    dst, bank[:], ACT.Identity, bias=bias[:, j:j + 1], scale=scale[:, j:j + 1]))
            k.banks.give(n, u)
            ticks[j][half] = u
    return ticks


def both(ticks, tile):
    return [t[tile // HALF] for t in ticks]


def norm_pass(k, x_ready):
    k.rows_ready = normalise(k, k.x, k.rows, x_ready)
    k.cols_ready = transpose_rows(k, k.rows, k.cols, k.rows_ready)


def tile_cols(k, t, cols=None):
    cols = cols if cols is not None else k.cols
    return [cols[:, j, t * P:(t + 1) * P] for j in range(DC)]


def layer0_attention(k, x_ready):
    with ExitStack() as scope:
        w = k.l0
        seq = k.sb("l0_seq", [P, DC, CTX], scope=scope)
        states = k.sb("l0_states", [P, DC, CTX], scope=scope)
        keep = k.sb("l0_keep", [P, 1], scope=scope)
        keeps = k.sb("l0_keeps", [P, SC], scope=scope)
        mean_state = k.sb("l0_mean_state", [P, DC, B], scope=scope)
        mean_wide = k.sb("l0_mean_wide", [P, DC * B, P], scope=scope)
        y = k.sb("l0_y", [P, NT, D], scope=scope)
        k.rows_ready = normalise(k, k.x, k.rows, x_ready)
        t = k.act([k.l0_in], lambda e: e.activation(keep[:], w["decay"], ACT.Sigmoid))
        kept = k.dve([t, k.const_in], lambda e: e.tensor_scalar(keeps[:], k.c["ones"][:, 0:SC], keep[:, 0:1], None,
                                                                ALU.mult))
        n, bank, freed = k.banks.take()
        w_in = w["w_in"].rearrange("p (j e) -> p j e", j=DC)
        ctx = k.ctxt["ctx"].rearrange("p (j t) -> p j t", j=DC)
        for i in range(DC):
            t = k.mm(bank[:, i * CTX:(i + 1) * CTX], [(w_in[:, j, i * P:(i + 1) * P], ctx[:, j, :])
                                                      for j in range(DC)], [freed, k.l0_in, k.ctx_in])
        ticks = []
        for i in range(DC):
            ticks.append(k.act([t], lambda e, i=i: e.activation(seq[:, i, :], bank[:, i * CTX:(i + 1) * CTX],
                                                                ACT.Identity, bias=w["b_in"][:, i:i + 1])))
        k.banks.give(n, *ticks)
        for i in range(DC):
            for b in range(B):
                t = k.dve([ticks[i], kept], lambda e, i=i, b=b: e.tensor_tensor_scan(
                    states[:, i, b * SC:(b + 1) * SC], keeps[:], seq[:, i, b * SC:(b + 1) * SC], 0.0, ALU.mult,
                    ALU.add))
        t = k.dve([t], lambda e: e.tensor_reduce(
            mean_state[:].rearrange("p j b -> p (j b)"), states[:].rearrange("p j (b t) -> p (j b) t", b=B), AX.X,
            ALU.add))
        t = k.dve([t], lambda e: e.tensor_scalar(
            mean_wide[:], over(mean_state[:].rearrange("p j b -> p (j b)"), P), 1.0 / SC, None, ALU.mult))
        w_out = w["w_out"].rearrange("p (j e) -> p j e", j=DC)
        wide = t
        added = []
        for b in range(B):
            n, bank, freed = k.banks.take()
            t = k.mm(bank[:, 0:D], [(mean_wide[:, j * B + b, :], w_out[:, j, :]) for j in range(DC)]
                     + [(k.c["ones"][0:1, :], w["b_out"][0:1, :])], [freed, wide, k.l0_in])
            for i in range(b * TPB, (b + 1) * TPB):
                t2 = k.dve([t, k.rows_ready[i]], lambda e, i=i, bank=bank: e.tensor_tensor(
                    y[:, i, :], k.rows[:, i, :], bank[:, 0:D], ALU.add))
                added.append(t2)
            k.banks.give(n, t2)
        done = normalise(k, y, y, added)
        out = []
        for i in range(NT):
            t = k.pool([done[i]], lambda e, i=i: e.tensor_tensor(y[:, i, :], y[:, i, :], w["gamma"], ALU.mult))
            t = k.pool([t], lambda e, i=i: e.tensor_tensor(y[:, i, :], y[:, i, :], w["beta"], ALU.add))
            out.append(k.dve([t], lambda e, i=i: e.tensor_tensor(k.x[:, i, :], k.x[:, i, :], y[:, i, :], ALU.add)))
    return out


def expert_weights(k, slot):
    return slot[:, 0:DC * 2 * I].rearrange("p (j n) -> p j n", j=DC), slot[:, DC * 2 * I:UNIT]


def open_experts(k, scope, name, first, end, after):
    ring = [k.sb(f"{name}{n}", [P, UNIT], scope=scope) for n in range(6)]
    k.experts, k.expert_arrival = Ring(ring, after), [k.arrival(f"{name}{n}_in") for n in range(len(ring))]
    k.fetched, k.next_expert, k.last_expert = {}, first, end
    for _ in ring:
        fetch_expert(k)


def fetch_expert(k):
    if k.next_expert < k.last_expert:
        n, slot, freed = k.experts.take()
        src = k.expert_dram[k.next_expert]
        k.fetched[k.next_expert] = (n, slot, k.sp.dma(freed, k.expert_arrival[n], lambda q: q.dma_start(slot[:], src)))
        k.next_expert += 1


def use_expert(k, e):
    return k.fetched.pop(e)


def drop_expert(k, n, *ticks):
    k.experts.give(n, *ticks)
    fetch_expert(k)


def routing(k, scope, n_exp, top, logits_ticks, scores, biased, biased_ready):
    best = k.sb("route_best", [P, NT, 8], scope=scope)
    where = k.sb("route_where", [P, NT, 8], U32, scope=scope)
    where_f = k.sb("route_where_f", [P, NT, 8], scope=scope)
    hits = k.sb("route_hits", [P, NT, top, n_exp], scope=scope)
    mask = k.sb("route_mask", [P, NT, n_exp], scope=scope)
    t = k.dve([biased_ready], *[lambda e, i=i: e.max(best[:, i, :], biased[:, i, :]) for i in range(NT)])
    t = k.dve([t], *[lambda e, i=i: e.max_index(where[:, i, :], best[:, i, :], biased[:, i, :]) for i in range(NT)])
    t = k.dve([t], lambda e: e.tensor_copy(where_f[:], where[:]))
    t = k.dve([t], *[lambda e, i=i: e.tensor_tensor(
        hits[:, i, :, :], over(where_f[:, i, 0:top], n_exp), under(k.c["iota_e"][:, 0:n_exp], top), ALU.is_equal)
        for i in range(NT)])
    t = k.dve([t], lambda e: e.tensor_reduce(mask[:], hits[:].rearrange("p t k e -> p t e k"), AX.X, ALU.add))
    return mask, t


def gate_logits(k, gate, n_exp, logits, ready):
    n, bank, freed = k.banks.take()
    gate = gate.rearrange("p (j e) -> p j e", j=DC)
    for i in range(NT):
        t = k.mm(bank[:, i * n_exp:(i + 1) * n_exp], [(c, gate[:, j, :]) for j, c in enumerate(tile_cols(k, i))],
                 [freed, both(ready, i), k.l0_in])
    u = k.copy(k.dve, logits[:].rearrange("p t e -> p (t e)"), bank[:, 0:NT * n_exp], [t])
    k.banks.give(n, u)
    return u


class Swiglu:

    def __init__(self, k, scope, depth=3):
        self.k = k
        self.gated = Ring([k.sb(f"swi_gated{n}", [P, I], scope=scope) for n in range(depth)])
        self.inner = Ring([k.sb(f"swi_inner{n}", [P, I], scope=scope) for n in range(depth)])
        self.turned = Ring([k.sb(f"swi_turned{n}", [P, I], scope=scope) for n in range(depth)])

    def open(self, job):
        k, m = self.k, job["m"]
        gu, _ = expert_weights(k, job["slot"])
        nb, bank, freed = k.banks.take()
        t = k.mm(bank[0:m, 0:2 * I], [(c, gu[:, j, :]) for j, c in enumerate(job["cols"])], [freed, job["after"]])
        ng, gated, gfree = self.gated.take()
        t1 = k.act([t, gfree, job.get("s_ready")], lambda e, s=job["s"]: e.activation(
            gated[0:m, :], bank[0:m, 0:I], ACT.Silu, scale=s))
        ni, inner, ifree = self.inner.take()
        t2 = k.dve([t1, ifree, job.get("s_ready")], lambda e, w=job["w"]: e.scalar_tensor_tensor(
            inner[0:m, :], bank[0:m, I:2 * I], w, gated[0:m, :], ALU.mult, ALU.mult))
        self.gated.give(ng, t2)
        if job.get("clip"):
            t2 = k.dve([t2], lambda e, c=job["clip"]: e.tensor_scalar(inner[0:m, :], inner[0:m, :], c, -c, ALU.min,
                                                                      ALU.max))
        job.update(nb=nb, bank=bank, ni=ni, inner=inner, inner_ready=t2, gu_done=t)

    def flip(self, job):
        k, m, bank = self.k, job["m"], job["bank"]
        t = k.turn([(bank[:, 2 * I:2 * I + m], job["inner"][0:m, :])], [job["inner_ready"]])
        self.inner.give(job["ni"], t)
        nt, turned, tfree = self.turned.take()
        u = k.copy(k.act if job.get("evac") == "act" else k.dve, turned[:, 0:m], bank[:, 2 * I:2 * I + m], [t, tfree])
        k.banks.give(job["nb"], u)
        job.update(nt=nt, turned=turned, turned_ready=u)

    def close(self, job, out, after, start, stop, shared=False):
        k, m = self.k, job["m"]
        _, down = expert_weights(k, job["slot"])
        t = k.mm(out, [(job["turned"][:, 0:m], down)], [job["turned_ready"], after], start, stop, shared)
        self.turned.give(job["nt"], t)
        return t


def layer0_ffn(k, x_ready):
    norm_pass(k, x_ready)
    nc = k.nc
    with ExitStack() as scope:
        sb = lambda name, shape, dt=F32: k.sb(name, shape, dt, scope)
        n_rows = TOK + SINK
        h_rows = nc.dram_tensor("h_rows", [n_rows, D], F32, kind="Internal").ap()
        sums = [nc.dram_tensor(f"sum{n}", [n_rows, D], F32, kind="Internal").ap() for n in range(2)]
        tiled = lambda dram: dram[0:TOK, :].rearrange("(t p) d -> p t d", p=P)
        zeros = sb("f0_zeros", [SINK, D])
        shared = sb("f0_shared", [P, NT, D])
        second = sb("f0_second", [P, NT, D])
        t = k.pool([], lambda e: e.memset(zeros[:], 0.0))
        rows_out = k.arrival("h_rows_out")
        k.sp.dma([k.rows_ready], rows_out, lambda e: e.dma_start(tiled(h_rows), k.rows[:]))
        k.sp.dma([t], rows_out, lambda e: e.dma_start(h_rows[TOK:n_rows, :], zeros[:]))
        rows_stored = (rows_out.sem, rows_out.count)
        sum_out = [k.arrival(f"sum{n}_out") for n in range(2)]
        k.sp.dma([x_ready], sum_out[0], lambda e: e.dma_start(tiled(sums[0]), k.x[:]))
        k.sp.dma([t], sum_out[0], lambda e: e.dma_start(sums[0][TOK:n_rows, :], zeros[:]))
        k.sp.dma([t], sum_out[1], lambda e: e.dma_start(sums[1][TOK:n_rows, :], zeros[:]))

        logits = sb("f0_logits", [P, NT, E0])
        size = sb("f0_size", [P, NT, E0])
        small = sb("f0_small", [P, NT, E0])
        one_plus = sb("f0_one_plus", [P, NT, E0])
        log1p = sb("f0_log1p", [P, NT, E0])
        flat = sb("f0_flat", [P, NT, E0])
        scores = sb("f0_scores", [P, NT, E0])
        biased = sb("f0_biased", [P, NT, E0])
        lg = gate_logits(k, k.l0["gate0"], E0, logits, k.cols_ready)
        t = k.act([lg], lambda e: e.activation(size[:], logits[:], ACT.Abs))
        z = k.act([t], lambda e: e.activation(small[:], size[:], ACT.Exp, scale=-1.0))
        t = k.dve([z], lambda e: e.tensor_scalar(one_plus[:], small[:], 1.0, None, ALU.add))
        ln = k.act([t], lambda e: e.activation(log1p[:], one_plus[:], ACT.Ln))
        t = k.dve([t, ln], lambda e: e.tensor_scalar(one_plus[:], one_plus[:], 1.0, None, ALU.subtract))
        t = k.dve([t], lambda e: e.tensor_scalar(flat[:], one_plus[:], 0.0, None, ALU.is_equal))
        t = k.dve([t], lambda e: e.tensor_tensor(one_plus[:], one_plus[:], flat[:], ALU.add))
        t = k.dve([t], lambda e: e.reciprocal(one_plus[:], one_plus[:]))
        t = k.dve([t], lambda e: e.tensor_tensor(log1p[:], log1p[:], one_plus[:], ALU.mult))
        t = k.dve([t], lambda e: e.tensor_tensor(log1p[:], log1p[:], flat[:], ALU.add))
        t = k.dve([t], lambda e: e.tensor_tensor(log1p[:], log1p[:], small[:], ALU.mult))
        t = k.dve([t], lambda e: e.scalar_tensor_tensor(log1p[:], logits[:], 0.0, log1p[:], ALU.max, ALU.add))
        flat_t = lambda a: a[:].rearrange("p t e -> p (t e)")
        t = k.dve([t], lambda e: e.tensor_scalar(small[:], log1p[:], 2.0 ** -126, None, ALU.max))
        t = rsqrt(k, flat_t(scores), flat_t(small), flat_t(flat), [t])
        t = k.dve([t], lambda e: e.tensor_tensor(scores[:], scores[:], log1p[:], ALU.mult))
        t = k.dve([t], lambda e: e.tensor_tensor(biased[:], scores[:], under(k.l0["bias0"], NT), ALU.add))
        mask, t = routing(k, scope, E0, K0, lg, scores, biased, t)

        weight = sb("f0_weight", [P, NT, E0])
        total = sb("f0_total", [P, NT])
        w = k.dve([t], lambda e: e.tensor_tensor(weight[:], mask[:], scores[:], ALU.mult))
        w = k.dve([w], lambda e: e.tensor_reduce(total[:], weight[:], AX.X, ALU.add))
        w = k.dve([w], lambda e: e.reciprocal(total[:], total[:]))
        w = k.dve([w], lambda e: e.tensor_scalar(total[:], total[:], 1.5, None, ALU.mult))
        w = k.dve([w], lambda e: e.tensor_tensor(weight[:], weight[:], over(total[:], E0), ALU.mult))

        before = sb("f0_before", [P, NT, E0])
        b = k.pool([], lambda e: e.memset(before[:, 0, :], 0.0))
        for i in range(1, NT):
            b = k.dve([t, b], lambda e, i=i: e.tensor_tensor(before[:, i, :], before[:, i - 1, :], mask[:, i - 1, :],
                                                             ALU.add))
        n, bank, freed = k.banks.take()
        for i in range(NT):
            q = k.mm(bank[:, i * E0:(i + 1) * E0], [(k.c["before"], mask[:, i, :]), (k.c["ones"], before[:, i, :])],
                     [freed, b, t])
        place = sb("f0_place", [P, NT, E0])
        u = k.dve([t], lambda e: e.tensor_scalar(place[:], mask[:], -999.0, 999.0, ALU.mult, ALU.add))
        u = k.dve([u, q], lambda e: e.tensor_tensor(place[:].rearrange("p t e -> p (t e)"),
                                                    place[:].rearrange("p t e -> p (t e)"), bank[:, 0:NT * E0],
                                                    ALU.add))
        k.banks.give(n, u)

        facts = sb("f0_facts", [P, NT, E0, 5], BF16)
        rest = sb("f0_rest", [P, NT, E0])
        f = k.pool([k.const_in], *[lambda e, i=i: e.memset(facts[:, i, :, 1], float(i * P)) for i in range(NT)])
        f = k.dve([w, f], lambda e: e.tensor_scalar(
            facts[:, :, :, 0].rearrange("p t e -> p (t e)"), weight[:].rearrange("p t e -> p (t e)"), 0.0,
            k.c["tokpart"], ALU.mult, ALU.add))
        f = k.dve([f], lambda e: e.tensor_copy(facts[:, :, :, 2], weight[:]))
        f = k.dve([f], lambda e: e.tensor_tensor(rest[:], weight[:], facts[:, :, :, 2], ALU.subtract))
        f = k.dve([f], lambda e: e.tensor_copy(facts[:, :, :, 3], rest[:]))
        f = k.dve([f], lambda e: e.tensor_tensor(rest[:], rest[:], facts[:, :, :, 3], ALU.subtract))
        f = k.dve([f], lambda e: e.tensor_copy(facts[:, :, :, 4], rest[:]))

        picks = Ring([sb(f"f0_pick{n}", [P, E0, CAP], BF16) for n in range(2)])
        nt_, tbank, tfree = k.banks.take()
        for i in range(NT):
            np_, pick, pfree = picks.take()
            t1 = k.dve([u, pfree], lambda e, i=i, pick=pick: e.tensor_tensor(
                pick[:], over(place[:, i, :], CAP), under(k.c["iota_c"], E0), ALU.is_equal))
            builds = [lambda e, i=i, x=x, pick=pick: e.matmul(
                tbank[0:CAP, x * 5:(x + 1) * 5], pick[:, x, :], facts[:, i, x, :], start=(i == 0 and x == 0),
                stop=(i == NT - 1), skip_group_check=True) for x in range(E0)]
            t2 = k.pe([t1, f, tfree], *builds)
            picks.give(np_, t2)
        table = sb("f0_table", [CAP, E0, 5])
        number = sb("f0_number", [CAP, E0])
        empty = sb("f0_empty", [CAP, E0])
        index = sb("f0_index", [CAP, E0], U32)
        slot_w = sb("f0_slot_w", [CAP, E0])
        t = k.dve([t2], lambda e: e.tensor_copy(table[:].rearrange("p e f -> p (e f)"), tbank[0:CAP, 0:E0 * 5]))
        k.banks.give(nt_, t)
        t1 = k.dve([t], lambda e: e.tensor_tensor(number[:], table[:, :, 0], table[:, :, 1], ALU.add))
        t1 = k.dve([t1], lambda e: e.tensor_scalar(empty[:], number[:], 0.0, k.c["slot1"][0:CAP, :], ALU.is_equal,
                                                   ALU.mult))
        t1 = k.dve([t1], lambda e: e.scalar_tensor_tensor(number[:], number[:], -1.0, empty[:], ALU.add, ALU.add))
        indexed = k.dve([t1], lambda e: e.tensor_copy(index[:], number[:]))
        t1 = k.dve([t], lambda e: e.tensor_tensor(slot_w[:], table[:, :, 2], table[:, :, 3], ALU.add))
        weighed = k.dve([t1], lambda e: e.tensor_tensor(slot_w[:], slot_w[:], table[:, :, 4], ALU.add))

        swi = Swiglu(k, scope)
        n, slot, came = use_expert(k, 0)
        jobs = [dict(cols=tile_cols(k, i), m=P, slot=slot, s=1.0, w=1.0, clip=10.0,
                     after=[came, *both(k.cols_ready, i)]) for i in range(NT)]
        outs = {}

        def finish_shared(i):
            if i % 2 == 0:
                outs[i] = k.banks.take()
            nb, bank, freed = outs[i - i % 2]
            half = bank[:, (i % 2) * D:(i % 2 + 1) * D]
            t = swi.close(jobs[i], half, freed, True, True)
            if i % 2:
                outs["mm"] = t
                outs["t"] = k.copy(k.act, shared[:, i - 1:i + 1, :], bank[:].rearrange("p (t d) -> p t d", t=2), [t])
                k.banks.give(nb, outs["t"])

        skew(NT, lambda i: swi.open(jobs[i]), lambda i: swi.flip(jobs[i]), finish_shared)
        drop_expert(k, n, outs["mm"])
        k.sp.dma([outs["t"]], sum_out[1], lambda e: e.dma_start(tiled(sums[1]), shared[:]))
        stored = [(s.sem, s.count) for s in sum_out]

        depth = 4
        got = Ring([sb(f"f0_got{n}", [CAP, D]) for n in range(depth)])
        got_arrival = [k.arrival(f"f0_got{n}_in") for n in range(depth)]
        tcols = Ring([sb(f"f0_cols{n}", [P, DC, CAP]) for n in range(3)])
        ys = Ring([sb(f"f0_ys{n}", [CAP, D]) for n in range(depth)])
        added = [k.arrival(f"f0_added{n}") for n in range(2)]
        jobs = [dict(m=CAP, evac="act") for _ in range(E0)]

        def gather(x):
            n, buf, freed = got.take()
            jobs[x].update(ng=n, got=buf, came=k.pool.dma(
                [freed, indexed, rows_stored], got_arrival[n], lambda e: e.indirect_dma_start(
                    buf[:], None, h_rows, bass.IndirectOffsetOnAxis(ap=index[:, x:x + 1], axis=0))))

        def flip_in(x):
            job = jobs[x]
            nb, bank, freed = k.banks.take()
            t = k.turn([(bank[:, j * P:j * P + CAP], job["got"][:, j * P:(j + 1) * P]) for j in range(DC)],
                       [freed, job["came"]])
            got.give(job["ng"], t)
            nc_, cols, cfree = tcols.take()
            u = k.copy(k.dve, cols[:], bank[:, 0:DC * P].rearrange("p (j n) -> p j n", j=DC)[:, :, 0:CAP], [t, cfree])
            k.banks.give(nb, u)
            ns, slot, arrived = use_expert(k, 1 + x)
            job.update(nc=nc_, cols=[cols[:, j, :] for j in range(DC)], ns=ns, slot=slot, after=[arrived, u],
                       s=1.0, w=slot_w[:, x:x + 1], s_ready=weighed)

        def first(x):
            swi.open(jobs[x])
            tcols.give(jobs[x]["nc"], jobs[x]["gu_done"])

        def add_back(x):
            job = jobs[x]
            nb, bank, freed = k.banks.take()
            t = swi.close(job, bank[0:CAP, 0:D], freed, True, True)
            drop_expert(k, job["ns"], t)
            ny, y, yfree = ys.take()
            u = k.copy(k.act, y[:], bank[0:CAP, 0:D], [t, yfree])
            k.banks.give(nb, u)
            a = added[x % 2]
            tick = k.pool.dma([u, stored[x % 2], (a.sem, a.count) if a.count else None, indexed], a,
                              lambda e: e.indirect_dma_start(
                sums[x % 2], bass.IndirectOffsetOnAxis(ap=index[:, x:x + 1], axis=0), y[:], None,
                compute_op=ALU.add))
            ys.give(ny, tick)

        skew(E0, gather, lambda x: None, flip_in, first, lambda x: swi.flip(jobs[x]), add_back)
        back = k.arrival("sums_in")
        every = [(a.sem, a.count) for a in added]
        k.sp.dma([every, x_ready], back, lambda e: e.dma_start(k.x[:], tiled(sums[0])))
        k.sp.dma([], back, lambda e: e.dma_start(second[:], tiled(sums[1])))
        done = (back.sem, back.count)
        out = [(k.dve if i % 2 else k.pool)([done], lambda e, i=i: e.tensor_tensor(
            k.x[:, i, :], k.x[:, i, :], second[:, i, :], ALU.add)) for i in range(NT)]
    return out


def layer1_attention(k, x_ready):
    norm_pass(k, x_ready)
    with ExitStack() as scope:
        sb = lambda name, shape, dt=F32: k.sb(name, shape, dt, scope)
        w, c, W = k.l1, k.c, k.l1_in
        scale = float(1.0 / np.sqrt(np.float32(HD1 + R1)))
        ctx = k.ctxt["ctx"].rearrange("p (j t) -> p j t", j=DC)
        kvc = sb("a1_kvc", [KVC, CTX])
        n, bank, freed = k.banks.take()
        t = k.mm(bank[0:KVC, 0:CTX], [(w["kvc"].rearrange("p (j n) -> p j n", j=DC)[:, j, :], ctx[:, j, :])
                                      for j in range(DC)], [freed, W, k.ctx_in])
        kvc_ready = k.copy(k.act, kvc[:], bank[0:KVC, 0:CTX], [t, x_ready])
        k.banks.give(n, kvc_ready)
        qc = sb("a1_qc", [QC, TOK])
        dq = w["dq"].rearrange("p (j n) -> p j n", j=DC)
        qc_ready = []
        for half in range(TOK // BANK):
            n, bank, freed = k.banks.take()
            sl = slice(half * BANK, (half + 1) * BANK)
            t = k.mm(bank[0:QC, :], [(dq[:, j, :], k.cols[:, j, sl]) for j in range(DC)],
                     [freed, W, [r[half] for r in k.cols_ready]])
            qc_ready.append(k.copy(k.dve, qc[:, sl], bank[0:QC, :], [t]))
            k.banks.give(n, qc_ready[-1])
        key_blocks = sb("a1_key_blocks", [P, B, 2 * SC])
        turn_a = sb("a1_turn_a", [P, CTX])
        turn_b = sb("a1_turn_b", [P, CTX])
        n, bank, freed = k.banks.take()
        t = k.mm(bank[:, 0:CTX], [(w["kr"][0:KVC, :], kvc[:])], [freed, W, kvc_ready])
        t = k.mm(bank[:, CTX:2 * CTX], [(w["kr_swap"][0:KVC, :], kvc[:])], [])
        by_b = lambda ap: ap.rearrange("p (b s) -> p b s", b=B)
        u1 = k.dve([t, x_ready], lambda e: e.tensor_tensor(by_b(turn_a[:]), by_b(bank[:, 0:CTX]),
                                                           under(c["cos_k"], B), ALU.mult))
        u2 = k.dve([t], lambda e: e.tensor_tensor(by_b(turn_b[:]), by_b(bank[:, CTX:2 * CTX]),
                                                  under(c["sin_k"], B), ALU.mult))
        k.banks.give(n, u2)
        z = k.pool([x_ready], lambda e: e.memset(key_blocks[:], 0.0))
        u = k.dve([u1, u2], lambda e: e.tensor_tensor(turn_a[:], turn_a[:], turn_b[:], ALU.add))
        blocks_ready = k.dve([u, z], *[lambda e, h=h: e.tensor_scalar(
            key_blocks[h * R1:(h + 1) * R1, :, h * SC:(h + 1) * SC], by_b(turn_a[h * R1:(h + 1) * R1, :]), scale, None,
            ALU.mult) for h in range(2)])
        kq = sb("a1_kq", [QC, B, H1, SC])
        vo = sb("a1_vo", [P, B, H1 // 2, D])
        knope = Ring([sb(f"a1_knope{n}", [P, CTX]) for n in range(3)])
        vhead = Ring([sb(f"a1_vhead{n}", [P, CTX]) for n in range(3)])
        uk = w["uk"][0:KVC, :].rearrange("p (h d) -> p h d", h=H1)
        uv = w["uv"][0:KVC, :].rearrange("p (h d) -> p h d", h=H1)
        uq = w["uq"].rearrange("p (h d) -> p h d", h=H1)
        wo = w["wo"].rearrange("p (h d) -> p h d", h=H1)
        heads = [dict() for _ in range(H1)]

        def head_kv(h):
            n, bank, freed = k.banks.take()
            t = k.mm(bank[:, 0:CTX], [(uk[:, h, :], kvc[:])], [freed, W, kvc_ready])
            t = k.mm(bank[:, CTX:2 * CTX], [(uv[:, h, :], kvc[:])], [])
            nk, kb, kf = knope.take()
            nv, vb, vf = vhead.take()
            line = k.act if h % 2 else k.dve
            t1 = k.copy(line, kb[:], bank[:, 0:CTX], [t, kf])
            t2 = k.copy(line, vb[:], bank[:, CTX:2 * CTX], [t, vf])
            k.banks.give(n, t2)
            heads[h].update(nk=nk, kb=kb, nv=nv, vb=vb, t1=t1, t2=t2)

        def head_fold(h):
            d = heads[h]
            n, bank, freed = k.banks.take()
            t = k.mm(bank[0:QC, 0:CTX], [(uq[:, h, :], d["kb"][:])], [freed, d["t1"]])
            knope.give(d["nk"], t)
            d["kq"] = k.act([t], lambda e: e.activation(kq[:, :, h, :], by_b(bank[0:QC, 0:CTX]), ACT.Copy, scale=scale))
            k.banks.give(n, d["kq"])
            lo = (h % 2) * SC
            d["vo"] = []
            for pair in range(B // 2):
                n, bank, freed = k.banks.take()
                for b in range(2):
                    bb = pair * 2 + b
                    t = k.mm(bank[lo:lo + SC, b * D:(b + 1) * D], [(d["vb"][:, bb * SC:(bb + 1) * SC], wo[:, h, :])],
                             [freed, d["t2"], W])
                d["vo"].append(k.copy(k.dve if pair else k.act, vo[lo:lo + SC, pair * 2:pair * 2 + 2, h // 2, :],
                                      bank[lo:lo + SC, :].rearrange("p (b d) -> p b d", b=2), [t]))
                k.banks.give(n, d["vo"][-1])
            vhead.give(d["nv"], t)

        skew(H1, head_kv, head_fold)
        kq_ready = [d["kq"] for d in heads]
        vo_ready = [d["vo"] for d in heads]
        qrot = sb("a1_qrot", [P, H1 // 2, BANK])
        part = Ring([sb(f"a1_part{n}", [P, BANK]) for n in range(3)])
        qr = w["qr"][0:QC, :].rearrange("p (h d) -> p h d", d=P)
        qrs = w["qr_swap"][0:QC, :].rearrange("p (h d) -> p h d", d=P)
        qrot_ready = [[None] * (H1 // 2) for _ in range(2)]
        by_s = lambda ap: ap.rearrange("p (b s) -> p b s", s=S)

        def rotate(half, free):
            sl = slice(half * BANK, (half + 1) * BANK)
            for pr in range(H1 // 2):
                ticks = []
                for src, tab, dst in ((qr, "cos_q", None), (qrs, "sin_q", part)):
                    n, bank, freed = k.banks.take()
                    t = k.mm(bank[:], [(src[:, pr, :], qc[:, sl])], [freed, W, qc_ready[half]])
                    if dst is None:
                        o, pf = qrot[:, pr, :], free
                    else:
                        npart, pbuf, pf = part.take()
                        o = pbuf[:]
                    ticks.append(k.dve([t, pf], lambda e, o=o, bank=bank, tab=tab: e.tensor_tensor(
                        by_s(o), by_s(bank[:]), under(c[tab], 2), ALU.mult)))
                    k.banks.give(n, ticks[-1])
                t = k.pool(ticks, lambda e: e.tensor_tensor(qrot[:, pr, :], qrot[:, pr, :], pbuf[:], ALU.add))
                part.give(npart, t)
                qrot_ready[half][pr] = t
        seg = sb("a1_seg", [P, NT])
        block = sb("a1_block", [P, NT, SC])
        under_seg = sb("a1_under", [P, NT, SC])
        t = k.dve([k.seg_in, x_ready], lambda e: e.tensor_copy(seg[:], k.seg_i[:]))
        keys = under(k.keys[:], NT)
        t1 = k.dve([t, k.const_in], lambda e: e.tensor_tensor(block[:], keys, over(seg[:], SC), ALU.is_le))
        t2 = k.dve([t1], lambda e: e.tensor_scalar(seg[:], seg[:], float(LOOK), None, ALU.subtract))
        t2 = k.dve([t2], lambda e: e.tensor_tensor(under_seg[:], keys, over(seg[:], SC), ALU.is_ge))
        t = k.dve([t1, t2], lambda e: e.tensor_tensor(block[:], block[:], under_seg[:], ALU.mult))
        block_ready = k.dve([t], lambda e: e.tensor_scalar(block[:], block[:], -1.0, -NEG, ALU.add, ALU.mult))

        soft = Soft(k, scope, k.l1_space, [kq_ready, vo_ready])
        jobs = [dict() for _ in range(NT)]

        def score(i):
            b, job = i // TPB, jobs[i]
            sbuf = soft.begin(job)
            for hb in range(2):
                n, bank, freed = k.banks.take()
                hs = slice(hb * 8, hb * 8 + 8)
                t = k.mm(bank[:], [(qc[:, i * P:(i + 1) * P], kq[:, b, hs, :].rearrange("p h s -> p (h s)"))],
                         [freed, qc_ready, kq_ready], stop=False, shared=True)
                for pr in range(4):
                    t = k.mm(bank[:, pr * P:(pr + 1) * P], [(qrot[:, hb * 4 + pr, (i % HALF) * P:(i % HALF + 1) * P],
                                                             key_blocks[:, b, :])],
                             [blocks_ready, qrot_ready[i // HALF][hb * 4 + pr]], start=False, stop=(pr == 3),
                             shared=True)
                u = k.dve([t, block_ready, job["free"]], lambda e, bank=bank, hs=hs: e.tensor_tensor(
                    sbuf[:, hs, :], bank[:].rearrange("p (h s) -> p h s", h=8), under(block[:, i, :], 8), ALU.add))
                k.banks.give(n, u)
            job["scored"] = t
            soft.shift(job, sbuf, [u])

        def out(i):
            b, job = i // TPB, jobs[i]
            n, bank, freed = k.banks.take()
            t = k.mm(bank[:, 0:D], [(job["pt"][:, pr, :], vo[:, b, pr, :]) for pr in range(H1 // 2)],
                     [freed, vo_ready, job["pt_ready"]])
            soft.end(job, t)
            job["x"] = k.dve([t], lambda e: e.tensor_tensor(k.x[:, i, :], k.x[:, i, :], bank[:, 0:D], ALU.add))
            k.banks.give(n, job["x"])

        rotate(0, [])

        def score_or_rotate(i):
            score(i)
            if i == HALF - 1:
                rotate(1, [jobs[i]["scored"]])

        skew(NT, score_or_rotate, lambda i: soft.power(jobs[i], 1.0), lambda i: soft.flip(jobs[i]), out)
    return [job["x"] for job in jobs]


class Soft:

    def __init__(self, k, scope, space=None, after=()):
        self.k, heads, depth, cols = k, 16, 3, 16 * SC
        space = space if space is not None else k.sb("soft_space", [P, 5 * cols], scope=scope)
        part = [space[:, n * cols:(n + 1) * cols] for n in range(5)]
        self.s = Ring([a.rearrange("p (h s) -> p h s", h=heads) for a in part[:depth]], after)
        self.pt = Ring([a.rearrange("p (r q) -> p r q", q=P) for a in part[depth:]], after)
        self.top = Ring([k.sb(f"soft_top{n}", [P, heads], scope=scope) for n in range(depth)])
        self.sum = Ring([k.sb(f"soft_sum{n}", [P, heads], scope=scope) for n in range(depth)])

    def begin(self, job):
        job["ns"], job["s"], free = self.s.take()
        job["free"] = list(free)
        return job["s"]

    def shift(self, job, src, after):
        k, s = self.k, job["s"]
        nt, top, tf = self.top.take()
        t = k.dve([after, tf], lambda e: e.tensor_reduce(top[:], src, AX.X, ALU.max))
        job["shifted"] = k.pool([t], lambda e: e.tensor_tensor(s, src, over(top[:], SC), ALU.subtract))
        self.top.give(nt, job["shifted"])

    def power(self, job, scale):
        k, s = self.k, job["s"]
        nm, total, mf = self.sum.take()
        t = k.act([job["shifted"]], lambda e: e.activation(s, s, ACT.Exp, scale=scale))
        u = k.dve([t, mf], lambda e: e.tensor_reduce(total[:], s, AX.X, ALU.add))
        u = k.dve([u], lambda e: e.reciprocal(total[:], total[:]))
        job["probs"] = k.pool([u], lambda e: e.tensor_tensor(s, s, over(total[:], SC), ALU.mult))
        self.sum.give(nm, job["probs"])

    def flip(self, job):
        k, s = self.k, job["s"]
        npt, pt, pf = self.pt.take()
        job.update(npt=npt, pt=pt, pt_ready=[])
        for hb in range(2):
            n, bank, freed = k.banks.take()
            t = k.turn([(bank[:, pr * P:(pr + 1) * P],
                         s[:, 2 * (hb * 4 + pr):2 * (hb * 4 + pr) + 2, :].rearrange("p h s -> p (h s)"))
                        for pr in range(4)], [freed, job["probs"]])
            u = k.copy(k.act, pt[:, hb * 4:hb * 4 + 4, :].rearrange("p a b -> p (a b)"), bank[:], [t, pf])
            k.banks.give(n, u)
            job["pt_ready"].append(u)
        self.s.give(job["ns"], t)

    def end(self, job, tick):
        self.pt.give(job["npt"], tick)


def dense_experts(k, scope, first, count, scales, weights, ready):
    swi = Swiglu(k, scope)
    acc = [k.banks.take() for _ in range(NT // 2)]
    jobs, used = [], {}
    for e in range(count):
        for i in range(NT):
            jobs.append(dict(e=e, i=i, m=P, s=scales(e, i), w=weights(e, i), s_ready=ready, cols=tile_cols(k, i),
                             evac="act" if i % 2 else "dve"))

    def open_(n):
        job = jobs[n]
        if job["i"] == 0:
            used[job["e"]] = use_expert(k, first + job["e"])
        job["slot"] = used[job["e"]][1]
        job["after"] = [used[job["e"]][2], *both(k.cols_ready, job["i"])]
        swi.open(job)

    def close(n):
        job = jobs[n]
        e, i = job["e"], job["i"]
        _, bank, freed = acc[i // 2]
        job["t"] = swi.close(job, bank[:, (i % 2) * D:(i % 2 + 1) * D], freed, e == 0 and i % 2 == 0,
                             e == count - 1, shared=True)
        if i == NT - 1:
            drop_expert(k, used[e][0], job["t"])

    skew(len(jobs), open_, lambda n: swi.flip(jobs[n]), close)
    out = []
    for i in range(NT):
        n, bank, _ = acc[i // 2]
        out.append(k.dve([jobs[-NT + i]["t"], k.cols_ready, jobs[-1]["t"]], lambda e, i=i, bank=bank: e.tensor_tensor(
            k.x[:, i, :], k.x[:, i, :], bank[:, (i % 2) * D:(i % 2 + 1) * D], ALU.add)))
        if i % 2:
            k.banks.give(n, out[-1])
    return out


def sigmoid_exact(k, out, src, after):
    t = k.dve(after, lambda e: e.tensor_scalar(out[:], src[:], -88.0, None, ALU.max))
    t = k.act([t], lambda e: e.activation(out[:], out[:], ACT.Exp, scale=-1.0))
    t = k.dve([t], lambda e: e.tensor_scalar(out[:], out[:], 1.0, None, ALU.add))
    return k.dve([t], lambda e: e.reciprocal(out[:], out[:]))


def layer1_ffn(k, x_ready):
    norm_pass(k, x_ready)
    with ExitStack() as scope:
        sb = lambda name, shape, dt=F32: k.sb(name, shape, dt, scope)
        logits = sb("f1_logits", [P, NT, E1])
        scores = sb("f1_scores", [P, NT, E1])
        lg = gate_logits(k, k.l0["gate1"], E1, logits, k.cols_ready)
        t = sigmoid_exact(k, scores, logits, [lg])
        mask, t = routing(k, scope, E1, K1, lg, scores, scores, t)
        t = k.dve([t], lambda e: e.tensor_tensor(scores[:], scores[:], mask[:], ALU.mult))
        pick = lambda e, i: 1.0 if e == 0 else scores[:, i, e - 1:e]
        return dense_experts(k, scope, 1 + E0, 1 + E1, pick, pick, t)


def layer3_ffn(k, x_ready):
    norm_pass(k, x_ready)
    with ExitStack() as scope:
        sb = lambda name, shape, dt=F32: k.sb(name, shape, dt, scope)
        logits = sb("f3_logits", [P, NT, E3])
        affinity = sb("f3_affinity", [P, NT, E3])
        biased = sb("f3_biased", [P, NT, E3])
        total = sb("f3_total", [P, NT])
        lg = gate_logits(k, k.l0["gate3"], E3, logits, k.cols_ready)
        t = sigmoid_exact(k, affinity, logits, [lg])
        t = k.dve([t], lambda e: e.tensor_tensor(biased[:], affinity[:], under(k.l0["bias3"], NT), ALU.add))
        mask, t = routing(k, scope, E3, K3, lg, affinity, biased, t)
        t = k.dve([t], lambda e: e.tensor_tensor(mask[:], affinity[:], mask[:], ALU.mult))
        t = k.dve([t], lambda e: e.tensor_reduce(total[:], mask[:], AX.X, ALU.add))
        t = k.dve([t], lambda e: e.tensor_scalar(total[:], total[:], 1e-9, None, ALU.add))
        t = k.dve([t], lambda e: e.reciprocal(total[:], total[:]))
        t = k.dve([t], lambda e: e.tensor_tensor(mask[:], mask[:], over(total[:], E3), ALU.mult))
        return dense_experts(k, scope, 1 + E0 + 1 + E1, 2 + E3, lambda e, i: 1.0,
                             lambda e, i: 0.1 if e < 2 else mask[:, i, e - 2:e - 1], t)


def fp8_steps(k, y, m, after):
    t = k.dve(after, lambda e: e.tensor_scalar(y, y, FP8_MAX, -FP8_MAX, ALU.min, ALU.max))
    t = k.dve([t], lambda e: e.tensor_scalar(m.bitcast(U16), y.bitcast(U16), 0x7F80, None, ALU.bitwise_and))
    return k.dve([t], lambda e: e.tensor_scalar(m, m, 2.0 ** -6, 1.5 * 2.0 ** 20, ALU.max, ALU.mult))


def fp8_round(line, y, m, wide, out, after, free):
    t = line([after, free], lambda e: e.tensor_tensor(wide, y, m, ALU.add))
    return line([t], lambda e: e.tensor_tensor(out, wide, m, ALU.subtract))


def split(k, src, high, low, kept, after):
    t = k.dve(after, lambda e: e.tensor_scalar(kept.bitcast(I32), src.bitcast(I32), 12, 12, ALU.logical_shift_right,
                                               ALU.logical_shift_left))
    u = k.dve([t], lambda e: e.tensor_copy(high, kept))
    return u, k.pool([t], lambda e: e.tensor_tensor(low, src, kept, ALU.subtract))


def layer2_attention(k, x_ready):
    with ExitStack() as scope:
        sb = lambda name, shape, dt=F32: k.sb(name, shape, dt, scope)
        w, W = k.l2, k.l2_in
        raw_w = sb("a2_raw_w", [P, DC, GW])
        raw_p = sb("a2_raw_proj", [P, 2 * HPG * D])
        raw_w_arrival, raw_p_arrival = k.arrival("a2_raw_w_in"), k.arrival("a2_raw_proj_in")
        w_in, p_in = {}, {}

        def load_w(g, *after):
            if g < G2:
                w_in[g] = k.sp.dma(after, raw_w_arrival, lambda e: e.dma_start(
                    raw_w[:], k.group_dram[g][:, 0:DC * GW].rearrange("p (j n) -> p j n", j=DC)))

        def load_p(g, *after):
            if g < G2:
                p_in[g] = k.sp.dma(after, raw_p_arrival, lambda e: e.dma_start(raw_p[:], k.group_dram[g][:, DC * GW:]))

        load_w(0, x_ready)
        load_p(0)
        again = normalise(k, k.rows, k.rows, normalise(k, k.x, k.rows, x_ready))
        ln, acc = k.cols, k.rows
        ln_ready = transpose_rows(k, k.rows, ln, again, w["ln_w"], w["ln_b"], free=[W, x_ready])
        names = ("q", "qx", "k", "v")
        cols_of = {"q": slice(0, HPG * P), "qx": slice(HPG * P, 2 * HPG * P),
                   "k": slice(2 * HPG * P, (2 * HPG + 1) * P), "v": slice((2 * HPG + 1) * P, (2 * HPG + 2) * P)}
        own_w = (2 * HPG + 2) * P
        scaled = {n: sb(f"a2_in_{n}", [P, DC, TOK], F32R) for n in names}
        inv = sb("a2_inv", [P, 4, DC])
        fold = sb("a2_fold", [P, 4, DC])
        early = scope.enter_context(ExitStack())
        y = Ring([k.sb(f"a2_y{n}", [P, TOK], BF16, early) for n in range(4)])
        m = Ring([k.sb(f"a2_m{n}", [P, TOK], BF16, early) for n in range(4)])
        wide = Ring([k.sb(f"a2_wide{n}", [P, TOK], F32, early) for n in range(4)])
        in_ready, folded, jobs = {}, {}, []
        for q, name in enumerate(names):
            ti = k.dve([W, x_ready], lambda e, q=q, name=name: e.reciprocal(inv[:, q, :], w[f"{name}_in"]))
            folded[name] = k.dve([W], lambda e, q=q, name=name: e.tensor_scalar(
                fold[:, q, :], w[f"{name}_in"], w[f"w{name}_s"], None, ALU.mult))
            jobs += [dict(q=q, name=name, j=j, inv=ti) for j in range(DC)]

        def scale_down(n):
            job = jobs[n]
            ny, yb, yf = y.take()
            nm, mb, mf = m.take()
            t = k.act([job["inv"], ln_ready[job["j"]], yf], lambda e: e.activation(
                yb[:], ln[:, job["j"], :], ACT.Copy, scale=inv[:, job["q"], job["j"]:job["j"] + 1]))
            job.update(ny=ny, y=yb, nm=nm, m=mb, steps=fp8_steps(k, yb[:], mb[:], [t, mf]))

        def round_down(n):
            job = jobs[n]
            nw, wb, wf = wide.take()
            t = fp8_round(k.pool if n % 3 == 2 else k.dve, job["y"][:], job["m"][:], wb[:],
                          scaled[job["name"]][:, job["j"], :], job["steps"], wf)
            y.give(job["ny"], t)
            m.give(job["nm"], t)
            wide.give(nw, t)
            in_ready.setdefault(job["name"], []).append(t)

        skew(len(jobs), scale_down, round_down)
        early.close()
        used = list(in_ready.values())
        wparts = Ring([[sb(f"a2_w_{part}{n}", [P, DC, own_w], F32R) for part in ("high", "low")] for n in range(2)],
                      used)
        pparts = Ring([[sb(f"a2_proj_{part}{n}", [P, 2 * HPG, D], F32R) for part in ("high", "low")]
                       for n in range(2)], used)
        kept = Ring([sb("a2_kept", [P, BANK])], used)
        ismooth = sb("a2_ismooth", [P, 2 * NH2])
        pscale = sb("a2_pscale", [P, 1])
        sm = k.dve([W, used], lambda e: e.reciprocal(ismooth[:], w["smooth"]))
        ps = k.dve([W, used], lambda e: e.tensor_tensor(pscale[:], w["p_in"], w["p_w"], ALU.mult))
        ctx = k.ctxt["ctx"].rearrange("p (j t) -> p j t", j=DC)
        twice = k.ctxt["twice"].rearrange("p (j b t) -> p j b t", j=DC, b=B)
        softscale = float(1.0 / np.sqrt(D2))

        qn = Ring([sb("a2_qn", [P, TPB, 5, P])], used)
        qt = Ring([sb(f"a2_qt{n}", [P, 2 * HPG, S]) for n in range(2)], used)
        kt = Ring([sb(f"a2_kt{n}", [P, S]) for n in range(2)], used)
        vs = Ring([sb(f"a2_vs{n}", [P, TPB, D2]) for n in range(5)], used)
        kx = Ring([sb(f"a2_kx{n}", [P, CTX]) for n in range(2)], used)
        kxn = Ring([sb("a2_kxn", [P, CTX // P, D2])], used)
        vx = Ring([sb(f"a2_vx{n}", [P, B, D2]) for n in range(2)], used)
        stats = Moments(k, 5 * TPB, scope)
        n_own, n_all = HPG * S, HPG * (S + SC)
        probs = Ring([sb("a2_p", [P, TPB, n_all])], used)
        own = lambda p: p[:, 0:n_own].rearrange("p (h s) -> p h s", h=HPG)
        cross = lambda p: p[:, n_own:n_all].rearrange("p (h s) -> p h s", h=HPG)
        top = Ring([sb(f"a2_top{n}", [P, 2 * HPG]) for n in range(3)], used)
        tot = Ring([sb(f"a2_tot{n}", [P, 2 * HPG]) for n in range(3)], used)
        pt = Ring([k.cols[:, n, :].rearrange("p (h c t) -> p h c t", h=HPG, c=TPB) for n in range(2)], used)
        px = Ring([sb(f"a2_px{n}", [P, S]) for n in range(2)], used)
        cat = Ring([sb("a2_cat", [P, 2 * HPG * S], BF16)], used)
        catm = Ring([sb("a2_catm", [P, 2 * HPG * S], BF16)], used)
        catw = Ring([sb("a2_catw", [P, 2 * HPG * S])], used)
        catq = Ring([sb(f"a2_catq{n}", [P, 2 * HPG, S], F32R) for n in range(2)], used)
        acc_ready = [k.pool([ln_ready], lambda e, i=i: e.memset(acc[:, i, :], 0.0)) for i in range(NT)]
        units = [dict(g=g, b=b) for g in range(G2) for b in range(B)]
        groups = {}

        def split_pieces(pieces):
            ready = []
            for src, high, low, after in pieces:
                nk, kb, kf = kept.take()
                u = split(k, src, high, low, kb[:, 0:src.shape[1]], [after, kf])
                kept.give(nk, *u)
                ready += u
            return ready

        def split_w(g):
            gr = groups[g] = dict(came=w_in[g])
            gr["nw"], (high, low), free = wparts.take()
            gr["wparts"] = (high, low)
            pieces = []
            for j in range(DC):
                ready = [k.act([gr["came"], folded[name]], lambda e, q=q, cs=cols_of[name]: e.activation(
                    raw_w[:, j, cs], raw_w[:, j, cs], ACT.Copy, scale=fold[:, q, j:j + 1]))
                    for q, name in enumerate(names)]
                pieces += [(raw_w[:, j, cs], high[:, j, cs], low[:, j, cs], [ready[-1], free])
                           for cs in (slice(0, 2 * HPG * P), slice(2 * HPG * P, own_w))]
            gr["w_ready"] = split_pieces(pieces)

        def split_p(g):
            gr = groups[g]
            gr["np"], (high, low), free = pparts.take()
            gr["pparts"] = (high, low)
            flat = lambda a: a[:].rearrange("p c d -> p (c d)")
            gr["p_ready"] = split_pieces([(raw_p[:, a:a + BANK], flat(high)[:, a:a + BANK], flat(low)[:, a:a + BANK],
                                           [p_in[g], free]) for a in range(0, 2 * HPG * D, BANK)])
            load_p(g + 1, gr["p_ready"])

        def group_context(g):
            gr = groups[g]
            came = gr["came"]
            at = own_w
            nb, bank, freed = k.banks.take()
            for i in range(CTX // P):
                t = k.mm(bank[:, i * P:(i + 1) * P], [(ctx[:, j, i * P:(i + 1) * P], raw_w[:, j, at:at + P])
                                                      for j in range(DC)], [freed, came])
            for b in range(B):
                if b == 0:
                    n2, bank2, freed = k.banks.take()
                t2 = k.mm(bank2[:, b * P:(b + 1) * P], [(twice[:, j, b, :], raw_w[:, j, at + P:at + 2 * P])
                                                        for j in range(DC)], [freed, came])
            nn, kn, kf = kxn.take()
            t = moments(k, [bank[:, i * P:(i + 1) * P] for i in range(CTX // P)], stats, 1e-5, [[t, stats_free]] * 2)
            t = k.dve([t, kf], *[lambda e, i=i: e.tensor_scalar(
                kn[:, i, :], bank[:, i * P:(i + 1) * P], stats.minus[:, i:i + 1], stats.rstd[:, i:i + 1], ALU.add,
                ALU.mult) for i in range(CTX // P)])
            stats_free[:] = [t]
            k.banks.give(nb, t)
            nv, vb, vf = vx.take()
            gr["vx_ready"] = k.copy(k.act, vb[:].rearrange("p b d -> p (b d)"), bank2[:], [t2, vf])
            k.banks.give(n2, gr["vx_ready"])
            gr.update(nv=nv, vx=vb, nn=nn, kn=kn, kn_ready=t)
            load_w(g + 1, t2, gr["w_ready"])

        def group_keys(g):
            gr = groups[g]
            nb, bank, freed = k.banks.take()
            t = k.turn([(bank[:, i * P:(i + 1) * P], gr["kn"][:, i, :]) for i in range(CTX // P)],
                       [freed, gr["kn_ready"]])
            kxn.give(gr["nn"], t)
            nk, kb, kf = kx.take()
            gr["kx_ready"] = k.act([t, kf], lambda e: e.activation(
                kb[:], bank[:, 0:CTX], ACT.Identity, bias=w["kxln_b"], scale=w["kxln_w"]))
            k.banks.give(nb, gr["kx_ready"])
            gr.update(nk=nk, kx=kb)

        stats_free = []

        def project(n):
            un = units[n]
            g, b = un["g"], un["b"]
            if n == 0:
                split_w(0)
                split_p(0)
                group_context(0)
            gr = groups[g]
            nv, v, vf = vs.take()
            toks = [slice((b * TPB + ti) * P, (b * TPB + ti + 1) * P) for ti in range(TPB)]

            def product(out, name, ti, freed, shared):
                cs = cols_of[name]
                return k.mm(out, [(scaled[name][:, j, toks[ti]], part[:, j, cs]) for j in range(DC)
                                  for part in gr["wparts"]], [freed, in_ready[name], gr["w_ready"]])

            qbanks = []
            for ti in range(TPB):
                nb, bank, freed = k.banks.take()
                for a, name in ((0, "q"), (HPG * P, "qx")):
                    t = product(bank[:, a:a + HPG * P], name, ti, freed, True)
                qbanks.append((nb, bank, t))
            kb_, kbank, freed = k.banks.take()
            for ti in range(TPB):
                tk = product(kbank[:, ti * P:(ti + 1) * P], "k", ti, freed, True)
            vb_, vbank, freed = k.banks.take()
            for ti in range(TPB):
                tv = product(vbank[:, ti * P:(ti + 1) * P], "v", ti, freed, True)
            if b == B - 1:
                wparts.give(gr["nw"], tv)
            un["v_ready"] = k.copy(k.act, v[:].rearrange("p t d -> p (t d)"), vbank[:, 0:S], [tv, vf])
            k.banks.give(vb_, un["v_ready"])
            nn, q_n, nf = qn.take()
            srcs, after = [], []
            for nb, bank, t in qbanks:
                srcs += [bank[:, c * P:(c + 1) * P] for c in range(2 * HPG)]
                after += [[t, stats_free]] * (2 * HPG)
            srcs += [kbank[:, ti * P:(ti + 1) * P] for ti in range(TPB)]
            after += [tk] * TPB
            t = moments(k, srcs, stats, 1e-5, after)
            dst = [q_n[:, ti, c, :] for ti in range(TPB) for c in range(2 * HPG)] + [q_n[:, ti, 4, :]
                                                                                     for ti in range(TPB)]
            a = k.act([t, nf], *[lambda e, i=i: e.activation(
                dst[i], srcs[i], ACT.Identity, bias=stats.shift[:, i:i + 1], scale=stats.rstd[:, i:i + 1])
                for i in range(2 * HPG)])
            v_ = k.dve([t, nf], *[lambda e, i=i: e.tensor_scalar(
                dst[i], srcs[i], stats.minus[:, i:i + 1], stats.rstd[:, i:i + 1], ALU.add, ALU.mult)
                for i in range(2 * HPG, len(dst))])
            stats_free[:] = [a, v_]
            k.banks.give(qbanks[0][0], a)
            k.banks.give(qbanks[1][0], v_)
            k.banks.give(kb_, v_)
            un.update(nv=nv, v=v, nn=nn, qn=q_n, qn_ready=[a, v_])
            if b == B - 2 and g + 1 < G2:
                split_w(g + 1)
            if b == 1 and g:
                split_p(g)
            if b == B - 1 and g + 1 < G2:
                group_context(g + 1)

        def turn_queries(n):
            un = units[n]
            g, b = un["g"], un["b"]
            if b == 0:
                group_keys(g)
            q_n = un["qn"]
            nq, qb, qf = qt.take()
            nk, kb, kf = kt.take()
            ready = []
            for part, nm in enumerate(("qln", "qxln")):
                nb, bank, freed = k.banks.take()
                t = k.turn([(bank[:, (c * TPB + ti) * P:(c * TPB + ti + 1) * P], q_n[:, ti, part * HPG + c, :])
                            for c in range(HPG) for ti in range(TPB)], [freed, un["qn_ready"]])
                ready.append(k.act([t, qf], lambda e, part=part, nm=nm, bank=bank: e.activation(
                    qb[:, part * HPG:(part + 1) * HPG, :], bank[:].rearrange("p (c t) -> p c t", c=HPG), ACT.Identity,
                    bias=w[f"{nm}_b"], scale=w[f"{nm}_w"])))
                k.banks.give(nb, ready[-1])
            nb, bank, freed = k.banks.take()
            t = k.turn([(bank[:, ti * P:(ti + 1) * P], q_n[:, ti, 4, :]) for ti in range(TPB)], [freed])
            ready.append(k.act([t, kf], lambda e: e.activation(
                kb[:], bank[:, 0:S], ACT.Identity, bias=w["kln_b"], scale=w["kln_w"])))
            k.banks.give(nb, ready[-1])
            qn.give(un["nn"], t)
            un.update(nq=nq, q=qb, nk=nk, kt=kb, q_ready=ready)

        def attend(n):
            un = units[n]
            gr, b = groups[un["g"]], un["b"]
            qb, kb = un["q"], un["kt"]
            np_, pbuf, pf = probs.take()
            un.update(np=np_, probs=pbuf, p_ready=[])
            for ti in range(TPB):
                p = pbuf[:, ti, :]
                tok = slice(ti * P, (ti + 1) * P)
                n1, b1, f1 = k.banks.take()
                n2, b2, f2 = k.banks.take()
                for h in range(HPG):
                    t = k.mm(b1[:, h * S:(h + 1) * S], [(qb[:, h, tok], kb[:])], [f1, un["q_ready"]])
                for h in range(HPG):
                    t2 = k.mm(b2[:, h * SC:(h + 1) * SC], [(qb[:, HPG + h, tok], gr["kx"][:, b * SC:(b + 1) * SC])],
                              [f2, gr["kx_ready"]])
                nt, tp, tf = top.take()
                u = k.dve([t, tf], lambda e, b1=b1, tp=tp: e.tensor_reduce(
                    tp[:, 0:HPG], b1[:].rearrange("p (h s) -> p h s", h=HPG), AX.X, ALU.max))
                u = k.dve([t2, tf], lambda e, b2=b2, tp=tp: e.tensor_reduce(
                    tp[:, HPG:2 * HPG], b2[:, 0:HPG * SC].rearrange("p (h s) -> p h s", h=HPG), AX.X, ALU.max))
                u = k.dve([u], lambda e, tp=tp: e.tensor_scalar(tp[:], tp[:], -softscale, None, ALU.mult))
                ns, tt, sf = tot.take()
                for h in range(HPG):
                    a = k.act([u, pf, sf], lambda e, h=h, p=p, b1=b1, tp=tp, tt=tt: e.activation(
                        own(p)[:, h, :], b1[:, h * S:(h + 1) * S], ACT.Exp, bias=tp[:, h:h + 1], scale=softscale,
                        accum_out=tt[:, h:h + 1]))
                    a = k.act([], lambda e, h=h, p=p, b2=b2, tp=tp, tt=tt: e.activation(
                        cross(p)[:, h, :], b2[:, h * SC:(h + 1) * SC], ACT.Exp, bias=tp[:, HPG + h:HPG + h + 1],
                        scale=softscale, accum_out=tt[:, HPG + h:HPG + h + 1]))
                k.banks.give(n1, a)
                k.banks.give(n2, a)
                top.give(nt, a)
                r = k.dve([a], lambda e, tt=tt: e.reciprocal(tt[:], tt[:]))
                k.pool([r], lambda e, p=p, tt=tt: e.tensor_tensor(own(p), own(p), over(tt[:, 0:HPG], S), ALU.mult))
                z = k.pool([], lambda e, p=p, tt=tt: e.tensor_tensor(cross(p), cross(p), over(tt[:, HPG:2 * HPG], SC),
                                                                     ALU.mult))
                tot.give(ns, z)
                un["p_ready"].append(z)
            qt.give(un["nq"], t2)
            kt.give(un["nk"], t2)
            if b == B - 1:
                kx.give(gr["nk"], t2)

        def flip(n):
            un = units[n]
            nt, ptb, tf = pt.take()
            nx, pxb, xf = px.take()
            ready = []
            nc_, cbank, cfree = k.banks.take()
            for ti in range(TPB):
                p, z = un["probs"][:, ti, :], un["p_ready"][ti]
                tok = slice(ti * P, (ti + 1) * P)
                n1, b1, f1 = k.banks.take()
                t = k.turn([(b1[:, (h * TPB + kk) * P:(h * TPB + kk + 1) * P], own(p)[:, h, kk * P:(kk + 1) * P])
                            for h in range(HPG) for kk in range(TPB)], [f1, z])
                u = k.copy(k.act if ti else k.dve, ptb[:, :, :, tok],
                           b1[:].rearrange("p (h c t) -> p h c t", h=HPG, c=TPB), [t, tf])
                k.banks.give(n1, u)
                ready.append(u)
                t = k.turn([(cbank[:, tok], p[:, n_own:n_all])], [cfree, z])
            probs.give(un["np"], t)
            u = k.copy(k.dve, pxb[:], cbank[:, 0:S], [t, xf])
            k.banks.give(nc_, u)
            ready.append(u)
            un.update(nt=nt, pt=ptb, nx=nx, px=pxb, pt_ready=ready)

        def values(n):
            un = units[n]
            g, b = un["g"], un["b"]
            gr = groups[g]
            n1, b1, f1 = k.banks.take()
            for h in range(HPG):
                t = k.mm(b1[:, h * S:(h + 1) * S], [(un["v"][:, kk, :], un["pt"][:, h, kk, :]) for kk in range(TPB)],
                         [f1, un["v_ready"], un["pt_ready"]])
            side = [k.banks.take() for _ in range(HPG)]
            for h, (_, bank, freed) in enumerate(side):
                part = slice(h * SC, (h + 1) * SC)
                t2 = k.mm(bank[:, 0:S], [(gr["vx"][part, b, :], un["px"][part, :])], [freed, gr["vx_ready"]])
            vs.give(un["nv"], t2)
            pt.give(un["nt"], t2)
            px.give(un["nx"], t2)
            if b == B - 1:
                vx.give(gr["nv"], t2)
            nc_, cb, cf = cat.take()
            outs = [(b1[:, h * S:(h + 1) * S], t) for h in range(HPG)] + [(bank[:, 0:S], t2) for _, bank, _ in side]
            for c, (src, tick) in enumerate(outs):
                ch = (c // HPG) * NH2 + g * HPG + c % HPG
                u = k.act([tick, cf, sm], lambda e: e.activation(cb[:, c * S:(c + 1) * S], src, ACT.Copy,
                                                                 scale=ismooth[:, ch:ch + 1]))
            for number in (n1, side[0][0], side[1][0]):
                k.banks.give(number, u)
            nm, mb, mf = catm.take()
            nw, wb, wf = catw.take()
            nq, qb, qf = catq.take()
            t = fp8_steps(k, cb[:], mb[:], [u, mf])
            t = fp8_round(k.pool, cb[:], mb[:], wb[:], qb[:].rearrange("p c t -> p (c t)"), [t, qf], wf)
            cat.give(nc_, t)
            catm.give(nm, t)
            catw.give(nw, t)
            un.update(ncq=nq, catq=qb, cat_ready=t)

        def output(n):
            un = units[n]
            gr, b = groups[un["g"]], un["b"]
            nb, bank, freed = k.banks.take()
            for ti in range(TPB):
                t = k.mm(bank[:, ti * D:(ti + 1) * D],
                         [(un["catq"][:, c, ti * P:(ti + 1) * P], part[:, c, :]) for c in range(2 * HPG)
                          for part in gr["pparts"]], [freed, un["cat_ready"], gr["p_ready"]])
            catq.give(un["ncq"], t)
            i = b * TPB
            u = k.dve([t, acc_ready[i]], lambda e: e.tensor_tensor(
                acc[:, i:i + TPB, :], acc[:, i:i + TPB, :], bank[:].rearrange("p (t d) -> p t d", t=TPB), ALU.add))
            acc_ready[i] = acc_ready[i + 1] = u
            k.banks.give(nb, u)
            if b == B - 1:
                pparts.give(gr["np"], t)

        skew(len(units), project, turn_queries, attend, flip, values, output, oldest_first=True)
        out = [k.dve([acc_ready[i], ps], lambda e, i=i: e.scalar_tensor_tensor(
            k.x[:, i, :], acc[:, i, :], pscale[:, 0:1], k.x[:, i, :], ALU.mult, ALU.add)) for i in range(NT)]
    return out


def layer2_ffn(k, x_ready):
    with ExitStack() as scope:
        sb = lambda name, shape, dt=F32: k.sb(name, shape, dt, scope)
        w, W = k.l2f, k.l2f_in
        quantised = {}
        absum = sb("f2_absum", [P, 3])
        gamma = sb("f2_gamma", [P, 3])
        n, bank, freed = k.banks.take()
        t = [k.dve([W, x_ready], lambda e, q=q, name=name: e.tensor_reduce(
            absum[:, q:q + 1], w[name], AX.X, ALU.add, apply_absolute_value=True))
            for q, name in enumerate(("w1", "w2", "w3"))]
        t = k.mm(bank[:, 0:3], [(k.c["ones"], absum[:])], [freed, t])
        t = k.dve([t], lambda e: e.tensor_scalar(gamma[:], bank[:, 0:3], 1.0 / (FFN2 * D), 1e-8, ALU.mult, ALU.add))
        k.banks.give(n, t)
        g = k.dve([t], lambda e: e.reciprocal(gamma[:], gamma[:]))
        for q, name in enumerate(("w1", "w2", "w3")):
            t = k.dve([g], lambda e, q=q, name=name: e.tensor_scalar(w[name], w[name], gamma[:, q:q + 1], ROUND,
                                                                   ALU.mult, ALU.add))
            t = k.dve([t], lambda e, name=name: e.tensor_scalar(w[name], w[name], ROUND, 1.0, ALU.subtract, ALU.min))
            quantised[name] = k.dve([t], lambda e, name=name: e.tensor_scalar(w[name], w[name], -1.0, None, ALU.max))
        norm_pass(k, x_ready)
        hidden = sb("f2_hidden", [P, FC2, TOK])
        gate = Ring([sb(f"f2_gate{n}", [P, BANK]) for n in range(3)])
        w1 = w["w1"].rearrange("p (j n) -> p j n", j=DC)
        w2 = w["w2"].rearrange("p (j n) -> p j n", j=DC)
        w3 = w["w3"].rearrange("p (c d) -> p c d", d=D)
        last = {}
        for half in range(TOK // BANK):
            sl = slice(half * BANK, (half + 1) * BANK)
            for c in range(FC2):
                rows = min(P, FFN2 - c * P)
                tb = []
                for wt, nm in ((w1, "w1"), (w2, "w2")):
                    n, bank, freed = k.banks.take()
                    t = k.mm(bank[0:rows, :], [(wt[:, j, c * P:c * P + rows], k.cols[:, j, sl]) for j in range(DC)],
                             [freed, quantised[nm], [r[half] for r in k.cols_ready]])
                    tb.append((n, bank, t))
                ng, gb, gf = gate.take()
                u = k.act([tb[0][2], gf], lambda e, rows=rows, gb=gb, bank=tb[0][1]: e.activation(
                    gb[0:rows, :], bank[0:rows, :], ACT.Sigmoid))
                k.banks.give(tb[0][0], u)
                v = k.dve([u, tb[1][2]], lambda e, rows=rows, gb=gb, bank=tb[1][1], c=c, sl=sl: e.tensor_tensor(
                    hidden[0:rows, c, sl], gb[0:rows, :], bank[0:rows, :], ALU.mult))
                k.banks.give(tb[1][0], v)
                gate.give(ng, v)
                last[half] = v
        out = []
        for i in range(NT):
            n, bank, freed = k.banks.take()
            pairs = [(hidden[0:min(P, FFN2 - c * P), c, i * P:(i + 1) * P], w3[0:min(P, FFN2 - c * P), c, :])
                     for c in range(FC2)]
            t = k.mm(bank[:, 0:D], pairs, [freed, last[i // HALF], quantised["w3"]])
            out.append(k.dve([t], lambda e, i=i, bank=bank: e.tensor_tensor(k.x[:, i, :], k.x[:, i, :], bank[:, 0:D],
                                                                          ALU.add)))
            k.banks.give(n, out[-1])
    return out


def layer3_attention(k, x_ready):
    norm_pass(k, x_ready)
    with ExitStack() as scope:
        sb = lambda name, shape, dt=F32: k.sb(name, shape, dt, scope)
        w, W, c = k.l3, k.l3_in, k.c
        mat = {n: w[n].rearrange("p (j n) -> p j n", j=DC) for n in ("qw", "kw", "vw", "ow")}
        ctx = k.ctxt["ctx"].rearrange("p (j t) -> p j t", j=DC)
        twice = k.ctxt["twice"].rearrange("p (j b t) -> p j b t", j=DC, b=B)
        junk = Ring([sb(f"a3_junk{n}", [P, D]) for n in range(2)])
        ms = sb("a3_ms", [P, 10])
        rms = sb("a3_rms", [P, 10])
        spare = sb("a3_spare", [P, 10])
        qrow = sb("a3_q", [P, 10, D])
        qcol = sb("a3_qt", [P, DC, TOK])
        kcol = sb("a3_kt", [P, DC, CTX])
        kblock = sb("a3_kb", [P, B, DC, 8, SC])
        vblock = sb("a3_vb", [P, B, D])
        ones = c["ones"]

        def linear(lhs, weight, bias, bank_half, after):
            return k.mm(bank_half, [(a, mat[weight][:, j, :]) for j, a in enumerate(lhs)]
                        + [(ones[0:1, :], w[bias][0:1, :])], after)

        kept, squares = [], []
        for i in range(NT + CTX // P):
            n, bank, freed = k.banks.take()
            if i < NT:
                t = linear(tile_cols(k, i), "qw", "qb", bank[:, 0:D], [freed, both(k.cols_ready, i), W])
            else:
                m = i - NT
                t = linear([ctx[:, j, m * P:(m + 1) * P] for j in range(DC)], "kw", "kb", bank[:, 0:D], [freed, W])
            nj, jb, jf = junk.take()
            squares.append(k.act([t, jf, x_ready], lambda e, i=i, jb=jb, bank=bank: e.activation(
                jb[:], bank[:, 0:D], ACT.Square, accum_out=ms[:, i:i + 1])))
            junk.give(nj, squares[-1])
            kept.append(k.copy(k.dve, qrow[:, i, :], bank[:, 0:D], [t, squares[-1]]))
            k.banks.give(n, kept[-1])
        t = k.dve([squares[-1]], lambda e: e.tensor_scalar(ms[:], ms[:], 1.0 / D, 1e-6, ALU.mult, ALU.add))
        t = rsqrt(k, rms[:], ms[:], spare[:], [t])
        scaled = [(k.dve if i % 2 else k.pool)([t, kept[i]], lambda e, i=i: e.tensor_scalar(
            qrow[:, i, :], qrow[:, i, :], rms[:, i:i + 1], 0.0, ALU.mult, ALU.add)) for i in range(10)]
        no_bias = sb("a3_zero", [P, DC])
        z = k.pool([x_ready], lambda e: e.memset(no_bias[:], 0.0))
        q_ready = transpose_rows(k, qrow, qcol, scaled, w["nq"], no_bias[:], free=[z])
        n, bank, freed = k.banks.take()
        t = k.turn([(bank[:, (j * 2 + m) * P:(j * 2 + m + 1) * P], qrow[:, NT + m, j * P:(j + 1) * P])
                    for j in range(DC) for m in range(CTX // P)], [freed, scaled[8:]])
        kk = [k.act([t], lambda e, j=j, bank=bank: e.activation(kcol[:, j, :], bank[:, j * CTX:(j + 1) * CTX], ACT.Copy,
                                                              scale=w["nk"][:, j:j + 1])) for j in range(DC)]
        k.banks.give(n, kk[-1])
        kb_ready = [k.dve([kk], *[lambda e, b=b, j=j: e.tensor_tensor(
            kblock[:, b, j, :, :], under(kcol[:, j, b * SC:(b + 1) * SC], 8), over(c["head16"], SC), ALU.mult)
            for j in range(DC)]) for b in range(B)]
        vb_ready = []
        for b in range(B):
            n, bank, freed = k.banks.take()
            t = linear([twice[:, j, b, :] for j in range(DC)], "vw", "vb", bank[:, 0:D], [freed, W])
            vb_ready.append(k.dve([t], lambda e, b=b, bank=bank: e.tensor_tensor(vblock[:, b, :], bank[:, 0:D],
                                                                              c["pair"], ALU.mult)))
            k.banks.give(n, vb_ready[-1])
        soft = Soft(k, scope)
        orow = Ring([sb(f"a3_o{n}", [P, D]) for n in range(2)])
        ocol = Ring([sb(f"a3_ot{n}", [P, DC, P]) for n in range(2)])
        jobs = [dict() for _ in range(NT)]

        def score(i):
            b, job = i // TPB, jobs[i]
            sbuf = soft.begin(job)
            for j in range(DC):
                n, bank, freed = k.banks.take()
                t = k.mm(bank[:], [(qcol[:, j, i * P:(i + 1) * P], kblock[:, b, j, :, :].rearrange("p h s -> p (h s)"))],
                         [freed, kb_ready[b], both(q_ready, i)])
                u = k.copy(k.act, sbuf[:, j * 8:(j + 1) * 8, :].rearrange("p h s -> p (h s)"), bank[:],
                           [t, job["free"]])
                k.banks.give(n, u)
            soft.shift(job, sbuf, [u])

        def mix(i):
            b, job = i // TPB, jobs[i]
            n, bank, freed = k.banks.take()
            for pr in range(H3 // 2):
                cs = slice(pr * 2 * HD3, (pr + 1) * 2 * HD3)
                t = k.mm(bank[:, cs], [(job["pt"][:, pr, :], vblock[:, b, cs])], [freed, vb_ready[b], job["pt_ready"]])
            soft.end(job, t)
            no, o, of = orow.take()
            u = k.copy(k.dve, o[:], bank[:, 0:D], [t, of])
            t = k.turn([(bank[:, D + j * P:D + (j + 1) * P], o[:, j * P:(j + 1) * P]) for j in range(DC)], [u])
            orow.give(no, t)
            nt, ot, tf = ocol.take()
            u = k.copy(k.act, ot[:].rearrange("p j t -> p (j t)"), bank[:, D:2 * D], [t, tf])
            k.banks.give(n, u)
            job.update(nt=nt, ot=ot, ot_ready=u)

        def out(i):
            job = jobs[i]
            n, bank, freed = k.banks.take()
            t = linear([job["ot"][:, j, :] for j in range(DC)], "ow", "ob", bank[:, 0:D], [freed, job["ot_ready"]])
            ocol.give(job["nt"], t)
            job["x"] = k.dve([t], lambda e: e.tensor_tensor(k.x[:, i, :], k.x[:, i, :], bank[:, 0:D], ALU.add))
            k.banks.give(n, job["x"])

        skew(NT, score, lambda i: soft.power(jobs[i], float(HD3) ** -0.5), lambda i: soft.flip(jobs[i]), mix, out)
    return [job["x"] for job in jobs]


LAYERS = [layer0_attention, layer0_ffn, layer1_attention, layer1_ffn, layer2_attention, layer2_ffn,
          layer3_attention, layer3_ffn]


def build(nc, a, upto=len(LAYERS)):
    with ExitStack() as ctx:
        k = Core(nc, ctx)
        k.x = k.sb("x", [P, NT, D])
        k.rows = k.sb("rows", [P, NT, D])
        k.cols = k.sb("cols", [P, DC, TOK])
        k.moments = Moments(k, NT)
        k.seg_i = k.sb("seg_i", [P, NT], I32)
        k.keys = k.sb("keys", [P, SC])
        const = k.sb("const", [P, width(CONST)])
        ctxt = k.sb("ctxt", [P, width(CTXP)])
        l0 = k.sb("l0_weights", [P, width(L0A)])
        l2 = k.sb("l2_vectors", [P, width(L2A)])
        experts_scope, l1_scope = ExitStack(), ExitStack()
        ctx.callback(experts_scope.close)
        ctx.callback(l1_scope.close)
        k.c, k.ctxt, k.l0, k.l2 = views(const, CONST), views(ctxt, CTXP), views(l0, L0A), views(l2, L2A)

        x_in = k.load("x_in", k.x[:], a["x"])
        k.const_in = k.load("const_in", const[:], a["const"])
        k.l0_in = k.load("l0_in", l0[:], a["l0"])
        k.ctx_in = k.load("ctx_in", ctxt[:], a["ctx"])
        k.expert_dram, k.group_dram = a["experts"], a["groups"]
        open_experts(k, experts_scope, "expert", 0, 1 + E0 + 1 + E1, [])
        l1 = k.sb("l1_weights", [P, width(L1A)], scope=l1_scope)
        k.l1, k.l1_space = views(l1, L1A), l1[:, width(L1A) - (H1 * HD1 + H1 * D):width(L1A)]
        k.seg_in = k.load("seg_in", k.seg_i[:], a["seg"])
        k.l1_in = k.load("l1_in", l1[:], a["l1"])
        k.l2_in = k.load("l2_in", l2[:], a["l2"])
        k.pool.wait([k.const_in])
        keys_ready = k.pool([k.const_in], lambda e: e.iota(k.keys[:], [[1, SC]], base=0, channel_multiplier=0,
                                                           allow_small_or_imprecise_dtypes=True))
        k.dve.wait([keys_ready, k.const_in])
        k.act.wait([k.const_in])
        k.pe.wait([k.const_in])

        ready = [x_in] * NT
        for layer in LAYERS[:upto]:
            ready = layer(k, ready)
            if layer is layer1_attention:
                l1_scope.close()
            if layer is layer1_ffn:
                experts_scope.close()
                l2f = k.sb("l2f_weights", [P, width(L2F)])
                k.l2f = views(l2f, L2F)
                k.l2f_in = k.load("l2f_in", l2f[:], a["l2f"], [ready])
            if layer is layer2_attention:
                l3 = k.sb("l3_weights", [P, width(L3A)])
                k.l3 = views(l3, L3A)
                k.l3_in = k.load("l3_in", l3[:], a["l3"], [ready])
                open_experts(k, ctx, "expert_l3_", 1 + E0 + 1 + E1, a["experts"].shape[0], [ready])
        stored = k.sp.dma([ready], k.arrival("out_stored"), lambda e: e.dma_start(a["out"], k.x[:]))
        k.sp.wait([stored])


def pack(spec, parts):
    out = np.zeros((P, width(spec)), np.float32)
    at = 0
    for name, n in spec:
        v = np.asarray(parts[name])
        v = v.reshape(v.shape[0], -1)
        out[:v.shape[0], at:at + v.shape[1]] = v
        assert v.shape[1] == n, (name, v.shape, n)
        at += n
    return out


def chunks(w):
    w = np.asarray(w)
    return w.reshape(-1, P, w.shape[-1]).transpose(1, 0, 2).reshape(P, -1)


def column(v):
    return np.ascontiguousarray(np.asarray(v).reshape(-1, P).T)


def everywhere(v):
    v = np.asarray(v).reshape(1, -1)
    return np.broadcast_to(v, (P, v.shape[1]))


def expert(gate_t, up_t, down_t):
    gu = np.concatenate([gate_t.reshape(DC, P, I), up_t.reshape(DC, P, I)], axis=2)
    return np.concatenate([gu.transpose(1, 0, 2).reshape(P, -1), down_t], axis=1)


def constants():
    part = np.arange(P)
    half = R1 // 2
    inv_freq = np.float32(1.0) / np.float32(10000.0) ** (np.arange(half, dtype=np.float32) / np.float32(half))

    def tables(n):
        ang = (np.arange(n, dtype=np.float32)[:, None] * inv_freq).astype(np.float32)
        feature = part % R1
        cos, sin = np.cos(ang).T[feature % half], np.sin(ang).T[feature % half]
        return cos.astype(np.float32), (sin * np.where(feature < half, -1.0, 1.0)[:, None]).astype(np.float32)

    cos_q, sin_q = tables(S)
    cos_k, sin_k = tables(SC)
    head = np.arange(D) // HD3
    return pack(CONST, {
        "ident": np.eye(P), "ones": np.ones((P, P)), "before": (part[:, None] < part[None, :]),
        "iota_e": everywhere(np.arange(32)), "iota_c": everywhere(np.arange(CAP)),
        "cos_q": cos_q, "sin_q": sin_q, "cos_k": cos_k, "sin_k": sin_k,
        "head16": (part[:, None] // HD3 == np.arange(8)[None, :]),
        "pair": ((part[:, None] // SC) == (head[None, :] % 2)),
        "slot1": (TOK + 1 + part)[:, None], "tokpart": (part + 1)[:, None]})


def swap_halves(w):
    w = np.asarray(w)
    return w.reshape(w.shape[0], -1, 2, R1 // 2)[:, :, ::-1, :].reshape(w.shape[0], -1)


def lay_out(v):
    v = {n: np.asarray(x) for n, x in v.items()}
    ctx_t = v["ctx_2048"].reshape(CTX, D).T
    by_batch = ctx_t.reshape(D, B, 1, SC)
    twice = np.broadcast_to(by_batch, (D, B, 2, SC)).reshape(D, B * 2 * SC)
    a = {"x": v["x"].reshape(NT, P, D).transpose(1, 0, 2), "const": constants(),
         "ctx": pack(CTXP, {"ctx": chunks(ctx_t), "twice": chunks(twice)}),
         "seg": v["itok_BxS_0_1023"].reshape(NT, P).T}
    g = lambda n: v["L0_xattn_" + n]
    a["l0"] = pack(L0A, {
        "w_in": chunks(g("W_in").T), "w_out": chunks(g("W_out").T), "b_in": column(g("b_in")),
        "b_out": everywhere(g("b_out")), "gamma": everywhere(g("gamma")), "beta": everywhere(g("beta")),
        "decay": everywhere(g("decay")), "gate0": chunks(v["L0_ffn_gate_w"].T), "bias0": everywhere(v["L0_ffn_bias"]),
        "gate1": chunks(v["L1_ffn_gate_w"].T), "gate3": chunks(v["L3_ffn_centroids"].T),
        "bias3": everywhere(v["L3_ffn_gate_bias"])})
    ex = [expert(v["L0_ffn_sg"].T, v["L0_ffn_su"].T, v["L0_ffn_sd"].T)]
    ex += [expert(v["L0_ffn_w_gate"][e].T, v["L0_ffn_w_up"][e].T, v["L0_ffn_w_down"][e].T) for e in range(E0)]
    ex += [expert(v["L1_ffn_sw1"].T, v["L1_ffn_sw3"].T, v["L1_ffn_sw2"].T)]
    ex += [expert(v["L1_ffn_w1"][e].T, v["L1_ffn_w3"][e].T, v["L1_ffn_w2"][e].T) for e in range(E1)]
    ex += [expert(v["L3_ffn_wg_s"][:, s], v["L3_ffn_wu_s"][:, s], v["L3_ffn_wd_s"][s, :])
           for s in (slice(0, I), slice(I, 2 * I))]
    ex += [expert(v["L3_ffn_wg"][e], v["L3_ffn_wu"][e], v["L3_ffn_wd"][e]) for e in range(E3)]
    a["experts"] = np.stack(ex)
    g = lambda n: v["L1_xattn_" + n]
    by_head = lambda w: w.reshape(-1, H1, HD1)
    a["l1"] = pack(L1A, {
        "kvc": chunks(g("W_kvc")), "dq": chunks(g("W_dq")),
        "uq": by_head(g("W_uq")).transpose(2, 1, 0).reshape(P, -1), "qr": g("W_qr"), "qr_swap": swap_halves(g("W_qr")),
        "uk": g("W_uk"), "kr": np.concatenate([g("W_kr")] * 2, axis=1),
        "kr_swap": np.concatenate([swap_halves(g("W_kr"))] * 2, axis=1), "uv": g("W_uv"), "wo": chunks(g("W_o"))})
    g = lambda n: v["L2_xattn_" + n]
    vec = {n: column(g(n)) for n in ("ln_w", "ln_b", "qln_w", "qln_b", "kln_w", "kln_b", "qxln_w", "qxln_b",
                                     "kxln_w", "kxln_b")}
    a["l2"] = pack(L2A, {
        **vec, "q_in": column(g("q_in_scale")), "qx_in": column(g("qx_in_scale")), "k_in": column(g("k_in_scale")),
        "v_in": column(g("v_in_scale")), "wq_s": everywhere(g("wq_scale")), "wqx_s": everywhere(g("wqx_scale")),
        "wk_s": everywhere(g("wk_scale")), "wv_s": everywhere(g("wv_scale")), "p_w": everywhere(g("proj_w_scale")),
        "p_in": everywhere(g("proj_in_scale")), "smooth": column(g("proj_smooth"))})
    kvx = g("w_kv_x")
    proj = g("wproj").T.reshape(2, G2, HPG, P, D)
    a["groups"] = np.stack([pack(L2G, {
        "w": chunks(np.concatenate([
            g("wq")[q * HPG * P:(q + 1) * HPG * P], g("wqx")[q * HPG * P:(q + 1) * HPG * P],
            g("wk")[q * P:(q + 1) * P], g("wv")[q * P:(q + 1) * P], kvx[q * P:(q + 1) * P],
            kvx[(G2 + q) * P:(G2 + q + 1) * P]]).T),
        "proj": proj[:, q].reshape(2 * HPG, P, D).transpose(1, 0, 2)}) for q in range(G2)])
    pad = lambda w: np.concatenate([w, np.zeros((FC2 * P - FFN2, D), np.float32)])
    a["l2f"] = pack(L2F, {"w1": chunks(v["L2_ffn_w1"].T), "w2": chunks(v["L2_ffn_w2"].T),
                          "w3": chunks(pad(v["L2_ffn_w3"].T))})
    g = lambda n: v["L3_xattn_" + n]
    a["l3"] = pack(L3A, {
        "qw": chunks(g("q_w").T), "kw": chunks(g("k_img_w").T), "vw": chunks(g("v_img_w").T), "ow": chunks(g("o_w").T),
        "qb": everywhere(g("q_b")), "kb": everywhere(g("k_img_b")), "vb": everywhere(g("v_img_b")),
        "ob": everywhere(g("o_b")), "nq": column(g("norm_q_w")), "nk": column(g("norm_k_img_w"))})
    return {n: np.ascontiguousarray(x) for n, x in a.items()}


def program(nc, arrays, **options):
    a = {n: nc.dram_tensor(f"in_{n}", x.shape, mybir.dt.from_np(x.dtype), kind="ExternalInput").ap()
         for n, x in arrays.items()}
    a["out"] = nc.dram_tensor("out", [P, NT, D], F32, kind="ExternalOutput").ap()
    build(nc, a, **options)


def kernel(**inputs):
    import concourse.bacc as bacc
    from concourse.bass_utils import run_bass_kernel_spmd

    nc = bacc.Bacc("TRN2", target_bir_lowering=False, num_devices=1)
    arrays = lay_out(inputs)
    program(nc, arrays)
    got = run_bass_kernel_spmd(nc, [{f"in_{n}": x for n, x in arrays.items()}], core_ids=[0])
    return got.results[0]["out"].transpose(1, 0, 2).reshape(B, S, D)
```

```python
from contextlib import ExitStack

import numpy as np

import concourse.bass as bass
from concourse import mybir

F32 = mybir.dt.float32
F32R = mybir.dt.float32r
BF16 = mybir.dt.bfloat16
U32 = mybir.dt.uint32
U16 = mybir.dt.uint16
I32 = mybir.dt.int32
ALU = mybir.AluOpType
ACT = mybir.ActivationFunctionType
AX = mybir.AxisListType

P = 128
B, S, D = 4, 256, 256
TOK = B * S
NT = TOK // P
DC = D // P
SC = 64
CTX = B * SC
TPB = S // P
BANK = 512
HALF = 4

E0, K0, CAP = 32, 6, 96
E1, K1 = 8, 2
E3, K3 = 16, 2
I = 128
UNIT = DC * 2 * I + D
SINK = CAP

H1, HD1, R1, KVC, QC, LOOK = 16, 128, 64, 64, 96, 8
EARLY = 8
NH2, G2, D2 = 16, 8, 128
HPG = NH2 // G2
GW = 8 * P
FFN2 = 704
FC2 = -(-FFN2 // P)
H3, HD3 = 16, 16
NEG = -1e30
ROUND = 1.5 * 2.0 ** 23
FP8_MAX = 448.0


CONST = [("ident", P), ("ones", P), ("before", P), ("iota_e", 32), ("iota_c", CAP), ("cos_q", S), ("sin_q", S),
         ("cos_k", SC), ("sin_k", SC), ("head16", 8), ("pair", D), ("slot1", 1), ("tokpart", 1), ("minus_half", 16)]
CTXP = [("ctx", DC * CTX), ("twice", DC * B * 2 * SC)]
L0A = [("w_in", DC * D), ("w_out", DC * D), ("b_in", DC), ("b_out", D), ("gamma", D), ("beta", D), ("decay", 1),
       ("gate0", DC * E0), ("bias0", E0), ("gate1", DC * E1), ("gate3", DC * E3), ("bias3", E3)]
L1K = [("kvc", DC * KVC), ("uk", H1 * HD1), ("uq", H1 * QC)]
L1V = [("uv", EARLY * HD1), ("wo", EARLY * D)]
L1A = [("dq", DC * QC), ("qr", H1 * R1), ("qr_swap", H1 * R1), ("kr", P), ("kr_swap", P),
       ("uv_late", (H1 - EARLY) * HD1), ("wo_late", (H1 - EARLY) * D)]
L2A = [("ln_w", DC), ("ln_b", DC), ("q_in", DC), ("qx_in", DC), ("k_in", DC), ("v_in", DC),
       ("wq_s", 1), ("wqx_s", 1), ("wk_s", 1), ("wv_s", 1), ("p_w", 1), ("p_in", 1),
       ("qln_w", 1), ("qln_b", 1), ("kln_w", 1), ("kln_b", 1), ("qxln_w", 1), ("qxln_b", 1), ("kxln_w", 1),
       ("kxln_b", 1), ("smooth", 2 * NH2)]
L2G = [("w", DC * GW), ("proj", 2 * HPG * D)]
L2F = [("w1", DC * FFN2), ("w2", DC * FFN2), ("w3", FC2 * D)]
L3C = [("kw", DC * D), ("vw", DC * D), ("kb", D), ("vb", D), ("nk", DC)]
L3A = [("qw", DC * D), ("ow", DC * D), ("qb", D), ("ob", D), ("nq", DC)]


def width(spec):
    return sum(n for _, n in spec)


def views(tile, spec, at=0):
    out = {}
    for name, n in spec:
        out[name] = tile[:, at:at + n]
        at += n
    return out


class Line:

    def __init__(self, engine, sem):
        self.engine, self.sem, self.count, self.met = engine, sem, 0, {}

    def wait(self, ticks):
        for t in ticks:
            if t is None:
                continue
            if isinstance(t, list):
                self.wait(t)
                continue
            sem, value = t
            if self.met.get(id(sem), 0) < value:
                self.met[id(sem)] = value
                self.engine.wait_ge(sem, value)

    def __call__(self, after, *steps):
        self.wait(after)
        for step in steps:
            last = step(self.engine)
        last.then_inc(self.sem, 1)
        self.count += 1
        return (self.sem, self.count)

    def dma(self, after, arrival, step):
        self.wait(after)
        step(self.engine).then_inc(arrival.sem, 16)
        arrival.count += 16
        return (arrival.sem, arrival.count)


class Arrival:

    def __init__(self, sem):
        self.sem, self.count = sem, 0


class Ring:

    def __init__(self, buffers, after=()):
        self.buffers, self.free, self.idle = buffers, [list(after) for _ in buffers], list(range(len(buffers)))

    def take(self):
        n = self.idle.pop(0)
        return n, self.buffers[n], self.free[n]

    def give(self, n, *ticks):
        self.free[n] = list(ticks)
        self.idle.append(n)


def skew(n, *stages, oldest_first=False):
    for r in range(n + len(stages) - 1):
        for k, stage in sorted(enumerate(stages), reverse=oldest_first, key=lambda pair: pair[0]):
            if 0 <= r - k < n:
                stage(r - k)


def over(ap, n):
    return ap.unsqueeze(2).broadcast_to([ap.shape[0], ap.shape[1], n])


def under(ap, n):
    return ap.unsqueeze(1).broadcast_to([ap.shape[0], n, ap.shape[1]])


class Core:

    def __init__(self, nc, ctx):
        self.nc, self.ctx = nc, ctx
        self.pe, self.dve, self.act, self.pool, self.sp = (
            Line(engine, ctx.enter_context(nc.semaphore(name))) for engine, name in (
                (nc.tensor, "matmul_done"), (nc.vector, "vector_done"), (nc.scalar, "scalar_done"),
                (nc.gpsimd, "pool_done"), (nc.sync, "sync_done")))
        self.banks = Ring([ctx.enter_context(nc.psum_tensor(f"bank{n}", [P, BANK], F32)) for n in range(8)])
        self.named = {}

    def sb(self, name, shape, dt=F32, scope=None):
        self.named[name] = self.named.get(name, 0) + 1
        if self.named[name] > 1:
            name += f"_{self.named[name]}"
        return (scope or self.ctx).enter_context(self.nc.sbuf_tensor(name, shape, dt))

    def arrival(self, name):
        return Arrival(self.ctx.enter_context(self.nc.semaphore(name)))

    def load(self, name, dst, src, after=()):
        return self.sp.dma(after, self.arrival(name), lambda e: e.dma_start(dst, src))

    def mm(self, out, pairs, after, start=True, stop=True, shared=False):
        builds = []
        for n, (lhs, rhs) in enumerate(pairs):
            builds.append(lambda e, a=lhs, b=rhs, s=start and n == 0, t=stop and n == len(pairs) - 1:
                          e.matmul(out, a, b, start=s, stop=t, skip_group_check=shared))
        return self.pe(after, *builds)

    def turn(self, jobs, after):
        ident = self.c["ident"]
        return self.pe(after, *[lambda e, o=o, i=i: e.transpose(o, i, ident[0:i.shape[0], 0:i.shape[0]])
                                for o, i in jobs])

    def copy(self, line, out, src, after):
        if line is self.act:
            return line(after, lambda e: e.activation(out, src, ACT.Copy))
        return line(after, lambda e: e.tensor_copy(out, src))


def rsqrt(k, out, v, spare, after):
    bits = out.bitcast(I32)
    t = k.dve(after, lambda e: e.tensor_scalar(bits, v.bitcast(I32), 1, None, ALU.logical_shift_right))
    t = k.dve([t], lambda e: e.tensor_scalar(bits, bits, -1, 0x5F3759DF, ALU.mult, ALU.add))
    for _ in range(3):
        t = k.dve([t], lambda e: e.scalar_tensor_tensor(spare, out, -0.5, v, ALU.mult, ALU.mult))
        t = k.dve([t], lambda e: e.tensor_tensor(spare, spare, out, ALU.mult))
        t = k.dve([t], lambda e: e.scalar_tensor_tensor(out, spare, 1.5, out, ALU.add, ALU.mult))
    return t


class Moments:

    def __init__(self, k, n, scope=None):
        self.stats = k.sb("stats", [P, n, 6], scope=scope)
        self.mv = k.sb("mean_var", [P, n, 2], scope=scope)
        self.minus, self.var, self.rstd, self.shift = (
            k.sb(name, [P, n], scope=scope) for name in ("minus_mean", "var", "rstd", "shift"))
        self.free = []


def moments(k, src, m, eps, after):
    n = len(src)
    for i in range(n):
        t = k.dve([after[i], m.free], lambda e, i=i: e.bn_stats(m.stats[:, i, :], src[i]))
    t = k.dve([t], *[lambda e, i=i: e.bn_aggr(m.mv[:, i, :], m.stats[:, i, :]) for i in range(n)])
    var, rstd, minus = m.var[:, 0:n], m.rstd[:, 0:n], m.minus[:, 0:n]
    t = k.dve([t], lambda e: e.tensor_scalar(var, m.mv[:, 0:n, 1], eps, None, ALU.add))
    u = k.dve([], lambda e: e.tensor_scalar(minus, m.mv[:, 0:n, 0], -1.0, None, ALU.mult))
    t = k.pool([t], lambda e: e.tensor_tensor(rstd, var, k.c["minus_half"][:, 0:n], ALU.pow))
    return [u, t], k.pool([u, t], lambda e: e.tensor_tensor(m.shift[:, 0:n], minus, rstd, ALU.mult))


def normalise(k, src, out, after, eps=1e-5, scalar_engine=True):
    halves = []
    for half, m in enumerate(k.moments):
        tiles = range(half * HALF, (half + 1) * HALF)
        halves.append(moments(k, [src[:, i, :] for i in tiles], m, eps, [after[i] for i in tiles]))
    ticks = []
    for (t, shifted), m in zip(halves, k.moments):
        done = []
        for c in range(HALF):
            i = len(ticks)
            if c == 1 and scalar_engine:
                ticks.append(k.act([shifted], lambda e: e.activation(
                    out[:, i, :], src[:, i, :], ACT.Identity, bias=m.shift[:, c:c + 1], scale=m.rstd[:, c:c + 1])))
            else:
                ticks.append((k.pool if c == 2 else k.dve)([t], lambda e: e.tensor_scalar(
                    out[:, i, :], src[:, i, :], m.minus[:, c:c + 1], m.rstd[:, c:c + 1], ALU.add, ALU.mult)))
            done.append(ticks[-1])
        m.free = done
    return ticks


def transpose_rows(k, rows, cols, ready, scale=None, bias=None, free=()):
    ticks = [[None, None] for _ in range(DC)]
    for half in range(NT // HALF):
        for j in range(DC):
            n, bank, freed = k.banks.take()
            t = k.turn([(bank[:, i * P:(i + 1) * P], rows[:, half * HALF + i, j * P:(j + 1) * P])
                        for i in range(HALF)], [freed, ready[half * HALF:(half + 1) * HALF]])
            dst = cols[:, j, half * BANK:(half + 1) * BANK]
            if scale is None:
                u = k.copy(k.act if j else k.dve, dst, bank[:], [t, *free])
            else:
                u = k.act([t, *free], lambda e, j=j, dst=dst, bank=bank: e.activation(
                    dst, bank[:], ACT.Identity, bias=bias[:, j:j + 1], scale=scale[:, j:j + 1]))
            k.banks.give(n, u)
            ticks[j][half] = u
    return ticks


def split(k, src, high, low, kept, after, line=None):
    t = k.dve(after, lambda e: e.tensor_scalar(kept.bitcast(I32), src.bitcast(I32), 12, 12, ALU.logical_shift_right,
                                               ALU.logical_shift_left))
    u = k.dve([t], lambda e: e.tensor_copy(high, kept))
    return u, (line or k.pool)([t], lambda e: e.tensor_tensor(low, src, kept, ALU.subtract))


class Split:

    def __init__(self, k, scope):
        kept = Ring([k.sb(f"cols_kept{n}", [P, BANK], scope=scope) for n in range(2)])
        self.high, self.low = (k.sb(f"cols_{part}", [P, DC, TOK], F32R, scope) for part in ("high", "low"))
        self.ready = [[None] * (TOK // BANK) for _ in range(DC)]
        for half in range(TOK // BANK):
            for j in range(DC):
                n, buf, freed = kept.take()
                cs = slice(half * BANK, (half + 1) * BANK)
                self.ready[j][half] = list(split(k, k.cols[:, j, cs], self.high[:, j, cs], self.low[:, j, cs], buf[:],
                                                 [k.cols_ready[j][half], freed], k.pool if half else k.dve))
                kept.give(n, *self.ready[j][half])

    def at(self, half):
        return [self.ready[j][half] for j in range(DC)]


def three(a, b):
    (ah, al), (bh, bl) = a, b
    return [(ah, bh), (ah, bl), (al, bh)]


def both(ticks, tile):
    return [t[tile // HALF] for t in ticks]


def norm_pass(k, x_ready):
    k.rows_ready = normalise(k, k.x, k.rows, x_ready)
    k.cols_ready = transpose_rows(k, k.rows, k.cols, k.rows_ready)


def tile_cols(k, t, cols=None):
    cols = cols if cols is not None else k.cols
    return [cols[:, j, t * P:(t + 1) * P] for j in range(DC)]


def layer0_attention(k, x_ready):
    with ExitStack() as scope:
        w = k.l0
        seq = k.sb("l0_seq", [P, DC, CTX], scope=scope)
        states = k.sb("l0_states", [P, DC, CTX], scope=scope)
        keep = k.sb("l0_keep", [P, 1], scope=scope)
        keeps = k.sb("l0_keeps", [P, SC], scope=scope)
        mean_state = k.sb("l0_mean_state", [P, DC, B], scope=scope)
        mean_wide = k.sb("l0_mean_wide", [P, DC * B, P], scope=scope)
        y = k.sb("l0_y", [P, NT, D], scope=scope)
        k.rows_ready = normalise(k, k.x, k.rows, x_ready)
        t = k.act([k.l0_in], lambda e: e.activation(keep[:], w["decay"], ACT.Sigmoid))
        kept = k.dve([t, k.const_in], lambda e: e.tensor_scalar(keeps[:], k.c["ones"][:, 0:SC], keep[:, 0:1], None,
                                                                ALU.mult))
        n, bank, freed = k.banks.take()
        w_in = w["w_in"].rearrange("p (j e) -> p j e", j=DC)
        ctx = k.ctxt["ctx"].rearrange("p (j t) -> p j t", j=DC)
        for i in range(DC):
            t = k.mm(bank[:, i * CTX:(i + 1) * CTX], [(w_in[:, j, i * P:(i + 1) * P], ctx[:, j, :])
                                                      for j in range(DC)], [freed, k.l0_in, k.ctx_in])
        ticks = []
        for i in range(DC):
            ticks.append(k.act([t], lambda e, i=i: e.activation(seq[:, i, :], bank[:, i * CTX:(i + 1) * CTX],
                                                                ACT.Identity, bias=w["b_in"][:, i:i + 1])))
        k.banks.give(n, *ticks)
        for i in range(DC):
            for b in range(B):
                t = k.dve([ticks[i], kept], lambda e, i=i, b=b: e.tensor_tensor_scan(
                    states[:, i, b * SC:(b + 1) * SC], keeps[:], seq[:, i, b * SC:(b + 1) * SC], 0.0, ALU.mult,
                    ALU.add))
        t = k.dve([t], lambda e: e.tensor_reduce(
            mean_state[:].rearrange("p j b -> p (j b)"), states[:].rearrange("p j (b t) -> p (j b) t", b=B), AX.X,
            ALU.add))
        t = k.dve([t], lambda e: e.tensor_scalar(
            mean_wide[:], over(mean_state[:].rearrange("p j b -> p (j b)"), P), 1.0 / SC, None, ALU.mult))
        w_out = w["w_out"].rearrange("p (j e) -> p j e", j=DC)
        wide = t
        added = []
        for b in range(B):
            n, bank, freed = k.banks.take()
            t = k.mm(bank[:, 0:D], [(mean_wide[:, j * B + b, :], w_out[:, j, :]) for j in range(DC)]
                     + [(k.c["ones"][0:1, :], w["b_out"][0:1, :])], [freed, wide, k.l0_in])
            for i in range(b * TPB, (b + 1) * TPB):
                t2 = k.dve([t, k.rows_ready[i]], lambda e, i=i, bank=bank: e.tensor_tensor(
                    y[:, i, :], k.rows[:, i, :], bank[:, 0:D], ALU.add))
                added.append(t2)
            k.banks.give(n, t2)
        layer1_keys(k, scope)
        done = normalise(k, y, y, added, scalar_engine=False)
        out = []
        for i in range(NT):
            line = k.pool if i % 3 == 2 else k.dve
            t = line([done[i]], lambda e, i=i: e.tensor_tensor(y[:, i, :], y[:, i, :], w["gamma"], ALU.mult))
            t = line([t], lambda e, i=i: e.tensor_tensor(y[:, i, :], y[:, i, :], w["beta"], ALU.add))
            out.append(k.dve([t], lambda e, i=i: e.tensor_tensor(k.x[:, i, :], k.x[:, i, :], y[:, i, :], ALU.add)))
        layer1_values(k, scope, 0, k.l1v["uv"], k.l1v["wo"], k.l1v_in, [k.act, k.act])
    return out


def expert_weights(k, slot):
    return slot[:, 0:DC * 2 * I].rearrange("p (j n) -> p j n", j=DC), slot[:, DC * 2 * I:UNIT]


def open_experts(k, slots, name, first, end, after):
    k.experts, k.expert_arrival = Ring(slots, after), [k.arrival(f"{name}{n}_in") for n in range(len(slots))]
    k.fetched, k.next_expert, k.last_expert = {}, first, end
    for _ in slots:
        fetch_expert(k)


def fetch_expert(k):
    if k.next_expert < k.last_expert:
        n, slot, freed = k.experts.take()
        src = k.expert_dram[k.next_expert]
        k.fetched[k.next_expert] = (n, slot, k.sp.dma(freed, k.expert_arrival[n], lambda q: q.dma_start(slot[:], src)))
        k.next_expert += 1


def use_expert(k, e):
    return k.fetched.pop(e)


def drop_expert(k, n, *ticks):
    k.experts.give(n, *ticks)
    fetch_expert(k)


def routing(k, scope, n_exp, top, biased, biased_ready):
    best = k.sb("route_best", [P, NT, 8], scope=scope)
    where = k.sb("route_where", [P, NT, 8], U32, scope=scope)
    where_f = k.sb("route_where_f", [P, NT, 8], scope=scope)
    hits = k.sb("route_hits", [P, NT, top, n_exp], scope=scope)
    mask = k.sb("route_mask", [P, NT, n_exp], scope=scope)
    t = k.dve([biased_ready], *[lambda e, i=i: e.max(best[:, i, :], biased[:, i, :]) for i in range(NT)])
    t = k.dve([t], *[lambda e, i=i: e.max_index(where[:, i, :], best[:, i, :], biased[:, i, :]) for i in range(NT)])
    t = k.dve([t], lambda e: e.tensor_copy(where_f[:], where[:]))
    yield None
    t = k.dve([t], *[lambda e, i=i: e.tensor_tensor(
        hits[:, i, :, :], over(where_f[:, i, 0:top], n_exp), under(k.c["iota_e"][:, 0:n_exp], top), ALU.is_equal)
        for i in range(NT)])
    t = k.dve([t], lambda e: e.tensor_reduce(mask[:], hits[:].rearrange("p t k e -> p t e k"), AX.X, ALU.add))
    yield mask, t


def gate_logits(k, gate, n_exp, logits, ready):
    n, bank, freed = k.banks.take()
    gate = gate.rearrange("p (j e) -> p j e", j=DC)
    for i in range(NT):
        t = k.mm(bank[:, i * n_exp:(i + 1) * n_exp], [(c, gate[:, j, :]) for j, c in enumerate(tile_cols(k, i))],
                 [freed, both(ready, i), k.l0_in])
    u = k.copy(k.dve, logits[:].rearrange("p t e -> p (t e)"), bank[:, 0:NT * n_exp], [t])
    k.banks.give(n, u)
    return u


class Swiglu:

    def __init__(self, k, scope, depth=3):
        self.k = k
        self.gated = Ring([k.sb(f"swi_gated{n}", [P, I], scope=scope) for n in range(depth)])
        self.inner = Ring([k.sb(f"swi_inner{n}", [P, I], scope=scope) for n in range(depth)])
        self.turned = Ring([k.sb(f"swi_turned{n}", [P, I], scope=scope) for n in range(depth)])

    def open(self, job):
        k, m = self.k, job["m"]
        gu, _ = expert_weights(k, job["slot"])
        nb, bank, freed = k.banks.take()
        t = k.mm(bank[0:m, 0:2 * I], [(c, gu[:, j, :]) for j, c in enumerate(job["cols"])], [freed, job["after"]])
        ng, gated, gfree = self.gated.take()
        t1 = k.act([t, gfree, job.get("s_ready")], lambda e, s=job["s"]: e.activation(
            gated[0:m, :], bank[0:m, 0:I], ACT.Silu, scale=s))
        job.update(nb=nb, bank=bank, ng=ng, gated=gated, gated_ready=t1, gu_done=t)

    def combine(self, job):
        k, m, bank, gated = self.k, job["m"], job["bank"], job["gated"]
        ni, inner, ifree = self.inner.take()
        t = k.dve([job["gated_ready"], ifree, job.get("s_ready")], lambda e: e.scalar_tensor_tensor(
            inner[0:m, :], bank[0:m, I:2 * I], job["w"], gated[0:m, :], ALU.mult, ALU.mult))
        self.gated.give(job["ng"], t)
        if job.get("clip"):
            t = k.dve([t], lambda e, c=job["clip"]: e.tensor_scalar(inner[0:m, :], inner[0:m, :], c, -c, ALU.min,
                                                                    ALU.max))
        job.update(ni=ni, inner=inner, inner_ready=t)

    def flip(self, job):
        k, m, bank = self.k, job["m"], job["bank"]
        t = k.turn([(bank[:, 2 * I:2 * I + m], job["inner"][0:m, :])], [job["inner_ready"]])
        self.inner.give(job["ni"], t)
        nt, turned, tfree = self.turned.take()
        u = k.copy(k.act if job.get("evac") == "act" else k.dve, turned[:, 0:m], bank[:, 2 * I:2 * I + m], [t, tfree])
        k.banks.give(job["nb"], u)
        job.update(nt=nt, turned=turned, turned_ready=u)

    def close(self, job, out, after, start, stop, shared=False):
        k, m = self.k, job["m"]
        _, down = expert_weights(k, job["slot"])
        t = k.mm(out, [(job["turned"][:, 0:m], down)], [job["turned_ready"], after], start, stop, shared)
        self.turned.give(job["nt"], t)
        return t


def layer0_ffn(k, x_ready):
    norm_pass(k, x_ready)
    for line in (k.dve, k.act, k.pool, k.sp):
        line.wait([k.kq_ready[-1], k.vo_ready[-1]])
    nc = k.nc
    with ExitStack() as scope:
        sb = lambda name, shape, dt=F32: k.sb(name, shape, dt, scope)
        n_rows = TOK + SINK
        h_rows = nc.dram_tensor("h_rows", [n_rows, D], F32, kind="Internal").ap()
        sums = [nc.dram_tensor(f"sum{n}", [n_rows, D], F32, kind="Internal").ap() for n in range(2)]
        tiled = lambda dram: dram[0:TOK, :].rearrange("(t p) d -> p t d", p=P)
        zeros = sb("f0_zeros", [SINK, D])
        shared = sb("f0_shared", [P, NT, D])
        t = k.pool([], lambda e: e.memset(zeros[:], 0.0))
        rows_out = k.arrival("h_rows_out")
        k.sp.dma([k.rows_ready], rows_out, lambda e: e.dma_start(tiled(h_rows), k.rows[:]))
        k.sp.dma([t], rows_out, lambda e: e.dma_start(h_rows[TOK:n_rows, :], zeros[:]))
        rows_stored = (rows_out.sem, rows_out.count)
        sum_out = [k.arrival(f"sum{n}_out") for n in range(2)]
        k.sp.dma([x_ready], sum_out[0], lambda e: e.dma_start(tiled(sums[0]), k.x[:]))
        k.sp.dma([t], sum_out[0], lambda e: e.dma_start(sums[0][TOK:n_rows, :], zeros[:]))
        k.sp.dma([t], sum_out[1], lambda e: e.dma_start(sums[1][TOK:n_rows, :], zeros[:]))

        logits = sb("f0_logits", [P, NT, E0])
        size = sb("f0_size", [P, NT, E0])
        small = sb("f0_small", [P, NT, E0])
        one_plus = sb("f0_one_plus", [P, NT, E0])
        log1p = sb("f0_log1p", [P, NT, E0])
        flat = sb("f0_flat", [P, NT, E0])
        scores = sb("f0_scores", [P, NT, E0])
        biased = sb("f0_biased", [P, NT, E0])
        lg = gate_logits(k, k.l0["gate0"], E0, logits, k.cols_ready)
        t = k.act([lg], lambda e: e.activation(size[:], logits[:], ACT.Abs))
        z = k.act([t], lambda e: e.activation(small[:], size[:], ACT.Exp, scale=-1.0))
        t = k.dve([z], lambda e: e.tensor_scalar(one_plus[:], small[:], 1.0, None, ALU.add))
        ln = k.act([t], lambda e: e.activation(log1p[:], one_plus[:], ACT.Ln))
        t = k.dve([t, ln], lambda e: e.tensor_scalar(one_plus[:], one_plus[:], 1.0, None, ALU.subtract))
        t = k.dve([t], lambda e: e.tensor_scalar(flat[:], one_plus[:], 0.0, None, ALU.is_equal))
        t = k.dve([t], lambda e: e.tensor_tensor(one_plus[:], one_plus[:], flat[:], ALU.add))
        t = k.dve([t], lambda e: e.reciprocal(one_plus[:], one_plus[:]))
        t = k.dve([t], lambda e: e.tensor_tensor(log1p[:], log1p[:], one_plus[:], ALU.mult))
        t = k.dve([t], lambda e: e.tensor_tensor(log1p[:], log1p[:], flat[:], ALU.add))
        t = k.dve([t], lambda e: e.tensor_tensor(log1p[:], log1p[:], small[:], ALU.mult))
        t = k.dve([t], lambda e: e.scalar_tensor_tensor(log1p[:], logits[:], 0.0, log1p[:], ALU.max, ALU.add))
        flat_t = lambda a: a[:].rearrange("p t e -> p (t e)")
        t = k.dve([t], lambda e: e.tensor_scalar(small[:], log1p[:], 2.0 ** -126, None, ALU.max))
        t = rsqrt(k, flat_t(scores), flat_t(small), flat_t(flat), [t])
        t = k.dve([t], lambda e: e.tensor_tensor(scores[:], scores[:], log1p[:], ALU.mult))
        t = k.dve([t], lambda e: e.tensor_tensor(biased[:], scores[:], under(k.l0["bias0"], NT), ALU.add))
        *_, (mask, t) = routing(k, scope, E0, K0, biased, t)

        layer1_values(k, scope, EARLY, k.l1["uv_late"], k.l1["wo_late"], k.l1_in, [k.act, k.act])

        weight = sb("f0_weight", [P, NT, E0])
        total = sb("f0_total", [P, NT])
        w = k.dve([t], lambda e: e.tensor_tensor(weight[:], mask[:], scores[:], ALU.mult))
        w = k.dve([w], lambda e: e.tensor_reduce(total[:], weight[:], AX.X, ALU.add))
        w = k.dve([w], lambda e: e.reciprocal(total[:], total[:]))
        w = k.dve([w], lambda e: e.tensor_scalar(total[:], total[:], 1.5, None, ALU.mult))
        w = k.dve([w], lambda e: e.tensor_tensor(weight[:], weight[:], over(total[:], E0), ALU.mult))

        before = sb("f0_before", [P, NT, E0])
        b = k.pool([], lambda e: e.memset(before[:, 0, :], 0.0))
        for i in range(1, NT):
            b = k.dve([t, b], lambda e, i=i: e.tensor_tensor(before[:, i, :], before[:, i - 1, :], mask[:, i - 1, :],
                                                             ALU.add))
        n, bank, freed = k.banks.take()
        for i in range(NT):
            q = k.mm(bank[:, i * E0:(i + 1) * E0], [(k.c["before"], mask[:, i, :]), (k.c["ones"], before[:, i, :])],
                     [freed, b, t])
        place = sb("f0_place", [P, NT, E0])
        u = k.dve([t], lambda e: e.tensor_scalar(place[:], mask[:], -999.0, 999.0, ALU.mult, ALU.add))
        u = k.dve([u, q], lambda e: e.tensor_tensor(place[:].rearrange("p t e -> p (t e)"),
                                                    place[:].rearrange("p t e -> p (t e)"), bank[:, 0:NT * E0],
                                                    ALU.add))
        k.banks.give(n, u)

        facts = sb("f0_facts", [P, NT, E0, 5], BF16)
        rest = sb("f0_rest", [P, NT, E0])
        f = k.pool([k.const_in], *[lambda e, i=i: e.memset(facts[:, i, :, 1], float(i * P)) for i in range(NT)])
        f = k.dve([w, f], lambda e: e.tensor_scalar(
            facts[:, :, :, 0].rearrange("p t e -> p (t e)"), weight[:].rearrange("p t e -> p (t e)"), 0.0,
            k.c["tokpart"], ALU.mult, ALU.add))
        f = k.dve([f], lambda e: e.tensor_copy(facts[:, :, :, 2], weight[:]))
        f = k.dve([f], lambda e: e.tensor_tensor(rest[:], weight[:], facts[:, :, :, 2], ALU.subtract))
        f = k.dve([f], lambda e: e.tensor_copy(facts[:, :, :, 3], rest[:]))
        f = k.dve([f], lambda e: e.tensor_tensor(rest[:], rest[:], facts[:, :, :, 3], ALU.subtract))
        f = k.dve([f], lambda e: e.tensor_copy(facts[:, :, :, 4], rest[:]))

        picks = Ring([sb(f"f0_pick{n}", [P, E0, CAP], BF16) for n in range(2)])
        table_number, tbank, tfree = k.banks.take()
        picked = []

        def pick_tokens(i):
            n, pick, freed = picks.take()
            t = k.dve([u, freed], lambda e: e.tensor_tensor(
                pick[:], over(place[:, i, :], CAP), under(k.c["iota_c"], E0), ALU.is_equal))
            picked.append(k.pe([t, f, tfree], *[lambda e, x=x: e.matmul(
                tbank[0:CAP, x * 5:(x + 1) * 5], pick[:, x, :], facts[:, i, x, :], start=(i == 0 and x == 0),
                stop=(i == NT - 1), skip_group_check=True) for x in range(E0)]))
            picks.give(n, picked[-1])

        swi = Swiglu(k, scope)
        n, slot, came = use_expert(k, 0)
        jobs = [dict(cols=tile_cols(k, i), m=P, slot=slot, s=1.0, w=1.0, clip=10.0, evac="act",
                     after=[came, *both(k.cols_ready, i)]) for i in range(NT)]
        outs = {}

        def finish_shared(i):
            if i % 2 == 0:
                outs[i] = k.banks.take()
            nb, bank, freed = outs[i - i % 2]
            half = bank[:, (i % 2) * D:(i % 2 + 1) * D]
            t = swi.close(jobs[i], half, freed, True, True)
            if i % 2:
                outs["mm"] = t
                outs["t"] = k.copy(k.act, shared[:, i - 1:i + 1, :], bank[:].rearrange("p (t d) -> p t d", t=2), [t])
                k.banks.give(nb, outs["t"])

        for r in range(NT + 2):
            if r < NT:
                swi.open(jobs[r])
            if 0 <= r - 1 < NT:
                swi.flip(jobs[r - 1])
            if r >= 2:
                finish_shared(r - 2)
            if r < NT:
                pick_tokens(r)
                swi.combine(jobs[r])
        drop_expert(k, n, outs["mm"])
        k.sp.dma([outs["t"]], sum_out[1], lambda e: e.dma_start(tiled(sums[1]), shared[:]))
        stored = [(s.sem, s.count) for s in sum_out]
        t2 = picked[-1]
        table = sb("f0_table", [CAP, E0, 5])
        number = sb("f0_number", [CAP, E0])
        empty = sb("f0_empty", [CAP, E0])
        index = sb("f0_index", [CAP, E0], U32)
        slot_w = sb("f0_slot_w", [CAP, E0])
        t = k.dve([t2], lambda e: e.tensor_copy(table[:].rearrange("p e f -> p (e f)"), tbank[0:CAP, 0:E0 * 5]))
        k.banks.give(table_number, t)
        t1 = k.dve([t], lambda e: e.tensor_tensor(number[:], table[:, :, 0], table[:, :, 1], ALU.add))
        t1 = k.dve([t1], lambda e: e.tensor_scalar(empty[:], number[:], 0.0, k.c["slot1"][0:CAP, :], ALU.is_equal,
                                                   ALU.mult))
        t1 = k.dve([t1], lambda e: e.scalar_tensor_tensor(number[:], number[:], -1.0, empty[:], ALU.add, ALU.add))
        indexed = k.dve([t1], lambda e: e.tensor_copy(index[:], number[:]))
        t1 = k.dve([t], lambda e: e.tensor_tensor(slot_w[:], table[:, :, 2], table[:, :, 3], ALU.add))
        weighed = k.dve([t1], lambda e: e.tensor_tensor(slot_w[:], slot_w[:], table[:, :, 4], ALU.add))


        depth = 4
        got = Ring([sb(f"f0_got{n}", [CAP, D]) for n in range(depth)])
        got_arrival = [k.arrival(f"f0_got{n}_in") for n in range(depth)]
        tcols = Ring([sb(f"f0_cols{n}", [P, DC, CAP]) for n in range(3)])
        ys = Ring([sb(f"f0_ys{n}", [CAP, D]) for n in range(depth)])
        added = [k.arrival(f"f0_added{n}") for n in range(2)]
        jobs = [dict(m=CAP, evac="act") for _ in range(E0)]

        def gather(x):
            n, buf, freed = got.take()
            jobs[x].update(ng=n, got=buf, came=k.pool.dma(
                [freed, indexed, rows_stored], got_arrival[n], lambda e: e.indirect_dma_start(
                    buf[:], None, h_rows, bass.IndirectOffsetOnAxis(ap=index[:, x:x + 1], axis=0))))

        def flip_in(x):
            job = jobs[x]
            nb, bank, freed = k.banks.take()
            t = k.turn([(bank[:, j * P:j * P + CAP], job["got"][:, j * P:(j + 1) * P]) for j in range(DC)],
                       [freed, job["came"]])
            got.give(job["ng"], t)
            nc_, cols, cfree = tcols.take()
            u = k.copy(k.dve, cols[:], bank[:, 0:DC * P].rearrange("p (j n) -> p j n", j=DC)[:, :, 0:CAP], [t, cfree])
            k.banks.give(nb, u)
            ns, slot, arrived = use_expert(k, 1 + x)
            job.update(nc=nc_, cols=[cols[:, j, :] for j in range(DC)], ns=ns, slot=slot, after=[arrived, u],
                       s=1.0, w=slot_w[:, x:x + 1], s_ready=weighed)

        def first(x):
            swi.open(jobs[x])
            swi.combine(jobs[x])
            tcols.give(jobs[x]["nc"], jobs[x]["gu_done"])

        def add_back(x):
            job = jobs[x]
            nb, bank, freed = k.banks.take()
            t = swi.close(job, bank[0:CAP, 0:D], freed, True, True)
            drop_expert(k, job["ns"], t)
            ny, y, yfree = ys.take()
            u = k.copy(k.act, y[:], bank[0:CAP, 0:D], [t, yfree])
            k.banks.give(nb, u)
            a = added[x % 2]
            tick = k.pool.dma([u, stored[x % 2], (a.sem, a.count) if a.count else None, indexed], a,
                              lambda e: e.indirect_dma_start(
                sums[x % 2], bass.IndirectOffsetOnAxis(ap=index[:, x:x + 1], axis=0), y[:], None,
                compute_op=ALU.add))
            ys.give(ny, tick)

        skew(E0, gather, lambda x: None, flip_in, first, lambda x: swi.flip(jobs[x]), add_back)
        back = k.arrival("sums_in")
        every = [(a.sem, a.count) for a in added]
        k.sp.dma([every, x_ready], back, lambda e: e.dma_start(k.x[:], tiled(sums[0])))
        k.sp.dma([], back, lambda e: e.dma_start(shared[:], tiled(sums[1])))
        done = (back.sem, back.count)
        out = [(k.dve if i % 2 else k.pool)([done], lambda e, i=i: e.tensor_tensor(
            k.x[:, i, :], k.x[:, i, :], shared[:, i, :], ALU.add)) for i in range(NT)]
    return out


def layer1_keys(k, scope):
    w = k.l1k
    scale = float(1.0 / np.sqrt(np.float32(HD1 + R1)))
    ctx = k.ctxt["ctx"].rearrange("p (j t) -> p j t", j=DC)
    knope = Ring([k.sb(f"a1_knope{n}", [P, CTX], scope=scope) for n in range(3)])
    n, bank, freed = k.banks.take()
    t = k.mm(bank[0:KVC, 0:CTX], [(w["kvc"].rearrange("p (j n) -> p j n", j=DC)[:, j, :], ctx[:, j, :])
                                  for j in range(DC)], [freed, k.l1k_in, k.ctx_in])
    k.kvc_ready = k.copy(k.act, k.kvc[:], bank[0:KVC, 0:CTX], [t])
    k.banks.give(n, k.kvc_ready)
    uk = w["uk"][0:KVC, :].rearrange("p (h d) -> p h d", h=H1)
    uq = w["uq"].rearrange("p (h d) -> p h d", h=H1)
    heads = [dict() for _ in range(H1)]
    k.kq_ready = []

    def project(h):
        n, bank, freed = k.banks.take()
        t = k.mm(bank[:, 0:CTX], [(uk[:, h, :], k.kvc[:])], [freed, k.kvc_ready])
        nk, buf, free = knope.take()
        u = k.copy(k.act, buf[:], bank[:, 0:CTX], [t, free])
        k.banks.give(n, u)
        heads[h].update(nk=nk, buf=buf, ready=u)

    def fold(h):
        d = heads[h]
        n, bank, freed = k.banks.take()
        t = k.mm(bank[0:QC, 0:CTX], [(uq[:, h, :], d["buf"][:])], [freed, d["ready"]])
        knope.give(d["nk"], t)
        k.kq_ready.append(k.act([t], lambda e: e.activation(
            k.kq[:, :, h, :], bank[0:QC, 0:CTX].rearrange("p (b s) -> p b s", b=B), ACT.Copy, scale=scale)))
        k.banks.give(n, k.kq_ready[-1])

    skew(H1, project, lambda h: None, fold)


def layer1_values(k, scope, first, uv, wo, weights_in, lines):
    uv = uv[0:KVC, :].rearrange("p (h d) -> p h d", d=HD1)
    wo = wo.rearrange("p (h d) -> p h d", d=D)
    vhead = Ring([k.sb(f"a1_vhead{n}", [P, CTX], scope=scope) for n in range(3)])
    heads = [dict() for _ in range(uv.shape[1])]

    def project(i):
        n, bank, freed = k.banks.take()
        t = k.mm(bank[:, 0:CTX], [(uv[:, i, :], k.kvc[:])], [freed, k.kvc_ready, weights_in])
        nv, buf, free = vhead.take()
        u = k.copy(lines[i % 2], buf[:], bank[:, 0:CTX], [t, free])
        k.banks.give(n, u)
        heads[i].update(nv=nv, buf=buf, ready=u)

    def times_wo(i):
        d, h = heads[i], first + i
        lo = (h % 2) * SC
        for pair in range(B // 2):
            n, bank, freed = k.banks.take()
            for b in range(2):
                bb = pair * 2 + b
                t = k.mm(bank[lo:lo + SC, b * D:(b + 1) * D], [(d["buf"][:, bb * SC:(bb + 1) * SC], wo[:, i, :])],
                         [freed, d["ready"]])
            k.vo_ready.append(k.copy(lines[pair], k.vo[lo:lo + SC, pair * 2:pair * 2 + 2, h // 2, :],
                                     bank[lo:lo + SC, :].rearrange("p (b d) -> p b d", b=2), [t]))
            k.banks.give(n, k.vo_ready[-1])
        vhead.give(d["nv"], t)

    skew(len(heads), project, times_wo)


def layer1_attention(k, x_ready):
    norm_pass(k, x_ready)
    with ExitStack() as scope:
        sb = lambda name, shape, dt=F32: k.sb(name, shape, dt, scope)
        w, c, W = k.l1, k.c, k.l1_in
        scale = float(1.0 / np.sqrt(np.float32(HD1 + R1)))
        qc = sb("a1_qc", [QC, TOK])
        dq = w["dq"].rearrange("p (j n) -> p j n", j=DC)
        qc_ready = []
        for half in range(TOK // BANK):
            n, bank, freed = k.banks.take()
            sl = slice(half * BANK, (half + 1) * BANK)
            t = k.mm(bank[0:QC, :], [(dq[:, j, :], k.cols[:, j, sl]) for j in range(DC)],
                     [freed, W, [r[half] for r in k.cols_ready]])
            qc_ready.append(k.copy(k.dve, qc[:, sl], bank[0:QC, :], [t]))
            k.banks.give(n, qc_ready[-1])
        key_blocks = sb("a1_key_blocks", [P, B, 2 * SC])
        turn_a = sb("a1_turn_a", [P, CTX])
        turn_b = sb("a1_turn_b", [P, CTX])
        n, bank, freed = k.banks.take()
        t = k.mm(bank[:, 0:CTX], [(w["kr"][0:KVC, :], k.kvc[:])], [freed, W, k.kvc_ready])
        t = k.mm(bank[:, CTX:2 * CTX], [(w["kr_swap"][0:KVC, :], k.kvc[:])], [])
        by_b = lambda ap: ap.rearrange("p (b s) -> p b s", b=B)
        u1 = k.dve([t, x_ready], lambda e: e.tensor_tensor(by_b(turn_a[:]), by_b(bank[:, 0:CTX]),
                                                           under(c["cos_k"], B), ALU.mult))
        u2 = k.dve([t], lambda e: e.tensor_tensor(by_b(turn_b[:]), by_b(bank[:, CTX:2 * CTX]),
                                                  under(c["sin_k"], B), ALU.mult))
        k.banks.give(n, u2)
        z = k.pool([x_ready], lambda e: e.memset(key_blocks[:], 0.0))
        u = k.dve([u1, u2], lambda e: e.tensor_tensor(turn_a[:], turn_a[:], turn_b[:], ALU.add))
        blocks_ready = k.dve([u, z], *[lambda e, h=h: e.tensor_scalar(
            key_blocks[h * R1:(h + 1) * R1, :, h * SC:(h + 1) * SC], by_b(turn_a[h * R1:(h + 1) * R1, :]), scale, None,
            ALU.mult) for h in range(2)])
        kq, vo, kq_ready, vo_ready = k.kq, k.vo, k.kq_ready, k.vo_ready
        qrot = sb("a1_qrot", [P, H1 // 2, BANK])
        part = Ring([sb(f"a1_part{n}", [P, BANK]) for n in range(3)])
        qr = w["qr"][0:QC, :].rearrange("p (h d) -> p h d", d=P)
        qrs = w["qr_swap"][0:QC, :].rearrange("p (h d) -> p h d", d=P)
        qrot_ready = [[None] * (H1 // 2) for _ in range(2)]
        by_s = lambda ap: ap.rearrange("p (b s) -> p b s", s=S)

        def rotate(half, free):
            sl = slice(half * BANK, (half + 1) * BANK)
            for pr in range(H1 // 2):
                ticks = []
                for src, tab, dst in ((qr, "cos_q", None), (qrs, "sin_q", part)):
                    n, bank, freed = k.banks.take()
                    t = k.mm(bank[:], [(src[:, pr, :], qc[:, sl])], [freed, W, qc_ready[half]])
                    if dst is None:
                        o, pf = qrot[:, pr, :], free
                    else:
                        npart, pbuf, pf = part.take()
                        o = pbuf[:]
                    ticks.append(k.dve([t, pf], lambda e, o=o, bank=bank, tab=tab: e.tensor_tensor(
                        by_s(o), by_s(bank[:]), under(c[tab], 2), ALU.mult)))
                    k.banks.give(n, ticks[-1])
                t = k.pool(ticks, lambda e: e.tensor_tensor(qrot[:, pr, :], qrot[:, pr, :], pbuf[:], ALU.add))
                part.give(npart, t)
                qrot_ready[half][pr] = t
        seg = sb("a1_seg", [P, NT])
        block = sb("a1_block", [P, NT, SC])
        under_seg = sb("a1_under", [P, NT, SC])
        t = k.dve([k.seg_in, x_ready], lambda e: e.tensor_copy(seg[:], k.seg_i[:]))
        keys = under(k.keys[:], NT)
        t1 = k.dve([t, k.const_in], lambda e: e.tensor_tensor(block[:], keys, over(seg[:], SC), ALU.is_le))
        t2 = k.dve([t1], lambda e: e.tensor_scalar(seg[:], seg[:], float(LOOK), None, ALU.subtract))
        t2 = k.dve([t2], lambda e: e.tensor_tensor(under_seg[:], keys, over(seg[:], SC), ALU.is_ge))
        t = k.dve([t1, t2], lambda e: e.tensor_tensor(block[:], block[:], under_seg[:], ALU.mult))
        block_ready = k.dve([t], lambda e: e.tensor_scalar(block[:], block[:], -1.0, -NEG, ALU.add, ALU.mult))

        soft = Soft(k, scope)
        jobs = [dict() for _ in range(NT)]

        def score(i):
            b, job = i // TPB, jobs[i]
            sbuf = soft.begin(job)
            for hb in range(2):
                n, bank, freed = k.banks.take()
                hs = slice(hb * 8, hb * 8 + 8)
                t = k.mm(bank[:], [(qc[:, i * P:(i + 1) * P], kq[:, b, hs, :].rearrange("p h s -> p (h s)"))],
                         [freed, qc_ready, kq_ready], stop=False, shared=True)
                for pr in range(4):
                    t = k.mm(bank[:, pr * P:(pr + 1) * P], [(qrot[:, hb * 4 + pr, (i % HALF) * P:(i % HALF + 1) * P],
                                                             key_blocks[:, b, :])],
                             [blocks_ready, qrot_ready[i // HALF][hb * 4 + pr]], start=False, stop=(pr == 3),
                             shared=True)
                u = k.dve([t, block_ready, job["free"]], lambda e, bank=bank, hs=hs: e.tensor_tensor(
                    sbuf[:, hs, :], bank[:].rearrange("p (h s) -> p h s", h=8), under(block[:, i, :], 8), ALU.add))
                k.banks.give(n, u)
            job["scored"] = t
            soft.shift(job, sbuf, [u])

        def out(i):
            b, job = i // TPB, jobs[i]
            n, bank, freed = k.banks.take()
            t = k.mm(bank[:, 0:D], [(job["pt"][:, pr, :], vo[:, b, pr, :]) for pr in range(H1 // 2)],
                     [freed, vo_ready, job["pt_ready"]])
            soft.end(job, t)
            job["x"] = k.dve([t], lambda e: e.tensor_tensor(k.x[:, i, :], k.x[:, i, :], bank[:, 0:D], ALU.add))
            k.banks.give(n, job["x"])

        rotate(0, [])

        def score_or_rotate(i):
            score(i)
            if i == HALF - 1:
                rotate(1, [jobs[i]["scored"]])

        skew(NT, score_or_rotate, lambda i: soft.power(jobs[i], 1.0), lambda i: soft.flip(jobs[i]), out,
             oldest_first=True)
    return [job["x"] for job in jobs]


class Soft:

    def __init__(self, k, scope, depth=3):
        self.k, heads = k, 16
        self.s = Ring([k.sb(f"soft_s{n}", [P, heads, SC], scope=scope)[:] for n in range(depth)])
        self.pt = Ring([k.sb(f"soft_pt{n}", [P, heads // 2, P], scope=scope)[:] for n in range(2)])
        self.top = Ring([k.sb(f"soft_top{n}", [P, heads], scope=scope) for n in range(depth)])
        self.sum = Ring([k.sb(f"soft_sum{n}", [P, heads], scope=scope) for n in range(depth)])

    def begin(self, job):
        job["ns"], job["s"], free = self.s.take()
        job["free"] = list(free)
        return job["s"]

    def shift(self, job, src, after):
        k, s = self.k, job["s"]
        nt, top, tf = self.top.take()
        t = k.dve([after, tf], lambda e: e.tensor_reduce(top[:], src, AX.X, ALU.max))
        job["shifted"] = k.pool([t], lambda e: e.tensor_tensor(s, src, over(top[:], SC), ALU.subtract))
        self.top.give(nt, job["shifted"])

    def power(self, job, scale, divide=True):
        k, s = self.k, job["s"]
        nm, total, mf = self.sum.take()
        t = k.act([job["shifted"]], lambda e: e.activation(s, s, ACT.Exp, scale=scale))
        u = k.dve([t, mf], lambda e: e.tensor_reduce(total[:], s, AX.X, ALU.add))
        u = k.dve([u], lambda e: e.reciprocal(total[:], total[:]))
        if divide:
            job["probs"] = k.pool([u], lambda e: e.tensor_tensor(s, s, over(total[:], SC), ALU.mult))
            self.sum.give(nm, job["probs"])
        else:
            job.update(probs=t, nm=nm, one_over=total, one_over_ready=u)

    def flip(self, job):
        k, s = self.k, job["s"]
        npt, pt, pf = self.pt.take()
        job.update(npt=npt, pt=pt, pt_ready=[])
        for hb in range(2):
            n, bank, freed = k.banks.take()
            t = k.turn([(bank[:, pr * P:(pr + 1) * P],
                         s[:, 2 * (hb * 4 + pr):2 * (hb * 4 + pr) + 2, :].rearrange("p h s -> p (h s)"))
                        for pr in range(4)], [freed, job["probs"]])
            u = k.copy(k.act, pt[:, hb * 4:hb * 4 + 4, :].rearrange("p a b -> p (a b)"), bank[:], [t, pf])
            k.banks.give(n, u)
            job["pt_ready"].append(u)
        self.s.give(job["ns"], t)

    def end(self, job, tick):
        self.pt.give(job["npt"], tick)


def dense_experts(k, scope, first, shared, routed, share, route, scale_input, x_ready):
    sb = lambda name, shape, dt=F32: k.sb(name, shape, dt, scope)
    parts = sb("dense_parts", [P, NT, 2, routed])
    rows = sb("dense_rows", [2 * routed, TOK], F32R)
    which = sb("dense_which", [2 * routed, routed])
    chooses = sb("dense_chooses", [2 * routed, routed, P], F32R)
    chosen, rows_ready = [], []

    def make_rows():
        *_, (weights, ready) = route
        t = k.dve([ready], lambda e: e.tensor_scalar(
            parts[:, :, 0, :].bitcast(I32), weights.bitcast(I32), 12, 12, ALU.logical_shift_right,
            ALU.logical_shift_left))
        t = k.dve([t], lambda e: e.tensor_tensor(parts[:, :, 1, :], weights, parts[:, :, 0, :], ALU.subtract))
        for half in range(TOK // BANK):
            n, bank, freed = k.banks.take()
            u = k.turn([(bank[0:2 * routed, i * P:(i + 1) * P],
                         parts[:, half * HALF + i, :, :].rearrange("p a e -> p (a e)")) for i in range(HALF)],
                       [freed, t])
            rows_ready.append(k.act([u], lambda e, half=half, bank=bank: e.activation(
                rows[:, half * BANK:(half + 1) * BANK], bank[0:2 * routed, :], ACT.Copy)))
            k.banks.give(n, rows_ready[-1])
        ident = k.c["ident"]
        t = k.pool([ready], lambda e: e.tensor_tensor(which[:], ident[0:2 * routed, 0:routed],
                                                      ident[0:2 * routed, routed:2 * routed], ALU.add))
        chosen.append(k.act([t], lambda e: e.activation(chooses[:], over(which[:], P), ACT.Copy)))

    count, halves = shared + routed, TOK // BANK
    wparts = Ring([[sb(f"dense_w_{part}{n}", [P, UNIT], F32R) for part in ("high", "low")] for n in range(3)])
    kept = Ring([sb(f"dense_kept{n}", [P, UNIT]) for n in range(2)])
    token_w = Ring([sb(f"dense_token_w{n}", [P, TOK]) for n in range(2)])
    gated = Ring([sb(f"dense_gated{n}", [P, BANK]) for n in range(3)])
    inner = Ring([sb(f"dense_inner{n}", [P, BANK]) for n in range(2)])
    inner_kept = Ring([sb(f"dense_inner_kept{n}", [P, BANK]) for n in range(2)])
    iparts = Ring([[sb(f"dense_inner_{part}{n}", [P, BANK], F32R) for part in ("high", "low")] for n in range(3)])
    acc = []
    experts = [dict() for _ in range(count)]
    steps = [dict(e=e, half=half) for e in range(count) for half in range(halves)]

    def prepare(e):
        ex = experts[e]
        n, slot, came = use_expert(k, first + e)
        nw, (high, low), wf = wparts.take()
        nk, buf, kf = kept.take()
        u = split(k, slot[:], high[:], low[:], buf[:], [came, wf, kf, x_ready])
        kept.give(nk, *u)
        drop_expert(k, n, *u)
        ex.update(nw=nw, high=expert_weights(k, high), low=expert_weights(k, low), ready=list(u), token_w_ready=[])

    def spread(e):
        if not rows_ready:
            make_rows()
        ex = experts[e]
        ex["nt"], ex["token_w"], tf = token_w.take()
        for half in range(halves):
            nb, bank, freed = k.banks.take()
            cs = slice(half * BANK, (half + 1) * BANK)
            t = k.mm(bank[:], [(chooses[:, e - shared, :], rows[:, cs])], [freed, chosen, rows_ready[half]])
            ex["token_w_ready"].append(k.copy(k.act, ex["token_w"][:, cs], bank[:], [t, tf]))
            k.banks.give(nb, ex["token_w_ready"][-1])

    def open_(n):
        step = steps[n]
        e, half = step["e"], step["half"]
        ex = experts[e]
        cs = slice(half * BANK, (half + 1) * BANK)
        (hgu, _), (lgu, _) = ex["high"], ex["low"]
        banks = []
        for part in range(2):
            nb, bank, freed = k.banks.take()
            fs = slice(part * I, (part + 1) * I)
            pairs = [pair for j in range(DC) for pair in three((hgu[:, j, fs], lgu[:, j, fs]),
                                                              (cols.high[:, j, cs], cols.low[:, j, cs]))]
            banks.append((nb, bank, k.mm(bank[:], pairs, [freed, ex["ready"], cols.at(half)])))
        (ng, gbank, tg), (nu, ubank, tu) = banks
        n1, g, gf = gated.take()
        if e >= shared:
            tw, tw_ready = ex["token_w"][:, cs], ex["token_w_ready"][half]
        if e >= shared and scale_input:
            t = k.dve([tg, gf, tw_ready], lambda q: q.tensor_tensor(g[:], gbank[:], tw, ALU.mult))
            k.banks.give(ng, t)
            t = k.act([t], lambda q: q.activation(g[:], g[:], ACT.Silu))
        else:
            t = k.act([tg, gf], lambda q: q.activation(g[:], gbank[:], ACT.Silu))
            k.banks.give(ng, t)
        n2, m, mf = inner.take()
        factor = share if e < shared else 1.0
        t = k.dve([t, tu, mf], lambda q: q.scalar_tensor_tensor(m[:], ubank[:], factor, g[:], ALU.mult, ALU.mult))
        k.banks.give(nu, t)
        gated.give(n1, t)
        if e >= shared:
            t = k.dve([t, tw_ready], lambda q: q.tensor_tensor(m[:], m[:], tw, ALU.mult))
            if half == halves - 1:
                token_w.give(ex["nt"], t)
        n3, kb, kf = inner_kept.take()
        step["ni"], step["inner"], fr = iparts.take()
        step["inner_ready"] = list(split(k, m[:], step["inner"][0][:], step["inner"][1][:], kb[:], [t, kf, fr]))
        inner_kept.give(n3, *step["inner_ready"])
        inner.give(n2, *step["inner_ready"])
        if e + 1 < count:
            if half == 0:
                prepare(e + 1)
            elif e + 1 >= shared:
                spread(e + 1)
        if n < min(2, halves * shared - 1):
            next(route)

    def close(n):
        step = steps[n]
        e, half = step["e"], step["half"]
        ex = experts[e]
        (_, hd), (_, ld) = ex["high"], ex["low"]
        for i in range(half * HALF, (half + 1) * HALF):
            _, bank, freed = acc[i // 2]
            ts = slice((i % HALF) * P, (i % HALF + 1) * P)
            t = k.mm(bank[:, (i % 2) * D:(i % 2 + 1) * D], three([a[:, ts] for a in step["inner"]], (hd, ld)),
                     [freed, step["inner_ready"]], e == 0 and i % 2 == 0, e == count - 1, shared=True)
            step[i] = t
        iparts.give(step["ni"], t)
        if half == halves - 1:
            wparts.give(ex["nw"], t)

    prepare(0)
    norm_pass(k, x_ready)
    next(route)
    cols = Split(k, scope)
    acc += [k.banks.take() for _ in range(NT // 2)]
    skew(len(steps), open_, lambda n: None, close)
    out = []
    for i in range(NT):
        n, bank, _ = acc[i // 2]
        t = steps[-halves + i // HALF][i | 1]
        out.append(k.dve([t], lambda e, i=i, bank=bank: e.tensor_tensor(
            k.x[:, i, :], k.x[:, i, :], bank[:, (i % 2) * D:(i % 2 + 1) * D], ALU.add)))
        if i % 2:
            k.banks.give(n, out[-1])
    return out


def sigmoid_exact(k, out, src, after):
    t = k.dve(after, lambda e: e.tensor_scalar(out[:], src[:], -88.0, None, ALU.max))
    t = k.act([t], lambda e: e.activation(out[:], out[:], ACT.Exp, scale=-1.0))
    t = k.dve([t], lambda e: e.tensor_scalar(out[:], out[:], 1.0, None, ALU.add))
    return k.dve([t], lambda e: e.reciprocal(out[:], out[:]))


def layer1_ffn(k, x_ready):
    with ExitStack() as scope:
        sb = lambda name, shape, dt=F32: k.sb(name, shape, dt, scope)
        logits = sb("f1_logits", [P, NT, E1])
        scores = sb("f1_scores", [P, NT, E1])

        def route():
            lg = gate_logits(k, k.l0["gate1"], E1, logits, k.cols_ready)
            t = sigmoid_exact(k, scores, logits, [lg])
            yield None
            for got in routing(k, scope, E1, K1, scores, t):
                yield None
            mask, t = got
            yield scores[:], k.dve([t], lambda e: e.tensor_tensor(scores[:], scores[:], mask[:], ALU.mult))

        return dense_experts(k, scope, 1 + E0, 1, E1, 1.0, route(), True, x_ready)


def layer3_ffn(k, x_ready):
    with ExitStack() as scope:
        sb = lambda name, shape, dt=F32: k.sb(name, shape, dt, scope)
        logits = sb("f3_logits", [P, NT, E3])
        affinity = sb("f3_affinity", [P, NT, E3])
        biased = sb("f3_biased", [P, NT, E3])
        total = sb("f3_total", [P, NT])

        def route():
            lg = gate_logits(k, k.l0["gate3"], E3, logits, k.cols_ready)
            t = sigmoid_exact(k, affinity, logits, [lg])
            yield None
            t = k.dve([t], lambda e: e.tensor_tensor(biased[:], affinity[:], under(k.l0["bias3"], NT), ALU.add))
            for got in routing(k, scope, E3, K3, biased, t):
                yield None
            mask, t = got
            t = k.dve([t], lambda e: e.tensor_tensor(mask[:], affinity[:], mask[:], ALU.mult))
            t = k.dve([t], lambda e: e.tensor_reduce(total[:], mask[:], AX.X, ALU.add))
            t = k.dve([t], lambda e: e.tensor_scalar(total[:], total[:], 1e-9, None, ALU.add))
            t = k.dve([t], lambda e: e.reciprocal(total[:], total[:]))
            yield mask[:], k.dve([t], lambda e: e.tensor_tensor(mask[:], mask[:], over(total[:], E3), ALU.mult))

        return dense_experts(k, scope, 1 + E0 + 1 + E1, 2, E3, 0.1, route(), False, x_ready)


def fp8_steps(k, y, m, after):
    t = k.dve(after, lambda e: e.tensor_scalar(y, y, FP8_MAX, -FP8_MAX, ALU.min, ALU.max))
    t = k.dve([t], lambda e: e.tensor_scalar(m.bitcast(U16), y.bitcast(U16), 0x7F80, None, ALU.bitwise_and))
    return k.dve([t], lambda e: e.tensor_scalar(m, m, 2.0 ** -6, 1.5 * 2.0 ** 20, ALU.max, ALU.mult))


def fp8_round(line, y, m, wide, out, after, free):
    t = line([after, free], lambda e: e.tensor_tensor(wide, y, m, ALU.add))
    return line([t], lambda e: e.tensor_tensor(out, wide, m, ALU.subtract))


def layer2_attention(k, x_ready):
    with ExitStack() as scope:
        sb = lambda name, shape, dt=F32: k.sb(name, shape, dt, scope)
        w, W = k.l2, k.l2_in
        raw_w = sb("a2_raw_w", [P, DC, GW])
        raw_p = sb("a2_raw_proj", [P, 2 * HPG * D])
        raw_w_arrival, raw_p_arrival = k.arrival("a2_raw_w_in"), k.arrival("a2_raw_proj_in")
        w_in, p_in = {}, {}

        def load_w(g, *after):
            if g < G2:
                w_in[g] = k.sp.dma(after, raw_w_arrival, lambda e: e.dma_start(
                    raw_w[:], k.group_dram[g][:, 0:DC * GW].rearrange("p (j n) -> p j n", j=DC)))

        def load_p(g, *after):
            if g < G2:
                p_in[g] = k.sp.dma(after, raw_p_arrival, lambda e: e.dma_start(raw_p[:], k.group_dram[g][:, DC * GW:]))

        load_w(0, x_ready)
        load_p(0)
        again = normalise(k, k.rows, k.rows, normalise(k, k.x, k.rows, x_ready))
        ln, acc = k.cols, k.rows
        ln_ready = transpose_rows(k, k.rows, ln, again, w["ln_w"], w["ln_b"], free=[W, x_ready])
        names = ("q", "qx", "k", "v")
        cols_of = {"q": slice(0, HPG * P), "qx": slice(HPG * P, 2 * HPG * P),
                   "k": slice(2 * HPG * P, (2 * HPG + 1) * P), "v": slice((2 * HPG + 1) * P, (2 * HPG + 2) * P)}
        own_w = (2 * HPG + 2) * P
        scaled = {n: sb(f"a2_in_{n}", [P, DC, TOK], F32R) for n in names}
        inv = sb("a2_inv", [P, 4, DC])
        fold = sb("a2_fold", [P, 4, DC])
        early = scope.enter_context(ExitStack())
        y = Ring([k.sb(f"a2_y{n}", [P, TOK], BF16, early) for n in range(4)])
        m = Ring([k.sb(f"a2_m{n}", [P, TOK], BF16, early) for n in range(4)])
        wide = Ring([k.sb(f"a2_wide{n}", [P, TOK], F32, early) for n in range(4)])
        in_ready, folded, jobs = {}, {}, []
        for q, name in enumerate(names):
            ti = k.dve([W, x_ready], lambda e, q=q, name=name: e.reciprocal(inv[:, q, :], w[f"{name}_in"]))
            folded[name] = k.dve([W], lambda e, q=q, name=name: e.tensor_scalar(
                fold[:, q, :], w[f"{name}_in"], w[f"w{name}_s"], None, ALU.mult))
            jobs += [dict(q=q, name=name, j=j, inv=ti) for j in range(DC)]

        def scale_down(n):
            job = jobs[n]
            ny, yb, yf = y.take()
            nm, mb, mf = m.take()
            t = k.act([job["inv"], ln_ready[job["j"]], yf], lambda e: e.activation(
                yb[:], ln[:, job["j"], :], ACT.Copy, scale=inv[:, job["q"], job["j"]:job["j"] + 1]))
            job.update(ny=ny, y=yb, nm=nm, m=mb, steps=fp8_steps(k, yb[:], mb[:], [t, mf]))

        def round_down(n):
            job = jobs[n]
            nw, wb, wf = wide.take()
            t = fp8_round(k.pool if n % 2 == 0 else k.dve, job["y"][:], job["m"][:], wb[:],
                          scaled[job["name"]][:, job["j"], :], job["steps"], wf)
            y.give(job["ny"], t)
            m.give(job["nm"], t)
            wide.give(nw, t)
            in_ready.setdefault(job["name"], []).append(t)

        skew(len(jobs), scale_down, round_down)
        early.close()
        used = list(in_ready.values())
        wparts = Ring([[sb(f"a2_w_{part}{n}", [P, DC, own_w], F32R) for part in ("high", "low")] for n in range(2)],
                      used)
        pparts = Ring([[sb(f"a2_proj_{part}{n}", [P, 2 * HPG, D], F32R) for part in ("high", "low")]
                       for n in range(2)], used)
        kept = Ring([sb(f"a2_kept{n}", [P, BANK]) for n in range(2)], used)
        ismooth = sb("a2_ismooth", [P, 2 * NH2])
        pscale = sb("a2_pscale", [P, 1])
        sm = k.dve([W, used], lambda e: e.reciprocal(ismooth[:], w["smooth"]))
        ps = k.dve([W, used], lambda e: e.tensor_tensor(pscale[:], w["p_in"], w["p_w"], ALU.mult))
        ctx = k.ctxt["ctx"].rearrange("p (j t) -> p j t", j=DC)
        twice = k.ctxt["twice"].rearrange("p (j b t) -> p j b t", j=DC, b=B)
        softscale = float(1.0 / np.sqrt(D2))

        qn = Ring([sb("a2_qn", [P, TPB, 5, P])], used)
        qt = Ring([sb(f"a2_qt{n}", [P, 2 * HPG, S]) for n in range(2)], used)
        kt = Ring([sb(f"a2_kt{n}", [P, S]) for n in range(2)], used)
        vs = Ring([sb(f"a2_vs{n}", [P, TPB, D2]) for n in range(5)], used)
        kx = Ring([sb(f"a2_kx{n}", [P, CTX]) for n in range(2)], used)
        kxn = Ring([sb("a2_kxn", [P, CTX // P, D2])], used)
        vx = Ring([sb(f"a2_vx{n}", [P, B, D2]) for n in range(2)], used)
        stats_q, stats_qk, stats_kx = (Moments(k, n, scope) for n in (2 * HPG, 2 * HPG + TPB, CTX // P))
        n_own, n_all = HPG * S, HPG * (S + SC)
        probs = Ring([sb("a2_p", [P, TPB, n_all])], used)
        own = lambda p: p[:, 0:n_own].rearrange("p (h s) -> p h s", h=HPG)
        cross = lambda p: p[:, n_own:n_all].rearrange("p (h s) -> p h s", h=HPG)
        top = Ring([sb(f"a2_top{n}", [P, 2 * TPB * HPG]) for n in range(2)], used)
        tot = Ring([sb(f"a2_tot{n}", [P, 2 * TPB * HPG]) for n in range(2)], used)
        pt = Ring([k.cols[:, n, :].rearrange("p (h c t) -> p h c t", h=HPG, c=TPB) for n in range(2)], used)
        px = Ring([sb(f"a2_px{n}", [P, S]) for n in range(2)], used)
        cat = Ring([sb("a2_cat", [P, 2 * HPG * S], BF16)], used)
        catm = Ring([sb("a2_catm", [P, 2 * HPG * S], BF16)], used)
        catw = Ring([sb("a2_catw", [P, 2 * HPG * S])], used)
        catq = Ring([sb(f"a2_catq{n}", [P, 2 * HPG, S], F32R) for n in range(2)], used)
        acc_ready = [k.pool([ln_ready], lambda e, i=i: e.memset(acc[:, i, :], 0.0)) for i in range(NT)]
        units = [dict(g=g, b=b) for g in range(G2) for b in range(B)]
        groups = {}

        def split_pieces(pieces):
            ready = []
            for src, high, low, after in pieces:
                nk, kb, kf = kept.take()
                u = split(k, src, high, low, kb[:, 0:src.shape[1]], [after, kf])
                kept.give(nk, *u)
                ready += u
            return ready

        def split_w(g, j):
            if j == 0:
                gr = groups[g] = dict(came=w_in[g], w_ready=[])
                gr["nw"], gr["wparts"], gr["w_free"] = wparts.take()
            gr = groups[g]
            high, low = gr["wparts"]
            ready = [k.act([gr["came"], folded[name]], lambda e, q=q, cs=cols_of[name]: e.activation(
                raw_w[:, j, cs], raw_w[:, j, cs], ACT.Copy, scale=fold[:, q, j:j + 1]))
                for q, name in enumerate(names)]
            gr["w_ready"] += split_pieces([(raw_w[:, j, cs], high[:, j, cs], low[:, j, cs], [ready[-1], gr["w_free"]])
                                           for cs in (slice(0, 2 * HPG * P), slice(2 * HPG * P, own_w))])

        def split_p(g):
            gr = groups[g]
            gr["np"], (high, low), free = pparts.take()
            gr["pparts"] = (high, low)
            flat = lambda a: a[:].rearrange("p c d -> p (c d)")
            gr["p_ready"] = split_pieces([(raw_p[:, a:a + BANK], flat(high)[:, a:a + BANK], flat(low)[:, a:a + BANK],
                                           [p_in[g], free]) for a in range(0, 2 * HPG * D, BANK)])
            load_p(g + 1, gr["p_ready"])

        def group_context(g):
            gr = groups[g]
            came = gr["came"]
            at = own_w
            nb, bank, freed = k.banks.take()
            for i in range(CTX // P):
                t = k.mm(bank[:, i * P:(i + 1) * P], [(ctx[:, j, i * P:(i + 1) * P], raw_w[:, j, at:at + P])
                                                      for j in range(DC)], [freed, came])
            for b in range(B):
                if b == 0:
                    n2, bank2, freed = k.banks.take()
                t2 = k.mm(bank2[:, b * P:(b + 1) * P], [(twice[:, j, b, :], raw_w[:, j, at + P:at + 2 * P])
                                                        for j in range(DC)], [freed, came])
            nn, kn, kf = kxn.take()
            t = k.copy(k.act, kn[:].rearrange("p t d -> p (t d)"), bank[:, 0:CTX], [t, kf])
            k.banks.give(nb, t)
            t, shifted = moments(k, [kn[:, i, :] for i in range(CTX // P)], stats_kx, 1e-5, [t] * (CTX // P))
            t = k.pool([t], *[lambda e, i=i: e.tensor_scalar(
                kn[:, i, :], kn[:, i, :], stats_kx.minus[:, i:i + 1], stats_kx.rstd[:, i:i + 1], ALU.add, ALU.mult)
                for i in range(CTX // P)])
            stats_kx.free = [t]
            nv, vb, vf = vx.take()
            gr["vx_ready"] = k.copy(k.act, vb[:].rearrange("p b d -> p (b d)"), bank2[:], [t2, vf])
            k.banks.give(n2, gr["vx_ready"])
            gr.update(nv=nv, vx=vb, nn=nn, kn=kn, kn_ready=t)
            load_w(g + 1, t2, gr["w_ready"])

        def group_keys(g):
            gr = groups[g]
            nb, bank, freed = k.banks.take()
            t = k.turn([(bank[:, i * P:(i + 1) * P], gr["kn"][:, i, :]) for i in range(CTX // P)],
                       [freed, gr["kn_ready"]])
            kxn.give(gr["nn"], t)
            nk, kb, kf = kx.take()
            gr["kx_ready"] = k.act([t, kf], lambda e: e.activation(
                kb[:], bank[:, 0:CTX], ACT.Identity, bias=w["kxln_b"], scale=w["kxln_w"]))
            k.banks.give(nb, gr["kx_ready"])
            gr.update(nk=nk, kx=kb)

        pending = []

        def weigh_pending():
            while pending:
                pending.pop()()

        def project(n):
            un = units[n]
            g, b = un["g"], un["b"]
            if n == 0:
                for j in range(DC):
                    split_w(0, j)
                group_context(0)
            gr = groups[g]
            nv, v, vf = vs.take()
            toks = [slice((b * TPB + ti) * P, (b * TPB + ti + 1) * P) for ti in range(TPB)]

            def product(out, name, ti, freed, shared):
                cs = cols_of[name]
                return k.mm(out, [(scaled[name][:, j, toks[ti]], part[:, j, cs]) for j in range(DC)
                                  for part in gr["wparts"]], [freed, in_ready[name], gr["w_ready"]])

            qbanks = []
            for ti in range(TPB):
                nb, bank, freed = k.banks.take()
                for a, name in ((0, "q"), (HPG * P, "qx")):
                    t = product(bank[:, a:a + HPG * P], name, ti, freed, True)
                qbanks.append((nb, bank, t))
            kv, kvbank, freed = k.banks.take()
            for ti in range(TPB):
                tv = product(kvbank[:, S + ti * P:S + (ti + 1) * P], "v", ti, freed, True)
            for ti in range(TPB):
                tk = product(kvbank[:, ti * P:(ti + 1) * P], "k", ti, [], True)
            if b == B - 1:
                wparts.give(gr["nw"], tk)
            un["v_ready"] = k.copy(k.act, v[:].rearrange("p t d -> p (t d)"), kvbank[:, S:2 * S], [tk, vf])
            nn, q_n, nf = qn.take()
            heads = lambda bank: [bank[:, c * P:(c + 1) * P] for c in range(2 * HPG)]
            (_, bank0, t0), (_, bank1, t1) = qbanks
            dst0 = [q_n[:, 0, c, :] for c in range(2 * HPG)]
            srcs1 = heads(bank1) + [kvbank[:, ti * P:(ti + 1) * P] for ti in range(TPB)]
            dst1 = [q_n[:, 1, c, :] for c in range(2 * HPG)] + [q_n[:, ti, 4, :] for ti in range(TPB)]
            _, t = moments(k, heads(bank0), stats_q, 1e-5, [t0] * (2 * HPG))
            weigh_pending()
            a = k.act([t, nf], *[lambda e, i=i, src=src: e.activation(
                dst0[i], src, ACT.Identity, bias=stats_q.shift[:, i:i + 1], scale=stats_q.rstd[:, i:i + 1])
                for i, src in enumerate(heads(bank0))])
            t, shifted = moments(k, srcs1, stats_qk, 1e-5, [t1] * (2 * HPG) + [un["v_ready"]] * TPB)
            v_ = k.dve([t, nf], *[lambda e, i=i, src=src: e.tensor_scalar(
                dst1[i], src, stats_qk.minus[:, i:i + 1], stats_qk.rstd[:, i:i + 1], ALU.add, ALU.mult)
                for i, src in enumerate(srcs1)])
            stats_q.free, stats_qk.free = [a], [v_, shifted]
            k.banks.give(qbanks[0][0], a)
            k.banks.give(qbanks[1][0], v_)
            k.banks.give(kv, v_)
            un.update(nv=nv, v=v, nn=nn, qn=q_n, qn_ready=[a, v_])
            if b == 0:
                split_p(g)
            if b in (1, 2) and g + 1 < G2:
                split_w(g + 1, b - 1)
            if b == B - 1 and g + 1 < G2:
                group_context(g + 1)

        def turn_queries(n):
            un = units[n]
            g, b = un["g"], un["b"]
            if b == 0:
                group_keys(g)
            q_n = un["qn"]
            nq, qb, qf = qt.take()
            nk, kb, kf = kt.take()
            ready = []
            for part, nm in enumerate(("qln", "qxln")):
                nb, bank, freed = k.banks.take()
                t = k.turn([(bank[:, (c * TPB + ti) * P:(c * TPB + ti + 1) * P], q_n[:, ti, part * HPG + c, :])
                            for c in range(HPG) for ti in range(TPB)], [freed, un["qn_ready"]])
                ready.append(k.act([t, qf], lambda e, part=part, nm=nm, bank=bank: e.activation(
                    qb[:, part * HPG:(part + 1) * HPG, :], bank[:].rearrange("p (c t) -> p c t", c=HPG), ACT.Identity,
                    bias=w[f"{nm}_b"], scale=w[f"{nm}_w"])))
                k.banks.give(nb, ready[-1])
            nb, bank, freed = k.banks.take()
            t = k.turn([(bank[:, ti * P:(ti + 1) * P], q_n[:, ti, 4, :]) for ti in range(TPB)], [freed])
            ready.append(k.act([t, kf], lambda e: e.activation(
                kb[:], bank[:, 0:S], ACT.Identity, bias=w["kln_b"], scale=w["kln_w"])))
            k.banks.give(nb, ready[-1])
            qn.give(un["nn"], t)
            un.update(nq=nq, q=qb, nk=nk, kt=kb, q_ready=ready)

        def attend(n):
            un = units[n]
            gr, b = groups[un["g"]], un["b"]
            qb, kb = un["q"], un["kt"]
            np_, pbuf, pf = probs.take()
            un.update(np=np_, probs=pbuf)
            toks = [slice(ti * P, (ti + 1) * P) for ti in range(TPB)]
            nc_, cbank, freed = k.banks.take()
            for ti in range(TPB):
                for h in range(HPG):
                    a = (ti * HPG + h) * SC
                    t2 = k.mm(cbank[:, a:a + SC], [(qb[:, HPG + h, toks[ti]], gr["kx"][:, b * SC:(b + 1) * SC])],
                              [freed, un["q_ready"], gr["kx_ready"]])
            nt, tp, tf = top.take()
            ns, tt, sf = tot.take()
            banks = []
            for ti in range(TPB):
                nb, bank, freed = k.banks.take()
                for h in range(HPG):
                    t = k.mm(bank[:, h * S:(h + 1) * S], [(qb[:, h, toks[ti]], kb[:])], [freed])
                banks.append((nb, bank, t))
            c0 = TPB * HPG
            u = k.dve([t2, tf], lambda e: e.tensor_reduce(
                tp[:, c0:2 * c0], cbank[:, 0:c0 * SC].rearrange("p (h s) -> p h s", h=c0), AX.X, ALU.max))
            u = k.dve([u], lambda e: e.tensor_scalar(tp[:, c0:2 * c0], tp[:, c0:2 * c0], -softscale, None, ALU.mult))
            for ti in range(TPB):
                for h in range(HPG):
                    c = c0 + ti * HPG + h
                    a = k.act([u, pf, sf], lambda e, h=h, ti=ti, c=c: e.activation(
                        cross(pbuf[:, ti, :])[:, h, :], cbank[:, (c - c0) * SC:(c - c0 + 1) * SC], ACT.Exp,
                        bias=tp[:, c:c + 1], scale=softscale, accum_out=tt[:, c:c + 1]))
            k.banks.give(nc_, a)
            for ti, (nb, bank, t) in enumerate(banks):
                cs = slice(ti * HPG, (ti + 1) * HPG)
                u = k.dve([t], lambda e, cs=cs, bank=bank: e.tensor_reduce(
                    tp[:, cs], bank[:].rearrange("p (h s) -> p h s", h=HPG), AX.X, ALU.max))
                u = k.dve([u], lambda e, cs=cs: e.tensor_scalar(tp[:, cs], tp[:, cs], -softscale, None, ALU.mult))
                for h in range(HPG):
                    c = ti * HPG + h
                    a = k.act([u], lambda e, h=h, ti=ti, c=c, bank=bank: e.activation(
                        own(pbuf[:, ti, :])[:, h, :], bank[:, h * S:(h + 1) * S], ACT.Exp, bias=tp[:, c:c + 1],
                        scale=softscale, accum_out=tt[:, c:c + 1]))
                k.banks.give(nb, a)
            top.give(nt, a)

            def weigh():
                r = k.dve([a], lambda e: e.reciprocal(tt[:], tt[:]))
                un["p_ready"] = []
                for ti in range(TPB):
                    p, first = pbuf[:, ti, :], ti * HPG
                    x = k.act([r], *[lambda e, h=h, p=p, first=first: e.activation(
                        own(p)[:, h, :], own(p)[:, h, :], ACT.Copy, scale=tt[:, first + h:first + h + 1])
                        for h in range(HPG)])
                    z = k.pool([r], lambda e, p=p, first=c0 + first: e.tensor_tensor(
                        cross(p), cross(p), over(tt[:, first:first + HPG], SC), ALU.mult))
                    un["p_ready"].append([x, z])
                tot.give(ns, x, z)

            pending.append(weigh)
            if n + 2 >= len(units):
                weigh_pending()
            qt.give(un["nq"], t2)
            kt.give(un["nk"], t2)
            if b == B - 1:
                kx.give(gr["nk"], t2)

        def flip(n):
            un = units[n]
            weigh_pending()
            nt, ptb, tf = pt.take()
            nx, pxb, xf = px.take()
            ready = []
            nc_, cbank, cfree = k.banks.take()
            for ti in range(TPB):
                p, z = un["probs"][:, ti, :], un["p_ready"][ti]
                tok = slice(ti * P, (ti + 1) * P)
                n1, b1, f1 = k.banks.take()
                t = k.turn([(b1[:, (h * TPB + kk) * P:(h * TPB + kk + 1) * P], own(p)[:, h, kk * P:(kk + 1) * P])
                            for h in range(HPG) for kk in range(TPB)], [f1, z])
                u = k.copy(k.act, ptb[:, :, :, tok],
                           b1[:].rearrange("p (h c t) -> p h c t", h=HPG, c=TPB), [t, tf])
                k.banks.give(n1, u)
                ready.append(u)
                t = k.turn([(cbank[:, tok], p[:, n_own:n_all])], [cfree, z])
            probs.give(un["np"], t)
            u = k.copy(k.dve, pxb[:], cbank[:, 0:S], [t, xf])
            k.banks.give(nc_, u)
            ready.append(u)
            un.update(nt=nt, pt=ptb, nx=nx, px=pxb, pt_ready=ready)

        def values(n):
            un = units[n]
            g, b = un["g"], un["b"]
            gr = groups[g]
            banks = [k.banks.take() for _ in range(HPG)]
            for h, (_, bank, freed) in enumerate(banks):
                t = k.mm(bank[:, 0:S], [(un["v"][:, kk, :], un["pt"][:, h, kk, :]) for kk in range(TPB)],
                         [freed, un["v_ready"], un["pt_ready"]])
            for h, (_, bank, freed) in enumerate(banks):
                part = slice(h * SC, (h + 1) * SC)
                t2 = k.mm(bank[:, S:2 * S], [(gr["vx"][part, b, :], un["px"][part, :])], [gr["vx_ready"]])
            vs.give(un["nv"], t2)
            pt.give(un["nt"], t2)
            px.give(un["nx"], t2)
            if b == B - 1:
                vx.give(gr["nv"], t2)
            nc_, cb, cf = cat.take()
            for h, (nb, bank, _) in enumerate(banks):
                for part in range(2):
                    c, ch = part * HPG + h, part * NH2 + g * HPG + h
                    u = k.act([t2, cf, sm], lambda e: e.activation(
                        cb[:, c * S:(c + 1) * S], bank[:, part * S:(part + 1) * S], ACT.Copy,
                        scale=ismooth[:, ch:ch + 1]))
                k.banks.give(nb, u)
            nm, mb, mf = catm.take()
            nw, wb, wf = catw.take()
            nq, qb, qf = catq.take()
            t = fp8_steps(k, cb[:], mb[:], [u, mf])
            line = k.pool if n + 2 < len(units) else k.dve
            t = fp8_round(line, cb[:], mb[:], wb[:], qb[:].rearrange("p c t -> p (c t)"), [t, qf], wf)
            cat.give(nc_, t)
            catm.give(nm, t)
            catw.give(nw, t)
            un.update(ncq=nq, catq=qb, cat_ready=t)
            if n >= len(units) - 3:
                for _ in range(4):
                    next(ffn_weights, None)

        def output(n):
            un = units[n]
            gr, b = groups[un["g"]], un["b"]
            nb, bank, freed = k.banks.take()
            for ti in range(TPB):
                t = k.mm(bank[:, ti * D:(ti + 1) * D],
                         [(un["catq"][:, c, ti * P:(ti + 1) * P], part[:, c, :]) for c in range(2 * HPG)
                          for part in gr["pparts"]], [freed, un["cat_ready"], gr["p_ready"]])
            catq.give(un["ncq"], t)
            i = b * TPB
            u = k.dve([t, acc_ready[i]], lambda e: e.tensor_tensor(
                acc[:, i:i + TPB, :], acc[:, i:i + TPB, :], bank[:].rearrange("p (t d) -> p t d", t=TPB), ALU.add))
            acc_ready[i] = acc_ready[i + 1] = u
            k.banks.give(nb, u)
            if b == B - 1:
                pparts.give(gr["np"], t)


        ffn_weights = ternary(k)
        skew(len(units), project, turn_queries, attend, flip, values, output, oldest_first=True)
        for _ in ffn_weights:
            pass
        out = [k.dve([acc_ready[i], ps], lambda e, i=i: e.scalar_tensor_tensor(
            k.x[:, i, :], acc[:, i, :], pscale[:, 0:1], k.x[:, i, :], ALU.mult, ALU.add)) for i in range(NT)]
    return out


def ternary(k):
    w, absum, gamma = k.l2f, k.l2f_absum, k.l2f_gamma
    names = ("w1", "w2", "w3")
    sums = []
    for q, name in enumerate(names):
        sums.append(k.dve([k.l2f_in], lambda e: e.tensor_reduce(absum[:, q:q + 1], w[name], AX.X, ALU.add,
                                                               apply_absolute_value=True)))
        yield
    n, bank, freed = k.banks.take()
    t = k.mm(bank[:, 0:3], [(k.c["ones"], absum[:])], [freed, sums])
    t = k.dve([t], lambda e: e.tensor_scalar(gamma[:], bank[:, 0:3], 1.0 / (FFN2 * D), 1e-8, ALU.mult, ALU.add))
    k.banks.give(n, t)
    g = k.dve([t], lambda e: e.reciprocal(gamma[:], gamma[:]))
    yield
    for q, name in enumerate(names):
        t = k.dve([g], lambda e: e.tensor_scalar(w[name], w[name], gamma[:, q:q + 1], ROUND, ALU.mult, ALU.add))
        yield
        t = k.dve([t], lambda e: e.tensor_scalar(w[name], w[name], ROUND, 1.0, ALU.subtract, ALU.min))
        yield
        k.l2f_ternary[name] = k.dve([t], lambda e: e.tensor_scalar(w[name], w[name], -1.0, None, ALU.max))
        yield


def layer2_ffn(k, x_ready):
    with ExitStack() as scope:
        sb = lambda name, shape, dt=F32: k.sb(name, shape, dt, scope)
        w, quantised = k.l2f, k.l2f_ternary
        context = layer3_context(k)
        next(context)
        norm_pass(k, x_ready)
        tern = {name: sb(f"f2_{name}", [P, w[name].shape[1]], F32R) for name in ("w1", "w2", "w3")}
        tern_ready = {name: k.copy(k.act, tern[name][:], w[name], [quantised[name], x_ready])
                      for name in ("w1", "w2", "w3")}
        next(context, None)
        cols = Split(k, scope)
        hidden = [sb(f"f2_hidden_{part}", [P, FC2, TOK], F32R) for part in ("high", "low")]
        gate = Ring([sb(f"f2_gate{n}", [P, BANK]) for n in range(3)])
        kept = Ring([sb(f"f2_kept{n}", [P, BANK]) for n in range(3)])
        w1, w2 = (tern[name][:].rearrange("p (j n) -> p j n", j=DC) for name in ("w1", "w2"))
        w3 = tern["w3"][:].rearrange("p (c d) -> p c d", d=D)
        last = {}
        for half in range(TOK // BANK):
            sl = slice(half * BANK, (half + 1) * BANK)
            for c in range(FC2):
                rows = min(P, FFN2 - c * P)
                tb = []
                for wt, nm in ((w1, "w1"), (w2, "w2")):
                    n, bank, freed = k.banks.take()
                    t = k.mm(bank[0:rows, :], [(wt[:, j, c * P:c * P + rows], part[:, j, sl]) for j in range(DC)
                                               for part in (cols.high, cols.low)],
                             [freed, tern_ready[nm], cols.at(half)])
                    tb.append((n, bank, t))
                ng, gb, gf = gate.take()
                u = k.act([tb[0][2], gf], lambda e, rows=rows, gb=gb, bank=tb[0][1]: e.activation(
                    gb[0:rows, :], bank[0:rows, :], ACT.Sigmoid))
                k.banks.give(tb[0][0], u)
                v = k.dve([u, tb[1][2]], lambda e, rows=rows, gb=gb, bank=tb[1][1]: e.tensor_tensor(
                    gb[0:rows, :], gb[0:rows, :], bank[0:rows, :], ALU.mult))
                k.banks.give(tb[1][0], v)
                nk, kb, kf = kept.take()
                last.setdefault(half, []).extend(split(k, gb[0:rows, :], hidden[0][0:rows, c, sl],
                                                       hidden[1][0:rows, c, sl], kb[0:rows, :], [v, kf]))
                gate.give(ng, last[half][-2:])
                kept.give(nk, last[half][-2:])
        out = []
        for i in range(NT):
            n, bank, freed = k.banks.take()
            pairs = [(part[0:min(P, FFN2 - c * P), c, i * P:(i + 1) * P], w3[0:min(P, FFN2 - c * P), c, :])
                     for c in range(FC2) for part in hidden]
            t = k.mm(bank[:, 0:D], pairs, [freed, last[i // HALF], tern_ready["w3"]])
            out.append(k.dve([t], lambda e, i=i, bank=bank: e.tensor_tensor(k.x[:, i, :], k.x[:, i, :], bank[:, 0:D],
                                                                          ALU.add)))
            k.banks.give(n, out[-1])
    return out


def layer3_row(k, lhs, weight, bias, out, after):
    w = k.l3
    matrix = w[weight].rearrange("p (j n) -> p j n", j=DC)
    return k.mm(out, [(a, matrix[:, j, :]) for j, a in enumerate(lhs)] + [(k.c["ones"][0:1, :], w[bias][0:1, :])],
                [after, k.l3_context_in if weight in ("kw", "vw") else k.l3_in])


def layer3_context(k):
    ctx = k.ctxt["ctx"].rearrange("p (j t) -> p j t", j=DC)
    twice = k.ctxt["twice"].rearrange("p (j b t) -> p j b t", j=DC, b=B)
    krow, ms, rms, junk, wide_v = k.l3_krow, k.l3_kms, k.l3_krms, k.l3_junk, k.l3_wide_v
    tiles = range(CTX // P)
    squares, kept = [], []
    for m in tiles:
        n, bank, freed = k.banks.take()
        t = layer3_row(k, [ctx[:, j, m * P:(m + 1) * P] for j in range(DC)], "kw", "kb", bank[:, 0:D], [freed])
        squares.append(k.act([t, squares, k.l3_space], lambda e: e.activation(junk[:], bank[:, 0:D], ACT.Square,
                                                                             accum_out=ms[:, m:m + 1])))
        kept.append(k.copy(k.act, krow[:, m, :], bank[:, 0:D], []))
        k.banks.give(n, kept[-1])
    t = k.pool([squares], lambda e: e.tensor_scalar(ms[:], ms[:], 1.0 / D, 1e-6, ALU.mult, ALU.add))
    t = k.pool([t], lambda e: e.tensor_tensor(rms[:], ms[:], k.c["minus_half"][:, 0:CTX // P], ALU.pow))
    scaled = k.pool([t, kept], *[lambda e, m=m: e.tensor_scalar(krow[:, m, :], krow[:, m, :], rms[:, m:m + 1], 0.0,
                                                                ALU.mult, ALU.add) for m in tiles])
    wide_ready = []
    for b in range(B):
        n, bank, freed = k.banks.take()
        t = layer3_row(k, [twice[:, j, b, :] for j in range(DC)], "vw", "vb", bank[:, 0:D], [freed])
        u = k.copy(k.act, wide_v[:, b, :], bank[:, 0:D], [t])
        k.banks.give(n, u)
        wide_ready.append(u)
    yield
    k.l3_v_ready = [k.pool([u], lambda e: e.tensor_tensor(k.l3_v[:, b, :], wide_v[:, b, :], k.c["pair"], ALU.mult))
                    for b, u in enumerate(wide_ready)]
    n, bank, freed = k.banks.take()
    t = k.turn([(bank[:, (j * 2 + m) * P:(j * 2 + m + 1) * P], krow[:, m, j * P:(j + 1) * P])
                for j in range(DC) for m in tiles], [freed, scaled])
    k.l3_k_ready = [k.act([t], lambda e, j=j, bank=bank: e.activation(
        k.l3_k[:, j, :], bank[:, j * CTX:(j + 1) * CTX], ACT.Copy, scale=k.l3["nk"][:, j:j + 1])) for j in range(DC)]
    k.banks.give(n, k.l3_k_ready[-1])


def layer3_attention(k, x_ready):
    with ExitStack() as scope:
        sb = lambda name, shape, dt=F32: k.sb(name, shape, dt, scope)
        w, c = k.l3, k.c
        junk = Ring([sb(f"a3_junk{n}", [P, D]) for n in range(2)])
        ms = sb("a3_ms", [P, NT])
        rms = sb("a3_rms", [P, NT])
        qrow = sb("a3_q", [P, NT, D])
        qcol = sb("a3_qt", [P, DC, TOK])
        kblock = sb("a3_kb", [P, B, DC, 8, SC])
        kcol, vblock = k.l3_k, k.l3_v
        norm_pass(k, x_ready)
        squares, kept, kb_ready = [], [], []
        for i in range(NT):
            n, bank, freed = k.banks.take()
            t = layer3_row(k, tile_cols(k, i), "qw", "qb", bank[:, 0:D], [freed, both(k.cols_ready, i)])
            nj, jb, jf = junk.take()
            squares.append(k.act([t, jf, x_ready], lambda e: e.activation(jb[:], bank[:, 0:D], ACT.Square,
                                                                         accum_out=ms[:, i:i + 1])))
            junk.give(nj, squares[-1])
            kept.append(k.copy(k.dve, qrow[:, i, :], bank[:, 0:D], [t, squares[-1]]))
            k.banks.give(n, kept[-1])
            if i % TPB:
                b = i // TPB
                kb_ready.append(k.dve([k.l3_k_ready], *[lambda e, j=j: e.tensor_tensor(
                    kblock[:, b, j, :, :], under(kcol[:, j, b * SC:(b + 1) * SC], 8), over(c["head16"], SC), ALU.mult)
                    for j in range(DC)]))
        t = k.dve([squares[-1]], lambda e: e.tensor_scalar(ms[:], ms[:], 1.0 / D, 1e-6, ALU.mult, ALU.add))
        t = k.pool([t], lambda e: e.tensor_tensor(rms[:], ms[:], c["minus_half"][:, 0:NT], ALU.pow))
        scaled = [(k.pool if i % 4 == 3 else k.dve)([t, kept[i]], lambda e, i=i: e.tensor_scalar(
            qrow[:, i, :], qrow[:, i, :], rms[:, i:i + 1], 0.0, ALU.mult, ALU.add)) for i in range(NT)]
        no_bias = sb("a3_zero", [P, DC])
        z = k.pool([x_ready], lambda e: e.memset(no_bias[:], 0.0))
        q_ready = transpose_rows(k, qrow, qcol, scaled, w["nq"], no_bias[:], free=[z])
        soft = Soft(k, scope, depth=4)
        orow = Ring([sb(f"a3_o{n}", [P, D]) for n in range(2)])
        ocol = Ring([sb(f"a3_ot{n}", [P, DC, P]) for n in range(2)])
        jobs = [dict() for _ in range(NT)]

        def score(i):
            b, job = i // TPB, jobs[i]
            sbuf = soft.begin(job)
            for j in range(DC):
                n, bank, freed = k.banks.take()
                t = k.mm(bank[:], [(qcol[:, j, i * P:(i + 1) * P],
                                    kblock[:, b, j, :, :].rearrange("p h s -> p (h s)"))],
                         [freed, kb_ready[b], both(q_ready, i)])
                u = k.copy(k.act, sbuf[:, j * 8:(j + 1) * 8, :].rearrange("p h s -> p (h s)"), bank[:],
                           [t, job["free"]])
                k.banks.give(n, u)
            soft.shift(job, sbuf, [u])

        def mix(i):
            b, job = i // TPB, jobs[i]
            n, bank, freed = k.banks.take()
            for pr in range(H3 // 2):
                cs = slice(pr * 2 * HD3, (pr + 1) * 2 * HD3)
                t = k.mm(bank[:, cs], [(job["pt"][:, pr, :], vblock[:, b, cs])],
                         [freed, k.l3_v_ready[b], job["pt_ready"]])
            soft.end(job, t)
            no, o, of = orow.take()
            u = k.dve([t, of, job["one_over_ready"]], lambda e: e.tensor_tensor(
                o[:].rearrange("p (h d) -> p h d", h=H3), bank[:, 0:D].rearrange("p (h d) -> p h d", h=H3),
                over(job["one_over"][:], HD3), ALU.mult))
            soft.sum.give(job["nm"], u)
            k.banks.give(n, u)
            job.update(no=no, o=o, o_ready=u)

        def turn_mix(i):
            job = jobs[i]
            o = job["o"]
            n, bank, freed = k.banks.take()
            t = k.turn([(bank[:, j * P:(j + 1) * P], o[:, j * P:(j + 1) * P]) for j in range(DC)],
                       [freed, job["o_ready"]])
            orow.give(job["no"], t)
            nt, ot, tf = ocol.take()
            u = k.copy(k.act, ot[:].rearrange("p j t -> p (j t)"), bank[:, 0:D], [t, tf])
            k.banks.give(n, u)
            job.update(nt=nt, ot=ot, ot_ready=u)

        def out(i):
            job = jobs[i]
            n, bank, freed = k.banks.take()
            t = layer3_row(k, [job["ot"][:, j, :] for j in range(DC)], "ow", "ob", bank[:, 0:D],
                           [freed, job["ot_ready"]])
            ocol.give(job["nt"], t)
            job["x"] = k.dve([t], lambda e: e.tensor_tensor(k.x[:, i, :], k.x[:, i, :], bank[:, 0:D], ALU.add))
            k.banks.give(n, job["x"])

        skew(NT, score, lambda i: None, lambda i: soft.power(jobs[i], float(HD3) ** -0.5, divide=False),
             lambda i: soft.flip(jobs[i]), mix, turn_mix, out, oldest_first=True)
    return [job["x"] for job in jobs]


LAYERS = [layer0_attention, layer0_ffn, layer1_attention, layer1_ffn, layer2_attention, layer2_ffn,
          layer3_attention, layer3_ffn]


def build(nc, a, upto=len(LAYERS)):
    with ExitStack() as ctx:
        k = Core(nc, ctx)
        k.x = k.sb("x", [P, NT, D])
        k.rows = k.sb("rows", [P, NT, D])
        k.cols = k.sb("cols", [P, DC, TOK])
        k.moments = [Moments(k, HALF) for _ in range(NT // HALF)]
        k.seg_i = k.sb("seg_i", [P, NT], I32)
        k.keys = k.sb("keys", [P, SC])
        const = k.sb("const", [P, width(CONST)])
        ctxt = k.sb("ctxt", [P, width(CTXP)])
        l0 = k.sb("l0_weights", [P, width(L0A)])
        l2 = k.sb("l2_vectors", [P, width(L2A)])
        experts_scope, l1_scope = ExitStack(), ExitStack()
        ctx.callback(experts_scope.close)
        ctx.callback(l1_scope.close)
        k.c, k.ctxt, k.l0, k.l2 = views(const, CONST), views(ctxt, CTXP), views(l0, L0A), views(l2, L2A)

        x_in = k.load("x_in", k.x[:], a["x"])
        k.const_in = k.load("const_in", const[:], a["const"])
        k.l0_in = k.load("l0_in", l0[:], a["l0"])
        k.ctx_in = k.load("ctx_in", ctxt[:], a["ctx"])
        k.expert_dram, k.group_dram = a["experts"], a["groups"]
        kv_scope = ExitStack()
        ctx.callback(kv_scope.close)
        slots = [k.sb(f"expert{n}", [P, UNIT], scope=experts_scope) for n in range(6)]
        k.kvc = k.sb("a1_kvc", [KVC, CTX], scope=l1_scope)
        k.kq = k.sb("a1_kq", [QC, B, H1, SC], scope=l1_scope)
        k.vo = k.sb("a1_vo", [P, B, H1 // 2, D], scope=l1_scope)
        k.vo_ready = []
        l1 = k.sb("l1_weights", [P, width(L1A)], scope=l1_scope)
        l1k = k.sb("l1_key_weights", [P, width(L1K)], scope=kv_scope)
        l1v = k.sb("l1_value_weights", [P, width(L1V)], scope=kv_scope)
        k.l1, k.l1k, k.l1v = views(l1, L1A), views(l1k, L1K), views(l1v, L1V)
        k.l1k_in = k.load("l1k_in", l1k[:], a["l1k"])
        k.l1v_in = k.load("l1v_in", l1v[:], a["l1v"])
        open_experts(k, slots, "expert", 0, 1 + E0 + 1 + E1, [])
        k.seg_in = k.load("seg_in", k.seg_i[:], a["seg"])
        k.l1_in = k.load("l1_in", l1[:], a["l1"])
        k.l2_in = k.load("l2_in", l2[:], a["l2"])
        k.pool.wait([k.const_in])
        keys_ready = k.pool([k.const_in], lambda e: e.iota(k.keys[:], [[1, SC]], base=0, channel_multiplier=0,
                                                           allow_small_or_imprecise_dtypes=True))
        k.dve.wait([keys_ready, k.const_in])
        k.act.wait([k.const_in])
        k.pe.wait([k.const_in])

        ready = [x_in] * NT
        for layer in LAYERS[:upto]:
            ready = layer(k, ready)
            if layer is layer0_attention:
                kv_scope.close()
                assert width(L3C) <= width(L0A[:6])
                k.l3 = views(l0, L3C)
                k.l3_context_in = k.load("l3_context_in", l0[:, 0:width(L3C)], a["l3_context"], [ready])
            if layer is layer1_attention:
                l1_scope.close()
            if layer is layer1_ffn:
                experts_scope.close()
                l2f = k.sb("l2f_weights", [P, width(L2F)])
                k.l2f, k.l2f_ternary = views(l2f, L2F), {}
                k.l2f_absum, k.l2f_gamma = k.sb("l2f_absum", [P, 3]), k.sb("l2f_gamma", [P, 3])
                k.l2f_in = k.load("l2f_in", l2f[:], a["l2f"], [ready])
            if layer is layer2_attention:
                l3 = k.sb("l3_weights", [P, width(L3A)])
                k.l3.update(views(l3, L3A))
                k.l3_in = k.load("l3_in", l3[:], a["l3"], [ready])
                k.l3_space = ready
                k.l3_k, k.l3_v = k.sb("l3_k", [P, DC, CTX]), k.sb("l3_v", [P, B, D])
                k.l3_krow, k.l3_wide_v = k.sb("l3_krow", [P, CTX // P, D]), k.sb("l3_wide_v", [P, B, D])
                k.l3_kms, k.l3_krms = k.sb("l3_kms", [P, CTX // P]), k.sb("l3_krms", [P, CTX // P])
                k.l3_junk = k.sb("l3_junk", [P, D])
                slots = [k.sb(f"l3_expert{n}", [P, UNIT]) for n in range(6)]
                open_experts(k, slots, "l3_expert", 1 + E0 + 1 + E1, a["experts"].shape[0], [ready])
        stored = k.sp.dma([ready], k.arrival("out_stored"), lambda e: e.dma_start(a["out"], k.x[:]))
        k.sp.wait([stored])


def pack(spec, parts):
    out = np.zeros((P, width(spec)), np.float32)
    at = 0
    for name, n in spec:
        v = np.asarray(parts[name])
        v = v.reshape(v.shape[0], -1)
        out[:v.shape[0], at:at + v.shape[1]] = v
        assert v.shape[1] == n, (name, v.shape, n)
        at += n
    return out


def chunks(w):
    w = np.asarray(w)
    return w.reshape(-1, P, w.shape[-1]).transpose(1, 0, 2).reshape(P, -1)


def column(v):
    return np.ascontiguousarray(np.asarray(v).reshape(-1, P).T)


def everywhere(v):
    v = np.asarray(v).reshape(1, -1)
    return np.broadcast_to(v, (P, v.shape[1]))


def expert(gate_t, up_t, down_t):
    gu = np.concatenate([gate_t.reshape(DC, P, I), up_t.reshape(DC, P, I)], axis=2)
    return np.concatenate([gu.transpose(1, 0, 2).reshape(P, -1), down_t], axis=1)


def constants():
    part = np.arange(P)
    half = R1 // 2
    inv_freq = np.float32(1.0) / np.float32(10000.0) ** (np.arange(half, dtype=np.float32) / np.float32(half))

    def tables(n):
        ang = (np.arange(n, dtype=np.float32)[:, None] * inv_freq).astype(np.float32)
        feature = part % R1
        cos, sin = np.cos(ang).T[feature % half], np.sin(ang).T[feature % half]
        return cos.astype(np.float32), (sin * np.where(feature < half, -1.0, 1.0)[:, None]).astype(np.float32)

    cos_q, sin_q = tables(S)
    cos_k, sin_k = tables(SC)
    head = np.arange(D) // HD3
    return pack(CONST, {
        "ident": np.eye(P), "ones": np.ones((P, P)), "before": (part[:, None] < part[None, :]),
        "iota_e": everywhere(np.arange(32)), "iota_c": everywhere(np.arange(CAP)),
        "cos_q": cos_q, "sin_q": sin_q, "cos_k": cos_k, "sin_k": sin_k,
        "head16": (part[:, None] // HD3 == np.arange(8)[None, :]),
        "pair": ((part[:, None] // SC) == (head[None, :] % 2)),
        "slot1": (TOK + 1 + part)[:, None], "tokpart": (part + 1)[:, None],
        "minus_half": np.full((P, 16), -0.5)})


def swap_halves(w):
    w = np.asarray(w)
    return w.reshape(w.shape[0], -1, 2, R1 // 2)[:, :, ::-1, :].reshape(w.shape[0], -1)


def lay_out(v):
    v = {n: np.asarray(x) for n, x in v.items()}
    ctx_t = v["ctx_2048"].reshape(CTX, D).T
    by_batch = ctx_t.reshape(D, B, 1, SC)
    twice = np.broadcast_to(by_batch, (D, B, 2, SC)).reshape(D, B * 2 * SC)
    a = {"x": v["x"].reshape(NT, P, D).transpose(1, 0, 2), "const": constants(),
         "ctx": pack(CTXP, {"ctx": chunks(ctx_t), "twice": chunks(twice)}),
         "seg": v["itok_BxS_0_1023"].reshape(NT, P).T}
    g = lambda n: v["L0_xattn_" + n]
    a["l0"] = pack(L0A, {
        "w_in": chunks(g("W_in").T), "w_out": chunks(g("W_out").T), "b_in": column(g("b_in")),
        "b_out": everywhere(g("b_out")), "gamma": everywhere(g("gamma")), "beta": everywhere(g("beta")),
        "decay": everywhere(g("decay")), "gate0": chunks(v["L0_ffn_gate_w"].T), "bias0": everywhere(v["L0_ffn_bias"]),
        "gate1": chunks(v["L1_ffn_gate_w"].T), "gate3": chunks(v["L3_ffn_centroids"].T),
        "bias3": everywhere(v["L3_ffn_gate_bias"])})
    ex = [expert(v["L0_ffn_sg"].T, v["L0_ffn_su"].T, v["L0_ffn_sd"].T)]
    ex += [expert(v["L0_ffn_w_gate"][e].T, v["L0_ffn_w_up"][e].T, v["L0_ffn_w_down"][e].T) for e in range(E0)]
    ex += [expert(v["L1_ffn_sw1"].T, v["L1_ffn_sw3"].T, v["L1_ffn_sw2"].T)]
    ex += [expert(v["L1_ffn_w1"][e].T, v["L1_ffn_w3"][e].T, v["L1_ffn_w2"][e].T) for e in range(E1)]
    ex += [expert(v["L3_ffn_wg_s"][:, s], v["L3_ffn_wu_s"][:, s], v["L3_ffn_wd_s"][s, :])
           for s in (slice(0, I), slice(I, 2 * I))]
    ex += [expert(v["L3_ffn_wg"][e], v["L3_ffn_wu"][e], v["L3_ffn_wd"][e]) for e in range(E3)]
    a["experts"] = np.stack(ex)
    g = lambda n: v["L1_xattn_" + n]
    by_head = lambda w: w.reshape(-1, H1, HD1)
    uv, wo = g("W_uv"), chunks(g("W_o"))
    a["l1k"] = pack(L1K, {"kvc": chunks(g("W_kvc")), "uk": g("W_uk"),
                          "uq": by_head(g("W_uq")).transpose(2, 1, 0).reshape(P, -1)})
    a["l1v"] = pack(L1V, {"uv": uv[:, :EARLY * HD1], "wo": wo[:, :EARLY * D]})
    a["l1"] = pack(L1A, {
        "dq": chunks(g("W_dq")), "qr": g("W_qr"), "qr_swap": swap_halves(g("W_qr")),
        "kr": np.concatenate([g("W_kr")] * 2, axis=1),
        "kr_swap": np.concatenate([swap_halves(g("W_kr"))] * 2, axis=1), "uv_late": uv[:, EARLY * HD1:],
        "wo_late": wo[:, EARLY * D:]})
    g = lambda n: v["L2_xattn_" + n]
    vec = {n: column(g(n)) for n in ("ln_w", "ln_b", "qln_w", "qln_b", "kln_w", "kln_b", "qxln_w", "qxln_b",
                                     "kxln_w", "kxln_b")}
    a["l2"] = pack(L2A, {
        **vec, "q_in": column(g("q_in_scale")), "qx_in": column(g("qx_in_scale")), "k_in": column(g("k_in_scale")),
        "v_in": column(g("v_in_scale")), "wq_s": everywhere(g("wq_scale")), "wqx_s": everywhere(g("wqx_scale")),
        "wk_s": everywhere(g("wk_scale")), "wv_s": everywhere(g("wv_scale")), "p_w": everywhere(g("proj_w_scale")),
        "p_in": everywhere(g("proj_in_scale")), "smooth": column(g("proj_smooth"))})
    kvx = g("w_kv_x")
    proj = g("wproj").T.reshape(2, G2, HPG, P, D)
    a["groups"] = np.stack([pack(L2G, {
        "w": chunks(np.concatenate([
            g("wq")[q * HPG * P:(q + 1) * HPG * P], g("wqx")[q * HPG * P:(q + 1) * HPG * P],
            g("wk")[q * P:(q + 1) * P], g("wv")[q * P:(q + 1) * P], kvx[q * P:(q + 1) * P],
            kvx[(G2 + q) * P:(G2 + q + 1) * P]]).T),
        "proj": proj[:, q].reshape(2 * HPG, P, D).transpose(1, 0, 2)}) for q in range(G2)])
    pad = lambda w: np.concatenate([w, np.zeros((FC2 * P - FFN2, D), np.float32)])
    a["l2f"] = pack(L2F, {"w1": chunks(v["L2_ffn_w1"].T), "w2": chunks(v["L2_ffn_w2"].T),
                          "w3": chunks(pad(v["L2_ffn_w3"].T))})
    g = lambda n: v["L3_xattn_" + n]
    a["l3_context"] = pack(L3C, {
        "kw": chunks(g("k_img_w").T), "vw": chunks(g("v_img_w").T), "kb": everywhere(g("k_img_b")),
        "vb": everywhere(g("v_img_b")), "nk": column(g("norm_k_img_w"))})
    a["l3"] = pack(L3A, {"qw": chunks(g("q_w").T), "ow": chunks(g("o_w").T), "qb": everywhere(g("q_b")),
                         "ob": everywhere(g("o_b")), "nq": column(g("norm_q_w"))})
    return {n: np.ascontiguousarray(x) for n, x in a.items()}


def program(nc, arrays, **options):
    a = {n: nc.dram_tensor(f"in_{n}", x.shape, mybir.dt.from_np(x.dtype), kind="ExternalInput").ap()
         for n, x in arrays.items()}
    a["out"] = nc.dram_tensor("out", [P, NT, D], F32, kind="ExternalOutput").ap()
    build(nc, a, **options)


def kernel(**inputs):
    import concourse.bacc as bacc
    from concourse.bass_utils import run_bass_kernel_spmd

    nc = bacc.Bacc("TRN2", target_bir_lowering=False, num_devices=1)
    arrays = lay_out(inputs)
    program(nc, arrays)
    got = run_bass_kernel_spmd(nc, [{f"in_{n}": x for n, x in arrays.items()}], core_ids=[0])
    return got.results[0]["out"].transpose(1, 0, 2).reshape(B, S, D)
```
